# Optimizing a Trainium2 kernel written in Bass

```python
import numpy as np
import jax
import jax.numpy as jnp

def _softmax(x, axis=-1):
    return jax.nn.softmax(x, axis=axis)

def _gelu(x):
    return jax.nn.gelu(x, approximate=True)

def _silu(x):
    return jax.nn.silu(x)

def _sigmoid(x):
    return jax.nn.sigmoid(x)

def _layernorm(x, axis=-1, eps=1e-05):
    m = jnp.mean(x, axis=axis, keepdims=True)
    v = jnp.var(x, axis=axis, keepdims=True)
    return (x - m) / jnp.sqrt(v + eps)

def _scatter_add(tgt, idx, src, axis=0):
    return tgt.at[idx].add(src)

def _segment_sum(src, seg, n):
    return jax.ops.segment_sum(src, seg, n)
kernel_name = 'mk_flamingo_gated_d4_seqx_r8_36b1dd'

def setup_inputs(seed: int=0):
    np.random.seed(seed)
    _w = jnp.asarray

    def _rec_inputs():
        import jax
        import jax.numpy as jnp
        _rk = jax.random.key(seed)
        x = 7.22e-05 + 1 * jax.random.normal(jax.random.fold_in(_rk, 1), (32, 64, 256), jnp.float32)
        _lenS = 64 - jax.random.randint(jax.random.fold_in(_rk, 7), (32,), 0, max(1, 64 // 4) + 1, jnp.int32)
        _lenS2 = 64 - jax.random.randint(jax.random.fold_in(_rk, 8), (32,), 0, max(1, 64 // 4) + 1, jnp.int32)
        _ctx_1024P = jax.random.normal(jax.random.fold_in(_rk, 11), (32, 16, 128), jnp.float32)
        _ctx_1024c = jax.random.dirichlet(jax.random.fold_in(_rk, 511), 0.3 * jnp.ones((16,), jnp.float32), (32, 64))
        _ctx_1024t = jnp.einsum('bsk,bkd->bsd', _ctx_1024c, _ctx_1024P)
        _ctx_1024t = _ctx_1024t * jax.lax.rsqrt(jnp.mean(jnp.square(_ctx_1024t)) + 1e-12) * 0.953939
        ctx_1024 = -0.000673644 + 1.00013 * (_ctx_1024t + 0.3 * jax.random.normal(jax.random.fold_in(_rk, 611), (32, 64, 128), jnp.float32))
        fside_BxSx2_0 = jax.random.uniform(jax.random.fold_in(_rk, 12), (32, 64, 2), jnp.float32, 0.0, 0.999707)
        _validS = jnp.arange(64)[None, :] < _lenS[:, None]
        _validS2 = jnp.arange(64)[None, :] < _lenS2[:, None]
        _causal = jnp.tril(jnp.ones((64, 64), dtype=bool))
        mask_BxS2_bf1 = jnp.ones((32, 64), dtype=bool)
        _g = jax.random.normal(jax.random.fold_in(_rk, 9001), (2, 4), jnp.float32)
        _g = jnp.sign(_g) * jnp.maximum(jnp.abs(_g), 1.0) + (_g == 0) * 1.0
        g_xattn = _g[0]
        g_ffn = _g[1]
        return (x, ctx_1024, fside_BxSx2_0, mask_BxS2_bf1, g_xattn, g_ffn)
    x, ctx_1024, fside_BxSx2_0, mask_BxS2_bf1, g_xattn, g_ffn = _rec_inputs()

    def _L0_xattn_setup():
        import jax, jax.numpy as jnp
        import numpy as np
        B, S1, S2, DCA = (2, 256, 128, 16)
        QDIM, KDIM, H = (256, 128, 16)
        HD = QDIM // H
        SCALE = HD ** (-0.5)
        EPS = 1e-06
        DCA_WEIGHT = 1.0

        def _ln(t, w, b):
            m = jnp.mean(t, axis=-1, keepdims=True)
            v = jnp.var(t, axis=-1, keepdims=True)
            return (t - m) * jax.lax.rsqrt(v + EPS) * w + b

        def _attn(q, k, v):
            s = jnp.einsum('bhqd,bhkd->bhqk', q, k) * SCALE
            p = jax.nn.softmax(s, axis=-1)
            return jnp.einsum('bhqk,bhkd->bhqd', p, v)
        key = jax.random.key(seed)
        ks = jax.random.split(key, 8)
        w = lambda k, shape: jax.random.normal(k, shape, jnp.float32) * 0.02
        return {'x': jax.random.normal(ks[0], (B, S1, QDIM), jnp.float32), 'y': jax.random.normal(ks[1], (B, S2 + DCA, KDIM), jnp.float32), 'Wq': w(ks[2], (QDIM, QDIM)), 'bq': jnp.zeros((QDIM,), jnp.float32), 'Wk': w(ks[3], (KDIM, QDIM)), 'bk': jnp.zeros((QDIM,), jnp.float32), 'Wv': w(ks[4], (KDIM, QDIM)), 'bv': jnp.zeros((QDIM,), jnp.float32), 'Wkv_dca': w(ks[5], (KDIM, 2 * QDIM)), 'bkv_dca': jnp.zeros((2 * QDIM,), jnp.float32), 'qn_w': jnp.ones((HD,), jnp.float32), 'qn_b': jnp.zeros((HD,), jnp.float32), 'kn_w': jnp.ones((HD,), jnp.float32), 'kn_b': jnp.zeros((HD,), jnp.float32), 'kn_dca_w': jnp.ones((HD,), jnp.float32), 'kn_dca_b': jnp.zeros((HD,), jnp.float32), 'Wo': w(ks[6], (QDIM, QDIM)), 'bo': jnp.zeros((QDIM,), jnp.float32)}
    _L0_xattn_all = _L0_xattn_setup()
    _L0_xattn_in = {k: v for k, v in _L0_xattn_all.items() if k in ('Wq', 'bq', 'Wk', 'bk', 'Wv', 'bv', 'Wkv_dca', 'bkv_dca', 'qn_w', 'qn_b', 'kn_w', 'kn_b', 'kn_dca_w', 'kn_dca_b', 'Wo', 'bo')}
    del _L0_xattn_all

    def _L0_ffn_setup():
        import jax, jax.numpy as jnp
        import numpy as np
        B, S, D = (4, 256, 256)
        E, K, M = (8, 2, 128)
        key = jax.random.key(seed)
        k0, k1, k2, k3, k4 = jax.random.split(key, 5)
        d_scale = D ** (-0.5)
        m_scale = M ** (-0.5)
        return {'x': jax.random.normal(k0, (B, S, D), jnp.float32), 'w_gate': jax.random.normal(k1, (D, E), jnp.float32) * d_scale, 'wi_0': jax.random.normal(k2, (E, D, M), jnp.float32) * d_scale, 'wi_1': jax.random.normal(k3, (E, D, M), jnp.float32) * d_scale, 'wo': jax.random.normal(k4, (E, M, D), jnp.float32) * m_scale}
    _L0_ffn_all = _L0_ffn_setup()
    _L0_ffn_in = {k: v for k, v in _L0_ffn_all.items() if k in ('w_gate', 'wi_0', 'wi_1', 'wo')}
    del _L0_ffn_all

    def _L1_xattn_setup():
        import jax, jax.numpy as jnp
        import numpy as np
        EPS = 1e-05

        def rmsnorm(x, g, eps=EPS):
            var = jnp.mean(jnp.square(x), axis=-1, keepdims=True)
            return x * jax.lax.rsqrt(var + eps) * g
        key = jax.random.key(seed)
        ks = jax.random.split(key, 8)
        B, Sq, Skv = (2, 512, 64)
        dim, cdim, H, D = (256, 128, 16, 128)
        inner = H * D
        s = lambda f: 1.0 / np.sqrt(f)
        return {'hidden_states': jax.random.normal(ks[0], (B, Sq, dim), jnp.float32), 'encoder_hidden_states': jax.random.normal(ks[1], (B, Skv, cdim), jnp.float32), 'Wq': jax.random.normal(ks[2], (dim, inner), jnp.float32) * s(dim), 'Wk': jax.random.normal(ks[3], (cdim, inner), jnp.float32) * s(cdim), 'Wv': jax.random.normal(ks[4], (cdim, inner), jnp.float32) * s(cdim), 'Wo': jax.random.normal(ks[5], (inner, dim), jnp.float32) * s(inner), 'gq': jnp.ones((D,), jnp.float32), 'gk': jnp.ones((D,), jnp.float32)}
    _L1_xattn_all = _L1_xattn_setup()
    _L1_xattn_in = {k: v for k, v in _L1_xattn_all.items() if k in ('Wq', 'Wk', 'Wv', 'Wo', 'gq', 'gk')}
    del _L1_xattn_all

    def _L1_ffn_setup():
        import jax, jax.numpy as jnp
        import numpy as np
        H = 256
        I = 176
        E = 8
        K = 2
        B, S = (2, 256)
        key = jax.random.key(seed)
        k0, k1, k2, k3, k4 = jax.random.split(key, 5)
        scale = 1.0 / np.sqrt(H)
        x = jax.random.normal(k0, (B, S, H), dtype=jnp.float32)
        Wr = jax.random.normal(k1, (H, E), dtype=jnp.float32) * scale
        Wg = jax.random.normal(k2, (E, H, I), dtype=jnp.float32) * scale
        Wu = jax.random.normal(k3, (E, H, I), dtype=jnp.float32) * scale
        Wd = jax.random.normal(k4, (E, I, H), dtype=jnp.float32) * (1.0 / np.sqrt(I))
        return {'x': x, 'Wr': Wr, 'Wg': Wg, 'Wu': Wu, 'Wd': Wd}
    _L1_ffn_all = _L1_ffn_setup()
    _L1_ffn_in = {k: v for k, v in _L1_ffn_all.items() if k in ('Wr', 'Wg', 'Wu', 'Wd')}
    del _L1_ffn_all

    def _L2_xattn_setup():
        import jax, jax.numpy as jnp
        import numpy as np
        DIM = 256
        CTX_DIM = 128
        N_HEADS = 32
        HEAD_DIM = DIM // N_HEADS
        POS_DIM = 2
        B, N, CTXN = (2, 256, 256)
        ROPE_BASE = 10000.0

        def apply_axial_rope(x, pos):
            b, n, h, d = x.shape
            p = pos.shape[-1]
            dpa = d // p
            half = dpa // 2
            freqs = ROPE_BASE ** (-jnp.arange(half, dtype=x.dtype) / half)
            ang = pos[..., :, None] * freqs
            cos = jnp.cos(ang)[:, :, None, :, :]
            sin = jnp.sin(ang)[:, :, None, :, :]
            xr = x.reshape(b, n, h, p, half, 2)
            x1, x2 = (xr[..., 0], xr[..., 1])
            out = jnp.stack([x1 * cos - x2 * sin, x1 * sin + x2 * cos], axis=-1)
            return out.reshape(b, n, h, d)
        key = jax.random.key(seed)
        ks = jax.random.split(key, 8)
        x = jax.random.normal(ks[0], (B, N, DIM), jnp.float32)
        ctx = jax.random.normal(ks[1], (B, CTXN, CTX_DIM), jnp.float32)
        pos_map = jax.random.uniform(ks[2], (B, N, POS_DIM), jnp.float32)
        ctx_pos_map = jax.random.uniform(ks[3], (B, CTXN, POS_DIM), jnp.float32)
        Wq = jax.random.normal(ks[4], (DIM, DIM), jnp.float32) / np.sqrt(DIM)
        Wkv = jax.random.normal(ks[5], (CTX_DIM, 2 * DIM), jnp.float32) / np.sqrt(CTX_DIM)
        Wout = jax.random.normal(ks[6], (DIM, DIM), jnp.float32) / np.sqrt(DIM)
        bout = jnp.zeros((DIM,), jnp.float32)
        return {'x': x, 'ctx': ctx, 'pos_map': pos_map, 'ctx_pos_map': ctx_pos_map, 'Wq': Wq, 'Wkv': Wkv, 'Wout': Wout, 'bout': bout}
    _L2_xattn_all = _L2_xattn_setup()
    _L2_xattn_in = {k: v for k, v in _L2_xattn_all.items() if k in ('Wq', 'Wkv', 'Wout', 'bout')}
    del _L2_xattn_all

    def _L2_ffn_setup():
        import jax, jax.numpy as jnp
        import numpy as np
        B, T, D = (4, 256, 256)
        E = 8
        K = 2
        F = 1024 // (E // 2)
        key = jax.random.key(seed)
        ks = jax.random.split(key, 5)
        s_in = 1.0 / np.sqrt(D)
        s_mid = 1.0 / np.sqrt(F)
        x = jax.random.normal(ks[0], (B, T, D), dtype=jnp.float32)
        Wr = jax.random.normal(ks[1], (D, E), dtype=jnp.float32) * s_in
        Wg = jax.random.normal(ks[2], (E, D, F), dtype=jnp.float32) * s_in
        Wu = jax.random.normal(ks[3], (E, D, F), dtype=jnp.float32) * s_in
        Wd = jax.random.normal(ks[4], (E, F, D), dtype=jnp.float32) * s_mid
        return {'x': x, 'Wr': Wr, 'Wg': Wg, 'Wu': Wu, 'Wd': Wd}
    _L2_ffn_all = _L2_ffn_setup()
    _L2_ffn_in = {k: v for k, v in _L2_ffn_all.items() if k in ('Wr', 'Wg', 'Wu', 'Wd')}
    del _L2_ffn_all

    def _L3_xattn_setup():
        import jax, jax.numpy as jnp
        import numpy as np
        N_HEADS = 16
        N_KV_HEADS = 8
        HEAD_DIM = 128
        D_TEXT = 256
        D_VISION = 128
        GROUPS = N_HEADS // N_KV_HEADS
        key = jax.random.key(seed)
        ks = jax.random.split(key, 6)
        B, T_text, T_vis = (4, 256, 72)
        text_hidden = jax.random.normal(ks[0], (B, T_text, D_TEXT), dtype=jnp.float32)
        vision_tokens = jax.random.normal(ks[1], (B, T_vis, D_VISION), dtype=jnp.float32)
        vision_mask = jnp.ones((B, T_vis), dtype=bool)
        s = 0.02
        Wq = jax.random.normal(ks[2], (D_TEXT, N_HEADS * HEAD_DIM), dtype=jnp.float32) * s
        Wk = jax.random.normal(ks[3], (D_VISION, N_KV_HEADS * HEAD_DIM), dtype=jnp.float32) * s
        Wv = jax.random.normal(ks[4], (D_VISION, N_KV_HEADS * HEAD_DIM), dtype=jnp.float32) * s
        Wo = jax.random.normal(ks[5], (N_HEADS * HEAD_DIM, D_TEXT), dtype=jnp.float32) * s
        return {'text_hidden': text_hidden, 'vision_tokens': vision_tokens, 'vision_mask': vision_mask, 'Wq': Wq, 'Wk': Wk, 'Wv': Wv, 'Wo': Wo}
    _L3_xattn_all = _L3_xattn_setup()
    _L3_xattn_in = {k: v for k, v in _L3_xattn_all.items() if k in ('Wq', 'Wk', 'Wv', 'Wo')}
    del _L3_xattn_all

    def _L3_ffn_setup():
        import jax, jax.numpy as jnp
        import numpy as np
        H = 256
        E = 8
        K = 2
        I = 16
        key = jax.random.key(seed)
        k1, k2, k3, k4 = jax.random.split(key, 4)
        B, T = (2, 512)
        x = jax.random.normal(k1, (B, T, H), dtype=jnp.float32)
        router_w = jax.random.normal(k2, (E, H), dtype=jnp.float32) / np.sqrt(H)
        down_w = jax.random.normal(k3, (E, I, H), dtype=jnp.float32) / np.sqrt(H)
        up_w = jax.random.normal(k4, (E, H, I), dtype=jnp.float32) / np.sqrt(I)
        return {'x': x, 'router_w': router_w, 'down_w': down_w, 'up_w': up_w}
    _L3_ffn_all = _L3_ffn_setup()
    _L3_ffn_in = {k: v for k, v in _L3_ffn_all.items() if k in ('router_w', 'down_w', 'up_w')}
    del _L3_ffn_all
    return {'x': x, 'ctx_1024': ctx_1024, 'fside_BxSx2_0': fside_BxSx2_0, 'mask_BxS2_bf1': mask_BxS2_bf1, 'g_xattn': g_xattn, 'g_ffn': g_ffn, 'L0_xattn_Wq': _L0_xattn_in['Wq'], 'L0_xattn_bq': _L0_xattn_in['bq'], 'L0_xattn_Wk': _L0_xattn_in['Wk'], 'L0_xattn_bk': _L0_xattn_in['bk'], 'L0_xattn_Wv': _L0_xattn_in['Wv'], 'L0_xattn_bv': _L0_xattn_in['bv'], 'L0_xattn_Wkv_dca': _L0_xattn_in['Wkv_dca'], 'L0_xattn_bkv_dca': _L0_xattn_in['bkv_dca'], 'L0_xattn_qn_w': _L0_xattn_in['qn_w'], 'L0_xattn_qn_b': _L0_xattn_in['qn_b'], 'L0_xattn_kn_w': _L0_xattn_in['kn_w'], 'L0_xattn_kn_b': _L0_xattn_in['kn_b'], 'L0_xattn_kn_dca_w': _L0_xattn_in['kn_dca_w'], 'L0_xattn_kn_dca_b': _L0_xattn_in['kn_dca_b'], 'L0_xattn_Wo': _L0_xattn_in['Wo'], 'L0_xattn_bo': _L0_xattn_in['bo'], 'L0_ffn_w_gate': _L0_ffn_in['w_gate'], 'L0_ffn_wi_0': _L0_ffn_in['wi_0'], 'L0_ffn_wi_1': _L0_ffn_in['wi_1'], 'L0_ffn_wo': _L0_ffn_in['wo'], 'L1_xattn_Wq': _L1_xattn_in['Wq'], 'L1_xattn_Wk': _L1_xattn_in['Wk'], 'L1_xattn_Wv': _L1_xattn_in['Wv'], 'L1_xattn_Wo': _L1_xattn_in['Wo'], 'L1_xattn_gq': _L1_xattn_in['gq'], 'L1_xattn_gk': _L1_xattn_in['gk'], 'L1_ffn_Wr': _L1_ffn_in['Wr'], 'L1_ffn_Wg': _L1_ffn_in['Wg'], 'L1_ffn_Wu': _L1_ffn_in['Wu'], 'L1_ffn_Wd': _L1_ffn_in['Wd'], 'L2_xattn_Wq': _L2_xattn_in['Wq'], 'L2_xattn_Wkv': _L2_xattn_in['Wkv'], 'L2_xattn_Wout': _L2_xattn_in['Wout'], 'L2_xattn_bout': _L2_xattn_in['bout'], 'L2_ffn_Wr': _L2_ffn_in['Wr'], 'L2_ffn_Wg': _L2_ffn_in['Wg'], 'L2_ffn_Wu': _L2_ffn_in['Wu'], 'L2_ffn_Wd': _L2_ffn_in['Wd'], 'L3_xattn_Wq': _L3_xattn_in['Wq'], 'L3_xattn_Wk': _L3_xattn_in['Wk'], 'L3_xattn_Wv': _L3_xattn_in['Wv'], 'L3_xattn_Wo': _L3_xattn_in['Wo'], 'L3_ffn_router_w': _L3_ffn_in['router_w'], 'L3_ffn_down_w': _L3_ffn_in['down_w'], 'L3_ffn_up_w': _L3_ffn_in['up_w']}

def reference(x, ctx_1024, fside_BxSx2_0, mask_BxS2_bf1, g_xattn, g_ffn, L0_xattn_Wq, L0_xattn_bq, L0_xattn_Wk, L0_xattn_bk, L0_xattn_Wv, L0_xattn_bv, L0_xattn_Wkv_dca, L0_xattn_bkv_dca, L0_xattn_qn_w, L0_xattn_qn_b, L0_xattn_kn_w, L0_xattn_kn_b, L0_xattn_kn_dca_w, L0_xattn_kn_dca_b, L0_xattn_Wo, L0_xattn_bo, L0_ffn_w_gate, L0_ffn_wi_0, L0_ffn_wi_1, L0_ffn_wo, L1_xattn_Wq, L1_xattn_Wk, L1_xattn_Wv, L1_xattn_Wo, L1_xattn_gq, L1_xattn_gk, L1_ffn_Wr, L1_ffn_Wg, L1_ffn_Wu, L1_ffn_Wd, L2_xattn_Wq, L2_xattn_Wkv, L2_xattn_Wout, L2_xattn_bout, L2_ffn_Wr, L2_ffn_Wg, L2_ffn_Wu, L2_ffn_Wd, L3_xattn_Wq, L3_xattn_Wk, L3_xattn_Wv, L3_xattn_Wo, L3_ffn_router_w, L3_ffn_down_w, L3_ffn_up_w):
    import jax
    import jax.numpy as jnp

    def _L0_xattn_ref(x, y, Wq, bq, Wk, bk, Wv, bv, Wkv_dca, bkv_dca, qn_w, qn_b, kn_w, kn_b, kn_dca_w, kn_dca_b, Wo, bo):
        import jax, jax.numpy as jnp
        import numpy as np
        B, S1, S2, DCA = (2, 256, 128, 16)
        QDIM, KDIM, H = (256, 128, 16)
        HD = QDIM // H
        SCALE = HD ** (-0.5)
        EPS = 1e-06
        DCA_WEIGHT = 1.0

        def _ln(t, w, b):
            m = jnp.mean(t, axis=-1, keepdims=True)
            v = jnp.var(t, axis=-1, keepdims=True)
            return (t - m) * jax.lax.rsqrt(v + EPS) * w + b

        def _attn(q, k, v):
            s = jnp.einsum('bhqd,bhkd->bhqk', q, k) * SCALE
            p = jax.nn.softmax(s, axis=-1)
            return jnp.einsum('bhqk,bhkd->bhqd', p, v)
        b, s1, _ = x.shape
        y_dca = y[:, -DCA:, :]
        y_main = y[:, :-DCA, :]
        kv_dca = (y_dca @ Wkv_dca + bkv_dca).reshape(b, DCA, 2, H, HD)
        k_dca = _ln(kv_dca[:, :, 0], kn_dca_w, kn_dca_b)
        v_dca = kv_dca[:, :, 1]
        s2 = y_main.shape[1]
        q = _ln((x @ Wq + bq).reshape(b, s1, H, HD), qn_w, qn_b)
        kv = jnp.concatenate([y_main @ Wk + bk, y_main @ Wv + bv], axis=-1)
        kv = kv.reshape(b, s2, H, 2 * HD)
        k = _ln(kv[..., :HD], kn_w, kn_b)
        v = kv[..., HD:]
        qT = q.transpose(0, 2, 1, 3)
        ctx = _attn(qT, k.transpose(0, 2, 1, 3), v.transpose(0, 2, 1, 3))
        ctx = ctx.transpose(0, 2, 1, 3).reshape(b, s1, QDIM)
        ctx_dca = _attn(qT, k_dca.transpose(0, 2, 1, 3), v_dca.transpose(0, 2, 1, 3))
        ctx_dca = ctx_dca.transpose(0, 2, 1, 3).reshape(b, s1, QDIM)
        ctx = ctx + DCA_WEIGHT * ctx_dca
        return ctx @ Wo + bo

    def _L0_ffn_ref(x, w_gate, wi_0, wi_1, wo):
        import jax, jax.numpy as jnp
        import numpy as np
        B, S, D = (4, 256, 256)
        E, K, M = (8, 2, 128)
        b, s, d = x.shape
        e = w_gate.shape[1]
        xf = x.reshape(-1, d)
        logits = jnp.dot(xf, w_gate)
        top_logits, top_idx = jax.lax.top_k(logits, K)
        weights = jax.nn.softmax(top_logits, axis=-1)
        flat_idx = top_idx.reshape(-1)
        sort_order = jnp.argsort(flat_idx)
        token_ids = sort_order // K
        sorted_x = jnp.take(xf, token_ids, axis=0)
        group_sizes = jnp.bincount(flat_idx, length=E).astype(jnp.int32)
        h0 = jax.lax.ragged_dot(sorted_x, wi_0, group_sizes)
        h1 = jax.lax.ragged_dot(sorted_x, wi_1, group_sizes)
        inter = jax.nn.silu(h0) * h1
        out_sorted = jax.lax.ragged_dot(inter, wo, group_sizes)
        unsort = jnp.argsort(sort_order)
        out = jnp.take(out_sorted, unsort, axis=0).reshape(-1, K, d)
        out = jnp.einsum('tkd,tk->td', out, weights)
        return out.reshape(b, s, d)

    def _L1_xattn_ref(hidden_states, encoder_hidden_states, Wq, Wk, Wv, Wo, gq, gk):
        import jax, jax.numpy as jnp
        import numpy as np
        EPS = 1e-05

        def rmsnorm(x, g, eps=EPS):
            var = jnp.mean(jnp.square(x), axis=-1, keepdims=True)
            return x * jax.lax.rsqrt(var + eps) * g
        B, Sq, _ = hidden_states.shape
        Skv = encoder_hidden_states.shape[1]
        D = gq.shape[0]
        H = Wq.shape[1] // D
        scale = 1.0 / np.sqrt(D)
        q = (hidden_states @ Wq).reshape(B, Sq, H, D)
        k = (encoder_hidden_states @ Wk).reshape(B, Skv, H, D)
        v = (encoder_hidden_states @ Wv).reshape(B, Skv, H, D)
        q = rmsnorm(q, gq)
        k = rmsnorm(k, gk)
        scores = jnp.einsum('bqhd,bkhd->bhqk', q, k) * scale
        attn = jax.nn.softmax(scores, axis=-1)
        out = jnp.einsum('bhqk,bkhd->bqhd', attn, v)
        out = out.reshape(B, Sq, H * D)
        return out @ Wo

    def _L1_ffn_ref(x, Wr, Wg, Wu, Wd):
        import jax, jax.numpy as jnp
        import numpy as np
        H = 256
        I = 176
        E = 8
        K = 2
        B, S = (2, 256)
        router_logits = jnp.einsum('bsh,he->bse', x, Wr)
        probs = jax.nn.softmax(router_logits.astype(jnp.float32), axis=-1)
        topk_w, topk_idx = jax.lax.top_k(probs, K)
        topk_w = topk_w / jnp.sum(topk_w, axis=-1, keepdims=True)
        onehot = jax.nn.one_hot(topk_idx, E, dtype=topk_w.dtype)
        combine = jnp.einsum('bsk,bske->bse', topk_w, onehot)
        g = jnp.einsum('bsh,ehi->besi', x, Wg)
        u = jnp.einsum('bsh,ehi->besi', x, Wu)
        h = jax.nn.silu(g) * u
        y = jnp.einsum('besi,eih->besh', h, Wd)
        out = jnp.einsum('bse,besh->bsh', combine.astype(x.dtype), y)
        return out

    def _L2_xattn_ref(x, ctx, pos_map, ctx_pos_map, Wq, Wkv, Wout, bout):
        import jax, jax.numpy as jnp
        import numpy as np
        DIM = 256
        CTX_DIM = 128
        N_HEADS = 32
        HEAD_DIM = DIM // N_HEADS
        POS_DIM = 2
        B, N, CTXN = (2, 256, 256)
        ROPE_BASE = 10000.0

        def apply_axial_rope(x, pos):
            b, n, h, d = x.shape
            p = pos.shape[-1]
            dpa = d // p
            half = dpa // 2
            freqs = ROPE_BASE ** (-jnp.arange(half, dtype=x.dtype) / half)
            ang = pos[..., :, None] * freqs
            cos = jnp.cos(ang)[:, :, None, :, :]
            sin = jnp.sin(ang)[:, :, None, :, :]
            xr = x.reshape(b, n, h, p, half, 2)
            x1, x2 = (xr[..., 0], xr[..., 1])
            out = jnp.stack([x1 * cos - x2 * sin, x1 * sin + x2 * cos], axis=-1)
            return out.reshape(b, n, h, d)
        b, n, _ = x.shape
        ctx_n = ctx.shape[1]
        q = (x @ Wq).reshape(b, n, N_HEADS, HEAD_DIM)
        k, v = jnp.split(ctx @ Wkv, 2, axis=-1)
        k = k.reshape(b, ctx_n, N_HEADS, HEAD_DIM)
        v = v.reshape(b, ctx_n, N_HEADS, HEAD_DIM)
        q = apply_axial_rope(q, pos_map)
        k = apply_axial_rope(k, ctx_pos_map)
        scale = 1.0 / np.sqrt(HEAD_DIM).astype(np.float32)
        logits = jnp.einsum('bqhd,bkhd->bhqk', q, k) * scale
        w = jax.nn.softmax(logits, axis=-1)
        attn = jnp.einsum('bhqk,bkhd->bqhd', w, v)
        attn = attn.reshape(b, n, N_HEADS * HEAD_DIM)
        return attn @ Wout + bout

    def _L2_ffn_ref(x, Wr, Wg, Wu, Wd):
        import jax, jax.numpy as jnp
        import numpy as np
        B, T, D = (4, 256, 256)
        E = 8
        K = 2
        F = 1024 // (E // 2)
        probs = jax.nn.softmax(x @ Wr, axis=-1)
        topk_w, topk_idx = jax.lax.top_k(probs, K)
        topk_w = topk_w / jnp.sum(topk_w, axis=-1, keepdims=True)
        output = jnp.zeros_like(x)
        for i in range(E):
            sel = topk_idx == i
            w_i = jnp.sum(topk_w * sel.astype(x.dtype), axis=-1, keepdims=True)
            h = jax.nn.silu(x @ Wg[i]) * (x @ Wu[i])
            e_out = h @ Wd[i]
            output = output + w_i * e_out
        return output

    def _L3_xattn_ref(text_hidden, vision_tokens, vision_mask, Wq, Wk, Wv, Wo):
        import jax, jax.numpy as jnp
        import numpy as np
        N_HEADS = 16
        N_KV_HEADS = 8
        HEAD_DIM = 128
        D_TEXT = 256
        D_VISION = 128
        GROUPS = N_HEADS // N_KV_HEADS
        B, T_text, _ = text_hidden.shape
        T_vis = vision_tokens.shape[1]
        scale = jnp.float32(np.sqrt(HEAD_DIM))
        q = (text_hidden @ Wq).reshape(B, T_text, N_HEADS, HEAD_DIM).transpose(0, 2, 1, 3)
        k = (vision_tokens @ Wk).reshape(B, T_vis, N_KV_HEADS, HEAD_DIM).transpose(0, 2, 1, 3)
        v = (vision_tokens @ Wv).reshape(B, T_vis, N_KV_HEADS, HEAD_DIM).transpose(0, 2, 1, 3)
        k = jnp.repeat(k, GROUPS, axis=1)
        v = jnp.repeat(v, GROUPS, axis=1)
        scores = jnp.einsum('bhtd,bhsd->bhts', q, k) / scale
        mask = vision_mask[:, None, None, :]
        scores = jnp.where(mask, scores, -jnp.inf)
        attn = jax.nn.softmax(scores, axis=-1)
        attn = jnp.nan_to_num(attn, nan=0.0)
        out = jnp.einsum('bhts,bhsd->bhtd', attn, v)
        out = out.transpose(0, 2, 1, 3).reshape(B, T_text, N_HEADS * HEAD_DIM)
        return out @ Wo

    def _L3_ffn_ref(x, router_w, down_w, up_w):
        import jax, jax.numpy as jnp
        import numpy as np
        H = 256
        E = 8
        K = 2
        I = 16
        logits = jnp.einsum('bth,eh->bte', x, router_w)
        weights = jax.nn.softmax(logits, axis=-1)
        top_w, top_idx = jax.lax.top_k(weights, K)
        topk_mask = jnp.sum(jax.nn.one_hot(top_idx, E, dtype=x.dtype), axis=-2)
        gate = weights * topk_mask
        h = jnp.einsum('bth,eih->beti', x, down_w)
        a = jax.nn.silu(h)
        expert_out = jnp.einsum('beti,ehi->beth', a, up_w)
        out = jnp.einsum('beth,bte->bth', expert_out, gate)
        return out
    x = x + jnp.tanh(g_xattn[0]) * _L0_xattn_ref(_layernorm(x, axis=-1), ctx_1024, L0_xattn_Wq, L0_xattn_bq, L0_xattn_Wk, L0_xattn_bk, L0_xattn_Wv, L0_xattn_bv, L0_xattn_Wkv_dca, L0_xattn_bkv_dca, L0_xattn_qn_w, L0_xattn_qn_b, L0_xattn_kn_w, L0_xattn_kn_b, L0_xattn_kn_dca_w, L0_xattn_kn_dca_b, L0_xattn_Wo, L0_xattn_bo)
    x = x + jnp.tanh(g_ffn[0]) * _L0_ffn_ref(_layernorm(x, axis=-1), L0_ffn_w_gate, L0_ffn_wi_0, L0_ffn_wi_1, L0_ffn_wo)
    x = x + jnp.tanh(g_xattn[1]) * _L1_xattn_ref(_layernorm(x, axis=-1), ctx_1024, L1_xattn_Wq, L1_xattn_Wk, L1_xattn_Wv, L1_xattn_Wo, L1_xattn_gq, L1_xattn_gk)
    x = x + jnp.tanh(g_ffn[1]) * _L1_ffn_ref(_layernorm(x, axis=-1), L1_ffn_Wr, L1_ffn_Wg, L1_ffn_Wu, L1_ffn_Wd)
    x = x + jnp.tanh(g_xattn[2]) * _L2_xattn_ref(_layernorm(x, axis=-1), ctx_1024, fside_BxSx2_0, fside_BxSx2_0, L2_xattn_Wq, L2_xattn_Wkv, L2_xattn_Wout, L2_xattn_bout)
    x = x + jnp.tanh(g_ffn[2]) * _L2_ffn_ref(_layernorm(x, axis=-1), L2_ffn_Wr, L2_ffn_Wg, L2_ffn_Wu, L2_ffn_Wd)
    x = x + jnp.tanh(g_xattn[3]) * _L3_xattn_ref(_layernorm(x, axis=-1), ctx_1024, mask_BxS2_bf1, L3_xattn_Wq, L3_xattn_Wk, L3_xattn_Wv, L3_xattn_Wo)
    x = x + jnp.tanh(g_ffn[3]) * _L3_ffn_ref(_layernorm(x, axis=-1), L3_ffn_router_w, L3_ffn_down_w, L3_ffn_up_w)
    return x

_drawn_inputs = setup_inputs


def setup_inputs(seed=0):
    import zlib

    import numpy as np

    out = dict(_drawn_inputs(seed))
    spreads = {'L0_xattn_bq': (0.0, 0.1),
     'L0_xattn_bk': (0.0, 0.1),
     'L0_xattn_bv': (0.0, 0.1),
     'L0_xattn_bkv_dca': (0.0, 0.1),
     'L0_xattn_qn_w': (1.0, 0.541),
     'L0_xattn_qn_b': (0.0, 0.4),
     'L0_xattn_kn_w': (1.0, 0.6),
     'L0_xattn_kn_b': (0.0, 0.8),
     'L0_xattn_kn_dca_w': (1.0, 0.6),
     'L0_xattn_kn_dca_b': (0.0, 0.8),
     'L0_xattn_bo': (0.0, 0.1),
     'L1_xattn_gq': (1.0, 0.2),
     'L1_xattn_gk': (1.0, 0.2),
     'L2_xattn_bout': (0.0, 0.1)}
    factors = {'L3_xattn_Wq': 8.0, 'L3_xattn_Wk': 8.0}
    for name, (base, spread) in spreads.items():
        noise = np.random.default_rng([zlib.crc32(name.encode()), seed]).standard_normal(out[name].shape)
        drawn = base * np.exp(spread * noise) if base else spread * noise
        out[name] = jnp.asarray(drawn.astype(out[name].dtype))
    for name, factor in factors.items():
        out[name] = (out[name] * factor).astype(out[name].dtype)
    return out
```

```python
from contextlib import ExitStack

import concourse.bass as bass
from concourse import mybir

F32 = mybir.dt.float32
U32 = mybir.dt.uint32
I32 = mybir.dt.int32
U8 = mybir.dt.uint8
ALU = mybir.AluOpType
ACT = mybir.ActivationFunctionType
AX = mybir.AxisListType.X

P = 128
PI = 3.141592653589793
BATCH, SEQ, DIM, CTX = 32, 64, 256, 128
TILES = BATCH * SEQ // P
KC = DIM // P
EXPERTS = 8
LN_EPS = 1e-5
CHUNK_HEADS = 8


def sem(signal):
    return signal[0]


def per(signal):
    return signal[1]


def at(signal, tile, n):
    return tile * signal[1] + (signal[2] + n)


def over_tiles(eng, body, lead=1, last=TILES - 1):
    for i in range(lead):
        body(i)
    with eng.Fori(lead, last) as i:
        body(i)
    body(last)


def first(i):
    return isinstance(i, int) and i == 0


def is_last(i):
    return isinstance(i, int) and i == TILES - 1


def flamingo_kernel(nc, io, out, parts):
    ctx = ExitStack()
    with ctx:
        signals, in_use = {}, []

        def sb(name, shape, dt=F32):
            return ctx.enter_context(nc.sbuf_tensor(name, shape, dt))

        def ps(name):
            return ctx.enter_context(nc.psum_tensor(name, [P, 512], F32))

        def counted(name, n):
            if name not in signals:
                signals[name] = [ctx.enter_context(nc.semaphore(name)), 0, 0]
            signals[name][1] = n
            in_use.append(signals[name])
            return signals[name]

        def block_ends():
            for one in in_use:
                one[2] += TILES * one[1]
            del in_use[:]

        x = sb("x", [P, TILES, DIM])
        attn_w = sb("attn_w", [P, 18432])
        ffn_w = sb("ffn_w", [P, 12288])
        ident = sb("ident", [P, P])
        ones = sb("ones", [P, P])
        gates_raw = sb("gates_raw", [P, 8])
        tanh_g = sb("tanh_g", [P, 8])
        half_g = sb("half_g", [P, 4])
        quarter_g = sb("quarter_g", [P, 4])
        minus_half = sb("minus_half", [P, 32])
        ln_eps = sb("ln_eps", [P, 1])
        rms_eps = sb("rms_eps", [P, 4])
        head_eps = sb("head_eps", [P, 32])
        iota8 = sb("iota8", [P, EXPERTS])
        small = {
            "st": sb("st", [P, 6]), "mv": sb("mv", [P, 2]), "rstd": sb("rstd", [P, 1]),
            "var": sb("var", [P, 1]),
        }
        xn = sb("xn", [P, DIM])
        xcT = sb("xcT", [P, 3, P])
        c_tok = sb("c_tok", [P, CTX])
        c_even = sb("c_even", [P, 2, CTX])
        c_odd = sb("c_odd", [P, 2, CTX])
        bank_t = [ps("bank_t0"), ps("bank_t1")]
        bank_p = [ps("bank_p0"), ps("bank_p1")]
        bank_s = [ps("bank_s0"), ps("bank_s1")]
        bank_o = ps("bank_o")
        bank_y = ps("bank_y")

        weights_in = {n: ctx.enter_context(nc.semaphore(f"w_{n}")) for n in
                      ("first", "l0x", "l0f", "l1x", "l1f", "l2x", "l2f", "l3x", "l3f")}
        w_count = {n: 0 for n in weights_in}
        setup = ctx.enter_context(nc.semaphore("setup"))
        gates_tanh = ctx.enter_context(nc.semaphore("gates_tanh"))
        stood_apart = ctx.enter_context(nc.semaphore("stood_apart"))
        gates_scaled = ctx.enter_context(nc.semaphore("gates_scaled"))
        out_stored = ctx.enter_context(nc.semaphore("out_stored"))

        def load(sp, key, dst, src):
            sp.dma_start(dst, src).then_inc(weights_in[key], 16)
            w_count[key] += 16

        ctx_rows = io["ctx_1024"].rearrange("b s c -> (b s) c").rearrange("(n p) c -> n p c", p=P)
        ctx_by_row = io["ctx_1024"].rearrange("(n b) s c -> n s b c", b=2)

        def aw(off, *shape):
            n = 1
            for s in shape:
                n *= s
            ap = attn_w[:, off:off + n]
            if len(shape) == 2:
                return ap.rearrange("p (a b) -> p a b", a=shape[0])
            if len(shape) == 3:
                return ap.rearrange("p (a b c) -> p a b c", a=shape[0], b=shape[1])
            return ap

        def fw(off, *shape):
            n = 1
            for s in shape:
                n *= s
            ap = ffn_w[:, off:off + n]
            if len(shape) == 2:
                return ap.rearrange("p (a b) -> p a b", a=shape[0])
            if len(shape) == 3:
                return ap.rearrange("p (a b c) -> p a b c", a=shape[0], b=shape[1])
            return ap

        def wait_apart(eng, sem, value):
            eng.wait_ge(sem, value)
            eng.sem_inc(stood_apart, 1)

        def ln_signals():
            S = counted
            return dict(stats=S("ln_stats", 1), var=S("ln_var", 1), aggr=S("ln_aggr", 1), rstd=S("ln_rstd", 1), xn=S("xn_ready", 1),
                        turned=S("x_turned", 1), xT=S("xT_ready", 1))

        def dve_layernorm(dve, s, i, x_done):
            if x_done is not None:
                x_done()
            if not first(i):
                dve.wait_ge(sem(s["xn"]), at(s["xn"], i, 0))
            dve.bn_stats(small["st"][:, :], x[:, i, :]).then_inc(sem(s["stats"]), 1)
            wait_apart(dve, sem(s["stats"]), at(s["stats"], i, 1))
            dve.bn_aggr(small["mv"][:, :], small["st"][:, :]).then_inc(sem(s["aggr"]), 1)
            dve.wait_ge(sem(s["rstd"]), at(s["rstd"], i, 1))
            if not first(i):
                dve.wait_ge(sem(s["turned"]), at(s["turned"], i, 0))
            dve.tensor_scalar(xn[:, :], x[:, i, :], small["mv"][:, 0:1], small["rstd"][:, 0:1],
                              ALU.subtract, ALU.mult).then_inc(sem(s["xn"]), 1)

        def pool_rstd(pool, s, i):
            pool.wait_ge(sem(s["aggr"]), at(s["aggr"], i, 1))
            if not first(i):
                pool.wait_ge(sem(s["xn"]), at(s["xn"], i, 0))
            pool.tensor_tensor(small["var"][:, :], small["mv"][:, 1:2], ln_eps[:, :], ALU.add)\
                .then_inc(sem(s["var"]), 1)
            pool.wait_ge(sem(s["var"]), at(s["var"], i, 1))
            pool.tensor_tensor(small["rstd"][:, :], small["var"][:, :], minus_half[:, 0:1], ALU.pow)\
                .then_inc(sem(s["rstd"]), 1)

        def pe_turn_x(pe, s, i, bank, c_in=None, bank_free=None):
            pe.wait_ge(sem(s["xn"]), at(s["xn"], i, 1))
            if bank_free is not None:
                bank_free()
            for k in range(KC):
                mm = pe.transpose(bank[:, k * P:(k + 1) * P], xn[:, k * P:(k + 1) * P], ident[:, :])
            if c_in is not None:
                c_in()
                mm = pe.transpose(bank[:, 2 * P:3 * P], c_tok[:, :], ident[:, :])
            mm.then_inc(sem(s["turned"]), 1)

        with nc.Block() as block:
            @block.sync
            def _(sp):
                sp.dma_start(x[:, :, :], io["x"].rearrange("b s d -> (b s) d").rearrange("(n p) d -> p n d", p=P))\
                    .then_inc(weights_in["first"], 16)
                sp.dma_start(gates_raw[:, 0:4], io["g_xattn"].rearrange("(a g) -> a g", a=1).broadcast_to([P, 4]))\
                    .then_inc(weights_in["first"], 16)
                sp.dma_start(gates_raw[:, 4:8], io["g_ffn"].rearrange("(a g) -> a g", a=1).broadcast_to([P, 4]))\
                    .then_inc(weights_in["first"], 16)

            @block.gpsimd
            def _(pool):
                pool.memset(ident[:, :], 0.0).then_inc(setup, 1)
                pool.memset(ones[:, :], 1.0).then_inc(setup, 1)
                pool.memset(c_even[:, :, :], 0.0).then_inc(setup, 1)
                pool.memset(c_odd[:, :, :], 0.0).then_inc(setup, 1)
                pool.memset(minus_half[:, :], -0.5).then_inc(setup, 1)
                pool.memset(ln_eps[:, :], LN_EPS).then_inc(setup, 1)
                pool.memset(rms_eps[:, :], P * LN_EPS).then_inc(setup, 1)
                pool.memset(head_eps[:, :], 16 * 1e-6).then_inc(setup, 1)
                pool.iota(iota8[:, :], [[1, EXPERTS]], base=0, channel_multiplier=0,
                          allow_small_or_imprecise_dtypes=True).then_inc(setup, 1)
                pool.wait_ge(setup, 9)
                pool.affine_select(out=ident[:, :], in_=ident[:, :], compare_op=ALU.not_equal, fill=1.0, base=0,
                                   pattern=[[-1, P]], channel_multiplier=1).then_inc(setup, 1)

            @block.scalar
            def _(act):
                act.wait_ge(weights_in["first"], 48)
                act.activation(tanh_g[:, :], gates_raw[:, :], ACT.Tanh).then_inc(gates_tanh, 1)

            @block.vector
            def _(dve):
                dve.wait_ge(gates_tanh, 1)
                dve.tensor_scalar(half_g[:, :], tanh_g[:, 4:8], 0.5, None, ALU.mult).then_inc(gates_scaled, 1)
                dve.tensor_scalar(quarter_g[:, :], tanh_g[:, 4:8], 0.25, None, ALU.mult).then_inc(gates_scaled, 1)

        lg = sb("lg", [P, EXPERTS])
        top = sb("top", [P, 8])
        top_i = sb("top_i", [P, 8], U32)
        top_f = sb("top_f", [P, 2])
        lead = sb("lead", [P, 1])
        lead_t = sb("lead_t", [P, 1])
        g_first = sb("g_first", [P, 1])
        g_second = sb("g_second", [P, 1])
        pick = sb("pick", [P, 2, EXPERTS])
        gate = sb("gate", [P, EXPERTS])
        th = sb("th", [P, 2, 256])
        hh = sb("hh", [P, 2, 256])
        hT = sb("hT", [P, 2, 2, P])

        def moe_part(layer, key, hid, loads):
            fk = hid // 2 if hid > P else hid
            fc = hid // fk
            wgu = fw(0, KC * EXPERTS, 2 * hid)
            wd = fw(KC * EXPERTS * 2 * hid, fc * EXPERTS, DIM)
            wr = router[:, layer, :, :]
            s = ln_signals()
            S = counted
            logits = S("logits_ready", 1)
            lg_in = S("logits_copied", 1)
            g_steps = S("gate_steps", 8)
            gated = S("gates_ready", 1)
            lead_s = S("lead_tanh", 1)
            gu = S("gate_up_ready", EXPERTS)
            tanh = S("tanh_ready", EXPERTS)
            hid1 = S("hidden_half", EXPERTS)
            hid2 = S("hidden_ready", EXPERTS)
            turned = S("hidden_turned", EXPERTS)
            hTr = S("hiddenT_ready", EXPERTS)
            down = S("down_ready", EXPERTS)
            added = S("expert_added", EXPERTS)
            nw = loads()

            with nc.Block() as block:
                @block.tensor
                def _(pe):
                    pe.wait_ge(weights_in[key], nw)

                    def turn_x(i):
                        pe_turn_x(pe, s, i, bank_s[1], bank_free=None if first(i) else
                                  (lambda: pe.wait_ge(sem(s["xT"]), at(s["xT"], i, 0))))

                    def route(i):
                        pe.wait_ge(sem(s["xT"]), at(s["xT"], i, 1))
                        if not first(i):
                            pe.wait_ge(sem(lg_in), at(lg_in, i, 0))
                        for k in range(KC):
                            mm = pe.matmul(bank_s[0][:, 0:EXPERTS], xcT[:, k, :], wr[:, k, :],
                                           start=(k == 0), stop=(k == KC - 1))
                        mm.then_inc(sem(logits), 1)

                    def gate_up(i, e):
                        if not (first(i) and e < 2):
                            pe.wait_ge(sem(hid2), at(hid2, i, e - 1))
                        for k in range(KC):
                            mm = pe.matmul(bank_p[e % 2][:, 0:2 * hid], xcT[:, k, :], wgu[:, k * EXPERTS + e, :],
                                           start=(k == 0), stop=(k == KC - 1))
                        mm.then_inc(sem(gu), 1)

                    def turn_h(i, e):
                        pe.wait_ge(sem(hid2), at(hid2, i, e + 1))
                        if not (first(i) and e < 2):
                            pe.wait_ge(sem(hTr), at(hTr, i, e - 1))
                        for c in range(fc):
                            mm = pe.transpose(bank_t[e % 2][0:fk, c * P:(c + 1) * P],
                                              hh[:, e % 2, c * fk:(c + 1) * fk], ident[:, :])
                        mm.then_inc(sem(turned), 1)

                    def down_e(i, e):
                        pe.wait_ge(sem(hTr), at(hTr, i, e + 1))
                        if not (first(i) and e < 2):
                            pe.wait_ge(sem(added), at(added, i, e - 1))
                        b = (bank_o, bank_y)[e % 2]
                        for c in range(fc):
                            mm = pe.matmul(b[:, 0:DIM], hT[0:fk, e % 2, c, :], wd[0:fk, c * EXPERTS + e, :],
                                           start=(c == 0), stop=(c == fc - 1))
                        mm.then_inc(sem(down), 1)

                    def tile(i):
                        route(i)
                        for e in range(EXPERTS):
                            gate_up(i, e)
                            if e >= 1:
                                turn_h(i, e - 1)
                            elif not first(i):
                                turn_h(i - 1, EXPERTS - 1)
                            if e >= 2:
                                down_e(i, e - 2)
                            elif not first(i):
                                down_e(i - 1, EXPERTS - 2 + e)
                            if e == EXPERTS - 1 and not is_last(i):
                                turn_x(i + 1)

                    turn_x(0)
                    over_tiles(pe, tile)
                    turn_h(TILES - 1, EXPERTS - 1)
                    down_e(TILES - 1, EXPERTS - 2)
                    down_e(TILES - 1, EXPERTS - 1)

                @block.scalar
                def _(act):
                    def xT_in(i):
                        act.wait_ge(sem(s["turned"]), at(s["turned"], i, 1))
                        if not first(i):
                            act.wait_ge(sem(gu), at(gu, i, 0))
                        act.activation(xcT[:, 0:KC, :], bank_s[1][:, 0:KC * P].rearrange("p (a b) -> p a b", b=P),
                                       ACT.Copy).then_inc(sem(s["xT"]), 1)

                    def tanh_e(i, e):
                        act.wait_ge(sem(gu), at(gu, i, e + 1))
                        if not (first(i) and e < 2):
                            act.wait_ge(sem(hid1), at(hid1, i, e - 1))
                        act.activation(th[:, e % 2, 0:hid], bank_p[e % 2][:, 0:hid], ACT.Tanh, scale=0.5)\
                            .then_inc(sem(tanh), 1)

                    def hT_in(i, e):
                        act.wait_ge(sem(turned), at(turned, i, e + 1))
                        if not (first(i) and e < 2):
                            act.wait_ge(sem(down), at(down, i, e - 1))
                        act.activation(hT[0:fk, e % 2, 0:fc, :],
                                       bank_t[e % 2][0:fk, 0:fc * P].rearrange("p (a b) -> p a b", b=P),
                                       ACT.Copy).then_inc(sem(hTr), 1)

                    def lead_in(i):
                        act.wait_ge(sem(g_steps), at(g_steps, i, 4))
                        act.activation(lead_t[:, :], lead[:, :], ACT.Tanh, scale=0.5).then_inc(sem(lead_s), 1)

                    def tile(i):
                        for e in range(EXPERTS):
                            tanh_e(i, e)
                            if e == 1:
                                lead_in(i)
                            if e >= 1:
                                hT_in(i, e - 1)
                            elif not first(i):
                                hT_in(i - 1, EXPERTS - 1)
                            if e == EXPERTS - 1 and not is_last(i):
                                xT_in(i + 1)

                    xT_in(0)
                    over_tiles(act, tile)
                    hT_in(TILES - 1, EXPERTS - 1)

                @block.gpsimd
                def _(pool):
                    over_tiles(pool, lambda i: pool_rstd(pool, s, i))

                @block.vector
                def _(dve):
                    def hidden(i, e):
                        dve.wait_ge(sem(tanh), at(tanh, i, e + 1))
                        if not (first(i) and e < 2):
                            dve.wait_ge(sem(turned), at(turned, i, e - 1))
                        if not (first(i) and e == 0):
                            dve.wait_ge(sem(hid2), at(hid2, i, e))
                        g, u = bank_p[e % 2][:, 0:hid], bank_p[e % 2][:, hid:2 * hid]
                        dve.scalar_tensor_tensor(th[:, e % 2, 0:hid], th[:, e % 2, 0:hid], 1.0, g,
                                                 ALU.add, ALU.mult).then_inc(sem(hid1), 1)
                        dve.wait_ge(sem(hid1), at(hid1, i, e + 1))
                        dve.tensor_tensor(hh[:, e % 2, 0:hid], th[:, e % 2, 0:hid], u, ALU.mult)\
                            .then_inc(sem(hid2), 1)

                    def gates(i):
                        dve.wait_ge(sem(logits), at(logits, i, 1))
                        if not first(i):
                            dve.wait_ge(sem(added), at(added, i, 0))
                        dve.tensor_copy(lg[:, :], bank_s[0][:, 0:EXPERTS]).then_inc(sem(lg_in), 1)
                        wait_apart(dve, sem(lg_in), at(lg_in, i, 1))
                        dve.max(top[:, :], lg[:, :]).then_inc(sem(g_steps), 1)
                        wait_apart(dve, sem(g_steps), at(g_steps, i, 1))
                        dve.max_index(top_i[:, :], top[:, :], lg[:, :]).then_inc(sem(g_steps), 1)
                        dve.wait_ge(sem(g_steps), at(g_steps, i, 2))
                        dve.tensor_copy(top_f[:, :], top_i[:, 0:2]).then_inc(sem(g_steps), 1)
                        dve.tensor_tensor(lead[:, :], top[:, 0:1], top[:, 1:2], ALU.subtract).then_inc(sem(g_steps), 1)
                        dve.wait_ge(sem(lead_s), at(lead_s, i, 1))
                        dve.tensor_scalar(g_first[:, :], lead_t[:, :], 1.0, quarter_g[:, layer:layer + 1],
                                          ALU.add, ALU.mult).then_inc(sem(g_steps), 1)
                        dve.wait_ge(sem(g_steps), at(g_steps, i, 5))
                        dve.tensor_scalar(g_second[:, :], g_first[:, :], half_g[:, layer:layer + 1], -1.0,
                                          ALU.subtract, ALU.mult).then_inc(sem(g_steps), 1)
                        dve.wait_ge(sem(g_steps), at(g_steps, i, 6))
                        dve.tensor_scalar(pick[:, 0, :], iota8[:, :], top_f[:, 0:1], g_first[:, 0:1],
                                          ALU.is_equal, ALU.mult).then_inc(sem(g_steps), 1)
                        dve.tensor_scalar(pick[:, 1, :], iota8[:, :], top_f[:, 1:2], g_second[:, 0:1],
                                          ALU.is_equal, ALU.mult).then_inc(sem(g_steps), 1)
                        dve.wait_ge(sem(g_steps), at(g_steps, i, 8))
                        dve.tensor_tensor(gate[:, :], pick[:, 0, :], pick[:, 1, :], ALU.add).then_inc(sem(gated), 1)

                    def add(i, e):
                        dve.wait_ge(sem(down), at(down, i, e + 1))
                        if e == 0:
                            dve.wait_ge(sem(gated), at(gated, i, 1))
                        else:
                            dve.wait_ge(sem(added), at(added, i, e))
                        b = (bank_o, bank_y)[e % 2]
                        dve.scalar_tensor_tensor(x[:, i, :], b[:, 0:DIM], gate[:, e:e + 1], x[:, i, :],
                                                 ALU.mult, ALU.add).then_inc(sem(added), 1)

                    def tile(i):
                        for e in range(EXPERTS):
                            hidden(i, e)
                            if e >= 2:
                                add(i, e - 2)
                            elif not first(i):
                                add(i - 1, EXPERTS - 2 + e)
                            if e == 1:
                                gates(i)
                            if e == 3 and not is_last(i):
                                dve_layernorm(dve, s, i + 1, None)

                    dve_layernorm(dve, s, 0, None)
                    over_tiles(dve, tile)
                    add(TILES - 1, EXPERTS - 2)
                    add(TILES - 1, EXPERTS - 1)
            block_ends()

        router = sb("router", [P, 4, KC, EXPERTS])


        stage = sb("stage", [P, 2, 512])
        qn = sb("qn", [P, 2, 512])
        ssq = sb("ssq", [P, 32])
        ssq_e = sb("ssq_e", [P, 32])
        rnorm = sb("rnorm", [P, 32])
        qk_all = sb("qk_all", [P, 4096])
        qT = qk_all[:, 0:2048].rearrange("p (h t) -> p h t", h=16)
        kT = qk_all[:, 2048:4096].rearrange("p (h t) -> p h t", h=16)
        smax = sb("smax", [P, 4, 2, 8])
        E = sb("E", [P, 4, 8, SEQ])
        ssum = sb("ssum", [P, 4, 2, 8])
        srec = sb("srec", [P, 4, 2, 8])
        PT = sb("PT", [P, 4, 4, P])
        o_all = sb("o_all", [P, 2304])
        OT = o_all[:, 0:2048].rearrange("p (h t) -> p h t", h=16)
        gcol = sb("gcol", [P, 3])

        def load_context(sp, i, s, turned, rows_used=None):
            if not first(i):
                sp.wait_ge(sem(turned), at(turned, i, 0))
            sp.dma_start(c_tok[:, :], ctx_rows[i]).then_inc(sem(s["c"]), 16)
            if rows_used is not None:
                if not first(i):
                    sp.wait_ge(sem(rows_used), at(rows_used, i, 0))
                sp.dma_start(c_even[0:SEQ, :, :], ctx_by_row[i]).then_inc(sem(s["ce"]), 16)
                sp.dma_start(c_odd[SEQ:P, :, :], ctx_by_row[i]).then_inc(sem(s["co"]), 16)

        def absorb_part(key, q_heads, kv_heads, wq, wk, wv, wo, m_out, w2_out):
            S = counted
            group = q_heads // kv_heads
            pairs = q_heads // 2
            turned, copied, mul, kept = (S(n, 1) for n in ("w_turned", "w_copied", "w_multiplied", "w_kept"))
            wT, wqT = qn, stage
            jobs = 1 if wq is None else 2
            with nc.Block() as block:
                @block.tensor
                def _(pe):
                    pe.wait_ge(weights_in[key], w_count[key])
                    for j in range(pairs):
                        n = j * jobs
                        if n >= 2:
                            pe.wait_ge(sem(copied), copied[2] + n - 1)
                        if wq is not None:
                            for a in range(2):
                                for k in range(KC):
                                    h = 2 * j + a
                                    mm = pe.transpose(bank_t[0][:, (a * KC + k) * P:(a * KC + k + 1) * P],
                                                      wq[:, k, h * P:(h + 1) * P], ident[:, :])
                            mm.then_inc(sem(turned), 1)
                            for a, w in enumerate((wk, wv)):
                                mm = pe.transpose(bank_t[1][:, a * P:(a + 1) * P], w[:, j * P:(j + 1) * P], ident[:, :])
                            mm.then_inc(sem(turned), 1)
                            pe.wait_ge(sem(copied), copied[2] + n + 2)
                            if n >= 2:
                                pe.wait_ge(sem(kept), kept[2] + n)
                            for a in range(2):
                                for k in range(KC):
                                    mm = pe.matmul(bank_p[0][:, (a * KC + k) * P:(a * KC + k + 1) * P],
                                                   wqT[:, 0, (a * KC + k) * P:(a * KC + k + 1) * P],
                                                   wT[:, 0, 0:P], start=True, stop=True)
                            mm.then_inc(sem(mul), 1)
                            for a in range(2):
                                h = 2 * j + a
                                mm = pe.matmul(bank_p[1][:, a * DIM:(a + 1) * DIM], wT[:, 0, P:2 * P], wo[:, h, :],
                                               start=True, stop=True)
                            mm.then_inc(sem(mul), 1)
                        else:
                            for a in range(2):
                                h = 2 * j + a
                                mm = pe.transpose(bank_t[j % 2][:, a * P:(a + 1) * P], wv[:, h * P:(h + 1) * P],
                                                  ident[:, :])
                            mm.then_inc(sem(turned), 1)
                            pe.wait_ge(sem(copied), copied[2] + n + 1)
                            if n >= 2:
                                pe.wait_ge(sem(kept), kept[2] + n - 1)
                            for a in range(2):
                                h = 2 * j + a
                                mm = pe.matmul(bank_p[j % 2][:, a * DIM:(a + 1) * DIM], wT[:, j % 2, a * P:(a + 1) * P],
                                               wo[:, h, :], start=True, stop=True)
                            mm.then_inc(sem(mul), 1)

                @block.scalar
                def _(act):
                    for j in range(pairs):
                        n = j * jobs
                        act.wait_ge(sem(turned), turned[2] + n + 1)
                        if n >= 2:
                            act.wait_ge(sem(mul), mul[2] + (n if wq is not None else n - 1))
                        if wq is not None:
                            act.activation(wqT[:, 0, :], bank_t[0][:, :], ACT.Copy).then_inc(sem(copied), 1)
                            act.wait_ge(sem(turned), turned[2] + n + 2)
                            act.activation(wT[:, 0, 0:2 * P], bank_t[1][:, 0:2 * P], ACT.Copy).then_inc(sem(copied), 1)
                        else:
                            act.activation(wT[:, j % 2, 0:2 * P], bank_t[j % 2][:, 0:2 * P], ACT.Copy)\
                                .then_inc(sem(copied), 1)

                @block.vector
                def _(dve):
                    for j in range(pairs):
                        n = j * jobs
                        if wq is not None:
                            dve.wait_ge(sem(mul), mul[2] + n + 1)
                            dve.tensor_copy(m_out[:, :, 2 * j:2 * j + 2, :].rearrange("p k a c -> p a k c"),
                                            bank_p[0][:, :].rearrange("p (a k c) -> p a k c", a=2, k=KC))\
                                .then_inc(sem(kept), 1)
                            dve.wait_ge(sem(mul), mul[2] + n + 2)
                            b = bank_p[1]
                        else:
                            dve.wait_ge(sem(mul), mul[2] + n + 1)
                            b = bank_p[j % 2]
                        dve.tensor_copy(w2_out[:, 2 * j:2 * j + 2, :], b[:, :].rearrange("p (a d) -> p a d", a=2))\
                            .then_inc(sem(kept), 1)
            for sg in in_use:
                sg[2] += pairs * jobs
            del in_use[:]

        def wide_attention(layer, key, wq, wk, m, w2, score_scale):
            normed_qk = wk is not None
            jobs = 8 if normed_qk else 4
            s = ln_signals()
            S = counted
            s["c"], s["ce"], s["co"] = S("c_loaded", 16), S("c_even_loaded", 16), S("c_odd_loaded", 16)
            proj = S("projected", jobs)
            sq, sqs, sqe, rn = (S(n, jobs if normed_qk else 0) for n in ("squared", "squares_summed", "norm_eps", "norm_ready"))
            normed = S("qk_normed", jobs if normed_qk else 0)
            qk_turned = S("qk_turned", jobs if normed_qk else 0)
            qkT = S("qkT_ready", jobs)
            scores = S("scores_ready", 2)
            masked, recv = (S(n, 0 if normed_qk else 2) for n in ("scores_masked", "sum_inverse_valid"))
            smx, sub, ex, sm, rec, probs = (S(n, 2) for n in (
                "score_max", "scores_shifted", "exp_ready", "exp_sum", "sum_inverse", "probs_ready"))
            p_turned = S("probs_turned", 2)
            pT = S("probsT_ready", 2)
            pv = S("pv_ready", 4)
            oT = S("pvT_copied", 4)
            y = S("y_ready", 1)
            added = S("y_added", 1)
            banks_o = [bank_o, bank_p[0], bank_p[1], bank_o]

            with nc.Block() as block:
                @block.sync
                def _(sp):
                    over_tiles(sp, lambda i: load_context(sp, i, s, s["turned"], pv))

                @block.tensor
                def _(pe):
                    def project(i, j):
                        for h in range(4) if not normed_qk else [0]:
                            for k in range(KC):
                                if not normed_qk:
                                    mm = pe.matmul(bank_p[j % 2][:, h * P:(h + 1) * P], m[:, k, 4 * j + h, :],
                                                   xcT[:, k, :], start=(k == 0), stop=(k == KC - 1))
                                elif j < 4:
                                    mm = pe.matmul(bank_p[j % 2][:, :], xcT[:, k, :],
                                                   wq[:, k, j * 512:(j + 1) * 512], start=(k == 0), stop=(k == KC - 1))
                                elif k == 0:
                                    mm = pe.matmul(bank_p[j % 2][:, :], xcT[:, 2, :],
                                                   wk[:, (j - 4) * 512:(j - 3) * 512], start=True, stop=True)
                        mm.then_inc(sem(proj), 1)

                    def turn(i, j):
                        pe.wait_ge(sem(normed), at(normed, i, j + 1))
                        if j >= 2:
                            pe.wait_ge(sem(qkT), at(qkT, i, j - 1))
                        else:
                            pe.wait_ge(sem(s["xT"]), at(s["xT"], i, 1))
                        for h in range(4):
                            mm = pe.transpose(bank_t[j % 2][:, h * P:(h + 1) * P], qn[:, j % 2, h * P:(h + 1) * P],
                                              ident[:, :])
                        mm.then_inc(sem(qk_turned), 1)

                    def front(i):
                        pe_turn_x(pe, s, i, bank_t[0], c_in=lambda: pe.wait_ge(sem(s["c"]), at(s["c"], i, 16)))
                        pe.wait_ge(sem(s["xT"]), at(s["xT"], i, 1))
                        for j in range(jobs):
                            if j >= 2:
                                if normed_qk:
                                    turn(i, j - 2)
                                else:
                                    pe.wait_ge(sem(qkT), at(qkT, i, j - 1))
                            project(i, j)
                        if normed_qk:
                            turn(i, jobs - 2)
                            turn(i, jobs - 1)
                        pe.wait_ge(sem(qkT), at(qkT, i, jobs))
                        for g in range(2):
                            if not first(i):
                                pe.wait_ge(sem(sub), at(sub, i - 1, g + 1))
                            for h in range(8):
                                for b in range(2):
                                    rows = slice(b * SEQ, (b + 1) * SEQ)
                                    keys = kT[:, 8 * g + h, rows] if normed_qk else xcT[:, 2, rows]
                                    mm = pe.matmul(bank_s[g][rows, h * SEQ:(h + 1) * SEQ], qT[:, 8 * g + h, rows],
                                                   keys, start=True, stop=True)
                            mm.then_inc(sem(scores), 1)

                    def pv_job(i, g, b):
                        if b == 0:
                            pe.wait_ge(sem(pT), at(pT, i, g + 1))
                        n = 2 * g + b
                        if n == 0:
                            pe.wait_ge(sem(s["ce"]), at(s["ce"], i, 16))
                            pe.wait_ge(sem(s["co"]), at(s["co"], i, 16))
                        if n == 3:
                            pe.wait_ge(sem(oT), at(oT, i, 1))
                        for a, c in enumerate((c_even, c_odd)):
                            mm = pe.matmul(banks_o[n][:, a * 256:(a + 1) * 256], c[:, b, :],
                                           PT[:, g, :, b * SEQ:(b + 1) * SEQ], start=True, stop=True)
                        mm.then_inc(sem(pv), 1)

                    def back(i):
                        for g in range(2):
                            pe.wait_ge(sem(probs), at(probs, i, g + 1))
                            for a in range(4):
                                mm = pe.transpose(bank_t[g][:, a * P:(a + 1) * P],
                                                  E[:, g, 2 * a:2 * a + 2, :].rearrange("p a b -> p (a b)"), ident[:, :])
                            mm.then_inc(sem(p_turned), 1)
                        for g in range(2):
                            for b in range(2):
                                pv_job(i, g, b)
                        for g in range(2):
                            pe.wait_ge(sem(oT), at(oT, i, 2 * g + 2))
                            if g == 0 and not first(i):
                                pe.wait_ge(sem(added), at(added, i, 0))
                            for h in range(8):
                                mm = pe.matmul(bank_y[:, 0:DIM], OT[:, 8 * g + h, :], w2[:, 8 * g + h, :],
                                               start=(g == 0 and h == 0), stop=(g == 1 and h == 7))
                        mm.then_inc(sem(y), 1)

                    def tile(i):
                        front(i)
                        if not first(i):
                            back(i - 1)

                    over_tiles(pe, tile)
                    back(TILES - 1)

                @block.scalar
                def _(act):
                    def square(i, j):
                        act.wait_ge(sem(proj), at(proj, i, j + 1))
                        if not (first(i) and j < 2):
                            act.wait_ge(sem(sqs), at(sqs, i, j - 1))
                        act.activation(stage[:, j % 2, :], bank_p[j % 2][:, :], ACT.Square).then_inc(sem(sq), 1)

                    def copy_T(i, j):
                        act.wait_ge(sem(qk_turned), at(qk_turned, i, j + 1))
                        if j == 0 and not first(i):
                            act.wait_ge(sem(scores), at(scores, i, 0))
                        src = bank_t[j % 2][:, :].rearrange("p (h t) -> p h t", h=4)
                        if j < 4:
                            act.activation(qT[:, 4 * j:4 * j + 4, :], src, ACT.Copy).then_inc(sem(qkT), 1)
                        else:
                            act.activation(kT[:, 4 * j - 16:4 * j - 12, :], src, ACT.Copy, scale=gcol[:, 2:3])\
                                .then_inc(sem(qkT), 1)

                    def front(i):
                        act.wait_ge(sem(s["turned"]), at(s["turned"], i, 1))
                        if not first(i):
                            act.wait_ge(sem(scores), at(scores, i, 0))
                        act.activation(xcT[:, :, :], bank_t[0][:, 0:3 * P].rearrange("p (a b) -> p a b", b=P),
                                       ACT.Copy).then_inc(sem(s["xT"]), 1)
                        for j in range(jobs):
                            if normed_qk:
                                square(i, j)
                                if j >= 2:
                                    copy_T(i, j - 2)
                            else:
                                act.wait_ge(sem(proj), at(proj, i, j + 1))
                                act.activation(qT[:, 4 * j:4 * j + 4, :],
                                               bank_p[j % 2][:, :].rearrange("p (h t) -> p h t", h=4), ACT.Copy)\
                                    .then_inc(sem(qkT), 1)
                        if normed_qk:
                            copy_T(i, jobs - 2)
                            copy_T(i, jobs - 1)

                    def copy_probs(i):
                        for g in range(2):
                            act.wait_ge(sem(p_turned), at(p_turned, i, g + 1))
                            act.activation(PT[:, g, :, :], bank_t[g][:, :].rearrange("p (a t) -> p a t", a=4), ACT.Copy)\
                                .then_inc(sem(pT), 1)

                    def exps(i):
                        for g in range(2):
                            act.wait_ge(sem(sub), at(sub, i, g + 1))
                            act.activation(E[:, g, :, :], E[:, g, :, :], ACT.Exp, scale=score_scale).then_inc(sem(ex), 1)

                    def tile(i):
                        front(i)
                        if not first(i):
                            copy_probs(i - 1)
                        exps(i)

                    over_tiles(act, tile)
                    copy_probs(TILES - 1)

                @block.gpsimd
                def _(pool):
                    def tile(i):
                        if normed_qk:
                            for j in range(jobs):
                                c = slice(4 * j, 4 * j + 4)
                                pool.wait_ge(sem(sqs), at(sqs, i, j + 1))
                                pool.tensor_tensor(ssq_e[:, c], ssq[:, c], rms_eps[:, 0:4], ALU.add).then_inc(sem(sqe), 1)
                                pool.wait_ge(sem(sqe), at(sqe, i, j + 1))
                                pool.tensor_tensor(rnorm[:, c], ssq_e[:, c], minus_half[:, 0:4], ALU.pow)\
                                    .then_inc(sem(rn), 1)
                        if not is_last(i):
                            pool_rstd(pool, s, i + 1)
                    pool_rstd(pool, s, 0)
                    over_tiles(pool, tile)

                @block.vector
                def _(dve):
                    def front(i):
                        for j in range(jobs):
                            c = slice(4 * j, 4 * j + 4)
                            dve.wait_ge(sem(sq), at(sq, i, j + 1))
                            if not first(i):
                                dve.wait_ge(sem(normed), at(normed, i, j))
                            dve.tensor_reduce(ssq[:, c], stage[:, j % 2, :].rearrange("p (h d) -> p h d", h=4), AX, ALU.add)\
                                .then_inc(sem(sqs), 1)
                            dve.wait_ge(sem(rn), at(rn, i, j + 1))
                            if j >= 2:
                                dve.wait_ge(sem(qk_turned), at(qk_turned, i, j - 1))
                            dve.tensor_tensor(qn[:, j % 2, :].rearrange("p (h d) -> p h d", h=4),
                                              bank_p[j % 2][:, :].rearrange("p (h d) -> p h d", h=4),
                                              rnorm[:, c].unsqueeze(2).broadcast_to([P, 4, P]), ALU.mult)\
                                .then_inc(sem(normed), 1)

                    def shift(i, g):
                        dve.wait_ge(sem(scores), at(scores, i, g + 1))
                        if not first(i):
                            dve.wait_ge(sem(p_turned), at(p_turned, i - 1, g + 1))
                        src = bank_s[g][:, :].rearrange("p (h k) -> p h k", h=8)
                        if not normed_qk:
                            dve.tensor_tensor(E[:, g, :, :], src,
                                              mask_add[:, i, :].unsqueeze(1).broadcast_to([P, 8, SEQ]), ALU.add)\
                                .then_inc(sem(masked), 1)
                            dve.wait_ge(sem(masked), at(masked, i, g + 1))
                            src = E[:, g, :, :]
                        dve.tensor_reduce(smax[:, g, 0, :], src, AX, ALU.max).then_inc(sem(smx), 1)
                        dve.wait_ge(sem(smx), at(smx, i, g + 1))
                        dve.tensor_tensor(E[:, g, :, :], src, smax[:, g, 0, :].unsqueeze(2).broadcast_to([P, 8, SEQ]),
                                          ALU.subtract).then_inc(sem(sub), 1)

                    def weigh(i, g):
                        dve.wait_ge(sem(ex), at(ex, i, g + 1))
                        dve.tensor_reduce(ssum[:, g, 0, :], E[:, g, :, :], AX, ALU.add).then_inc(sem(sm), 1)
                        dve.wait_ge(sem(sm), at(sm, i, g + 1))
                        dve.reciprocal(srec[:, g, 0, :], ssum[:, g, 0, :]).then_inc(sem(rec), 1)
                        dve.wait_ge(sem(rec), at(rec, i, g + 1))
                        if not normed_qk:
                            dve.tensor_tensor(srec[:, g, 0, :], srec[:, g, 0, :], mask_any[:, i, :].broadcast_to([P, 8]), ALU.mult)\
                                .then_inc(sem(recv), 1)
                            dve.wait_ge(sem(recv), at(recv, i, g + 1))
                        dve.tensor_tensor(E[:, g, :, :], E[:, g, :, :],
                                          srec[:, g, 0, :].unsqueeze(2).broadcast_to([P, 8, SEQ]), ALU.mult)\
                            .then_inc(sem(probs), 1)

                    def copy_pv(i, n):
                        g, b = n // 2, n % 2
                        dve.wait_ge(sem(pv), at(pv, i, n + 1))
                        if n == 0 and not first(i):
                            dve.wait_ge(sem(y), at(y, i, 0))
                        for a in range(2):
                            ins = dve.tensor_copy(OT[:, 8 * g + a:8 * g + 8:2, b * SEQ:(b + 1) * SEQ],
                                                  banks_o[n][:, a * 256:(a + 1) * 256].rearrange("p (h t) -> p h t", h=4))
                        ins.then_inc(sem(oT), 1)

                    def add(i):
                        dve.wait_ge(sem(y), at(y, i, 1))
                        dve.scalar_tensor_tensor(x[:, i, :], bank_y[:, 0:DIM], tanh_g[:, layer:layer + 1], x[:, i, :],
                                                 ALU.mult, ALU.add).then_inc(sem(added), 1)

                    def tile(i):
                        if normed_qk:
                            front(i)
                        if not is_last(i):
                            dve_layernorm(dve, s, i + 1, None)
                        shift(i, 0)
                        if not first(i):
                            copy_pv(i - 1, 0)
                            copy_pv(i - 1, 1)
                        shift(i, 1)
                        if not first(i):
                            copy_pv(i - 1, 2)
                            copy_pv(i - 1, 3)
                        weigh(i, 0)
                        weigh(i, 1)
                        if not first(i):
                            add(i - 1)

                    dve_layernorm(dve, s, 0, None)
                    over_tiles(dve, tile)
                    for n in range(4):
                        copy_pv(TILES - 1, n)
                    add(TILES - 1)
            block_ends()

        mask_add = sb("mask_add", [P, TILES, SEQ])
        mask_u8 = sb("mask_u8", [P, TILES, SEQ], U8)
        mask_any = sb("mask_any", [P, TILES, 1])

        def run_l1x():
            wq, wk, wv = aw(0, KC, 2048), aw(4096, 2048), aw(6144, 2048)
            wo, w2 = aw(8192, 16, DIM), aw(12288, 16, DIM)
            scaled = ctx.enter_context(nc.semaphore("l1_gain"))
            with nc.Block() as block:
                @block.sync
                def _(sp):
                    load(sp, "l1x", wq, io["L1_xattn_Wq"].rearrange("(k p) n -> p k n", p=P))
                    load(sp, "l1x", wk, io["L1_xattn_Wk"])
                    load(sp, "l1x", wv, io["L1_xattn_Wv"])
                    load(sp, "l1x", wo, io["L1_xattn_Wo"].rearrange("(h p) d -> p h d", p=P))
                    load(sp, "l1x", gcol[:, 0:1], io["L1_xattn_gq"].rearrange("(p a) -> p a", a=1))
                    load(sp, "l1x", gcol[:, 1:2], io["L1_xattn_gk"].rearrange("(p a) -> p a", a=1))

                @block.vector
                def _(dve):
                    dve.wait_ge(weights_in["l1x"], w_count["l1x"])
                    dve.tensor_tensor(gcol[:, 2:3], gcol[:, 0:1], gcol[:, 1:2], ALU.mult).then_inc(scaled, 1)
            absorb_part("l1x", 16, 16, None, None, wv, wo, None, w2)
            wide_attention(1, "l1x", wq, wk, None, w2, float(P) ** 0.5)

        def run_l3x():
            wq, wk, wv = aw(0, KC, 2048), aw(4096, 1024), aw(5120, 1024)
            wo, m, w2 = aw(6144, 16, DIM), aw(10240, KC * 16, P), aw(14336, 16, DIM)
            m = m.rearrange("p (k h) c -> p k h c", k=KC)
            made = ctx.enter_context(nc.semaphore("mask_made"))
            with nc.Block() as block:
                @block.sync
                def _(sp):
                    load(sp, "l3x", wq, io["L3_xattn_Wq"].rearrange("(k p) n -> p k n", p=P))
                    load(sp, "l3x", wk, io["L3_xattn_Wk"])
                    load(sp, "l3x", wv, io["L3_xattn_Wv"])
                    load(sp, "l3x", wo, io["L3_xattn_Wo"].rearrange("(h p) d -> p h d", p=P))
                    rows = io["mask_BxS2_bf1"].rearrange("(n b) k -> b n k", b=2)
                    for b in range(2):
                        load(sp, "l3x", mask_u8[b * SEQ:(b + 1) * SEQ, :, :],
                             rows[b:b + 1].broadcast_to([SEQ, TILES, SEQ]))

                @block.vector
                def _(dve):
                    dve.wait_ge(weights_in["l3x"], w_count["l3x"])
                    dve.tensor_copy(mask_add[:, :, :], mask_u8[:, :, :]).then_inc(made, 1)
                    dve.wait_ge(made, 1)
                    dve.tensor_reduce(mask_any[:, :, 0], mask_add[:, :, :], AX, ALU.max).then_inc(made, 1)
                    dve.wait_ge(made, 2)
                    dve.tensor_scalar(mask_add[:, :, :], mask_add[:, :, :], 1.0, 1e30, ALU.subtract, ALU.mult)\
                        .then_inc(made, 1)
            absorb_part("l3x", 16, 8, wq, wk, wv, wo, m, w2)
            wide_attention(3, "l3x", None, None, m, w2, float(P) ** -0.5)

        head_mask = sb("head_mask", [P, 16])
        pair_mask = sb("pair_mask", [P, DIM])
        qkT_n = o_all[:, 0:512].rearrange("p (a t) -> p a t", a=4)
        v_pairs = o_all[:, 512:1024].rearrange("p (b d) -> p b d", b=2)
        o_sb = o_all[:, 1024:1280]
        oT_n = o_all[:, 1280:1536].rearrange("p (k t) -> p k t", k=KC)
        c_parts = o_all[:, 1536:2304].rearrange("p (n k r t) -> p n k r t", n=2, k=3, r=2)
        key_side = sb("key_side", [2, 2, SEQ])
        kv_bias = attn_w[0:2, 2048:2560].rearrange("p (n d) -> p n d", n=2)
        row_bias = attn_w[0:1, 2560:2816]
        out_bias = attn_w[0:1, 2816:3072]
        norm_rows = attn_w[0:6, 3072:3200]
        norm_cols = sb("norm_cols", [P, 6])
        mean_n = sb("mean_n", [P, 2, 32])
        ropes = sb("ropes", [P, TILES, 16])
        ropes_w = attn_w[:, 4096:4352].rearrange("p (n a) -> p n a", n=4)
        ropes_i = attn_w[:, 4352:4416].bitcast(I32)
        pos = sb("pos", [P, TILES, 2])

        def narrow_attention(layer, key, hd, wq, wo, k_weights, v_weights, keys_main):
            split = keys_main < SEQ
            heads = DIM // hd
            in_half = P // hd
            chunks = heads // 8
            segs = [(0, keys_main), (keys_main, SEQ)] if split else [(0, SEQ)]
            score_scale = float(hd) ** -0.5
            kb = qk_all[:, 0:2 * 2 * in_half * SEQ].rearrange("p (f b h t) -> p f b h t", f=2, b=2, h=in_half)
            s = ln_signals()
            S = counted
            s["c"] = S("c_loaded", 16)
            c_split = S("context_split", 2 * len(segs))
            qk = S("qk_projected", 1)
            v = S("v_projected", 1)
            v_in = S("v_spread", 1)
            steps = S("qk_steps", 4 if split else 3)
            sqr, sqe, rn = (S(n, 1 if split else 0) for n in ("squared", "norm_eps", "norm_ready"))
            normed = S("qk_normed", 1)
            qk_turned = S("qk_turned", 1)
            qkT = S("qkT_ready", 3 if split else 1)
            spread = S("keys_spread", 4)
            scores = S("scores_ready", chunks)
            smx, sub, sm, probs = (S(n, chunks * len(segs)) for n in (
                "score_max", "scores_shifted", "exp_sum", "probs_ready"))
            if not split:
                probs[1] = 0
            ex = S("exp_ready", chunks)
            rec = S("sum_inverse", chunks)
            nseg = len(segs)
            p_turned = S("probs_turned", chunks)
            pT = S("probsT_ready", chunks)
            pv = S("pv_ready", 1)
            o_in = S("pv_copied", 1)
            o_turned = S("pv_turned", 1)
            oT = S("pvT_ready", 1)
            y = S("y_ready", 1)
            added = S("y_added", 1)

            with nc.Block() as block:
                @block.sync
                def _(sp):
                    over_tiles(sp, lambda i: load_context(sp, i, s, s["turned"]))

                @block.tensor
                def _(pe):
                    def keys_of(part, b=None):
                        return c_parts[:, part, 0 if b is None else 1 + b, :, :].rearrange("p r t -> p (r t)")

                    def project(i):
                        pe_turn_x(pe, s, i, bank_t[0], c_in=lambda: pe.wait_ge(sem(s["c"]), at(s["c"], i, 16)))
                        pe.wait_ge(sem(s["xT"]), at(s["xT"], i, 1))
                        for k in range(KC):
                            pe.matmul(bank_p[0][:, 0:DIM], xcT[:, k, :], wq[:, k, :], start=(k == 0),
                                      stop=(not split and k == KC - 1))
                        if split:
                            pe.matmul(bank_p[0][:, 0:DIM], ones[0:1, :], row_bias[:, :], start=False, stop=True)
                        pe.wait_ge(sem(c_split), at(c_split, i, per(c_split)))
                        for n, w in enumerate(k_weights):
                            mm = pe.matmul(bank_p[0][:, DIM:2 * DIM], keys_of(n), w, start=(n == 0),
                                           stop=(not split and n == len(k_weights) - 1))
                        if split:
                            mm = pe.matmul(bank_p[0][:, DIM:2 * DIM], key_side[:, :, :], kv_bias[:, 0, :],
                                           start=False, stop=True)
                        mm.then_inc(sem(qk), 1)
                        if not first(i):
                            pe.wait_ge(sem(v_in), at(v_in, i, 0))
                        for b in range(2):
                            o = bank_p[1][:, b * DIM:(b + 1) * DIM]
                            for n, w in enumerate(v_weights):
                                mm = pe.matmul(o, keys_of(n, b), w, start=(n == 0),
                                               stop=(not split and n == len(v_weights) - 1))
                            if split:
                                mm = pe.matmul(o, key_side[:, :, :], kv_bias[:, 1, :], start=False, stop=True)
                        mm.then_inc(sem(v), 1)

                    def score(i):
                        pe.wait_ge(sem(normed), at(normed, i, 1))
                        if not first(i):
                            pe.wait_ge(sem(pT), at(pT, i, 0))
                        for a in range(4):
                            mm = pe.transpose(bank_t[1][:, a * P:(a + 1) * P], qn[:, 0, a * P:(a + 1) * P], ident[:, :])
                        mm.then_inc(sem(qk_turned), 1)
                        pe.wait_ge(sem(qkT), at(qkT, i, per(qkT)))
                        for g in range(chunks):
                            f, h0 = g * 8 // in_half, g * 8 % in_half
                            pe.wait_ge(sem(spread), at(spread, i, 2 * f + 2))
                            if not (first(i) and g < 2):
                                pe.wait_ge(sem(sub), at(sub, i, nseg * (g - 1)))
                            for b in range(2):
                                rows = slice(b * SEQ, (b + 1) * SEQ)
                                mm = pe.matmul(bank_s[g % 2][rows, :], qkT_n[:, f, rows], kb[:, f, b, h0:h0 + 8, :],
                                               start=True, stop=True)
                            mm.then_inc(sem(scores), 1)

                    def turn_probs(i, g):
                        if split:
                            pe.wait_ge(sem(probs), at(probs, i, nseg * (g + 1)))
                        else:
                            pe.wait_ge(sem(ex), at(ex, i, g + 1))
                        if g >= 2:
                            pe.wait_ge(sem(pT), at(pT, i, g - 1))
                        for a in range(4):
                            mm = pe.transpose(bank_t[g % 2][:, a * P:(a + 1) * P],
                                              E[:, g, 2 * a:2 * a + 2, :].rearrange("p a b -> p (a b)"), ident[:, :])
                        mm.then_inc(sem(p_turned), 1)

                    def weigh_values(i, g):
                        pe.wait_ge(sem(pT), at(pT, i, g + 1))
                        if g == 0:
                            pe.wait_ge(sem(v_in), at(v_in, i, 1))
                        for a in range(4):
                            c = slice((8 * g + 2 * a) * hd, (8 * g + 2 * a + 2) * hd)
                            for b in range(2):
                                rows = slice(b * SEQ, (b + 1) * SEQ)
                                mm = pe.matmul(bank_o[rows, c], PT[:, g, a, rows], v_pairs[:, b, c],
                                               start=True, stop=True)
                        if g == chunks - 1:
                            mm.then_inc(sem(pv), 1)

                    def values(i):
                        if not first(i):
                            pe.wait_ge(sem(o_in), at(o_in, i, 0))
                        for g in range(chunks):
                            weigh_values(i, g)

                    def finish(i):
                        pe.wait_ge(sem(o_in), at(o_in, i, 1))
                        for k in range(KC):
                            mm = pe.transpose(bank_t[0][:, k * P:(k + 1) * P], o_sb[:, k * P:(k + 1) * P], ident[:, :])
                        mm.then_inc(sem(o_turned), 1)
                        pe.wait_ge(sem(oT), at(oT, i, 1))
                        if not first(i):
                            pe.wait_ge(sem(added), at(added, i, 0))
                        for k in range(KC):
                            pe.matmul(bank_y[:, 0:DIM], oT_n[:, k, :], wo[:, k, :], start=(k == 0), stop=False)
                        pe.matmul(bank_y[:, 0:DIM], ones[0:1, :], out_bias[:, :], start=False, stop=True)\
                            .then_inc(sem(y), 1)

                    def tile(i):
                        project(i)
                        if not (isinstance(i, int) and i < 2):
                            finish(i - 2)
                        if not first(i):
                            for g in range(chunks):
                                turn_probs(i - 1, g)
                        score(i)
                        if not first(i):
                            values(i - 1)

                    over_tiles(pe, tile, lead=2)
                    finish(TILES - 2)
                    for g in range(chunks):
                        turn_probs(TILES - 1, g)
                    values(TILES - 1)
                    finish(TILES - 1)

                @block.scalar
                def _(act):
                    def front(i):
                        act.wait_ge(sem(s["turned"]), at(s["turned"], i, 1))
                        if not first(i):
                            act.wait_ge(sem(v), at(v, i, 0))
                        act.activation(xcT[:, :, :], bank_t[0][:, 0:3 * P].rearrange("p (a b) -> p a b", b=P),
                                       ACT.Copy).then_inc(sem(s["xT"]), 1)
                        src = bank_t[0][:, 2 * P:3 * P].rearrange("p (b t) -> p b t", b=2)
                        for n, (a, e) in enumerate(segs):
                            act.activation(c_parts[:, n, 0, :, a:e], src[:, :, a:e], ACT.Copy).then_inc(sem(c_split), 1)
                            act.activation(c_parts[:, n, 1:3, :, a:e],
                                           src[:, :, a:e].unsqueeze(2).broadcast_to([P, 2, 2, e - a]), ACT.Copy)\
                                .then_inc(sem(c_split), 1)

                    def turned_qk(i):
                        if split:
                            act.wait_ge(sem(steps), at(steps, i, 3))
                            act.activation(stage[:, 0, :], qn[:, 0, :], ACT.Square).then_inc(sem(sqr), 1)
                        act.wait_ge(sem(qk_turned), at(qk_turned, i, 1))
                        if not first(i):
                            act.wait_ge(sem(scores), at(scores, i, 0))
                        if not split:
                            act.activation(qkT_n[:, :, :], bank_t[1][:, :].rearrange("p (a t) -> p a t", a=4), ACT.Copy)\
                                .then_inc(sem(qkT), 1)
                            return
                        act.activation(qkT_n[:, 0:2, :], bank_t[1][:, 0:2 * P].rearrange("p (a t) -> p a t", a=2),
                                       ACT.Identity, scale=norm_cols[:, 0:1], bias=norm_cols[:, 1:2]).then_inc(sem(qkT), 1)
                        src = bank_t[1][:, 2 * P:4 * P].rearrange("p (f t) -> p f t", t=SEQ)
                        dst = qkT_n[:, 2:4, :].rearrange("p f (b t) -> p (f b) t", b=2)
                        for n, (a, e) in enumerate(segs):
                            act.activation(dst[:, :, a:e], src[:, :, a:e], ACT.Identity,
                                           scale=norm_cols[:, 2 + 2 * n:3 + 2 * n], bias=norm_cols[:, 3 + 2 * n:4 + 2 * n])\
                                .then_inc(sem(qkT), 1)

                    def exps(i, g):
                        act.wait_ge(sem(sub), at(sub, i, nseg * (g + 1)))
                        act.activation(E[:, g, :, :], E[:, g, :, :], ACT.Exp, scale=score_scale).then_inc(sem(ex), 1)

                    def copy_probs(i, g):
                        act.wait_ge(sem(p_turned), at(p_turned, i, g + 1))
                        act.activation(PT[:, g, :, :], bank_t[g % 2][:, :].rearrange("p (a t) -> p a t", a=4), ACT.Copy)\
                            .then_inc(sem(pT), 1)

                    def copy_oT(i):
                        act.wait_ge(sem(o_turned), at(o_turned, i, 1))
                        if not first(i):
                            act.wait_ge(sem(y), at(y, i, 0))
                        act.activation(oT_n[:, :, :], bank_t[0][:, 0:KC * P].rearrange("p (a b) -> p a b", b=P), ACT.Copy)\
                            .then_inc(sem(oT), 1)

                    def tile(i):
                        front(i)
                        if not (isinstance(i, int) and i < 2):
                            copy_oT(i - 2)
                        if not first(i):
                            for g in range(chunks):
                                copy_probs(i - 1, g)
                        turned_qk(i)
                        for g in range(chunks):
                            exps(i, g)

                    over_tiles(act, tile, lead=2)
                    copy_oT(TILES - 2)
                    for g in range(chunks):
                        copy_probs(TILES - 1, g)
                    copy_oT(TILES - 1)

                @block.gpsimd
                def _(pool):
                    def tile(i):
                        if split:
                            pool.wait_ge(sem(steps), at(steps, i, 4))
                            pool.tensor_tensor(ssq_e[:, :], ssq[:, :], head_eps[:, :], ALU.add).then_inc(sem(sqe), 1)
                            pool.wait_ge(sem(sqe), at(sqe, i, 1))
                            pool.tensor_tensor(rnorm[:, :], ssq_e[:, :], minus_half[:, 0:32], ALU.pow).then_inc(sem(rn), 1)
                        pool.wait_ge(sem(qkT), at(qkT, i, per(qkT)))
                        if not first(i):
                            pool.wait_ge(sem(scores), at(scores, i, 0))
                        for f in range(2):
                            for b in range(2):
                                pool.tensor_tensor(
                                    kb[:, f, b, :, :],
                                    qkT_n[:, 2 + f, b * SEQ:(b + 1) * SEQ].unsqueeze(1).broadcast_to([P, in_half, SEQ]),
                                    head_mask[:, 0:in_half].unsqueeze(2).broadcast_to([P, in_half, SEQ]), ALU.mult)\
                                    .then_inc(sem(spread), 1)
                        if not is_last(i):
                            pool_rstd(pool, s, i + 1)
                    pool_rstd(pool, s, 0)
                    over_tiles(pool, tile)

                @block.vector
                def _(dve):
                    def norm_qk(i):
                        src = bank_p[0][:, :].rearrange("p (h d) -> p h d", d=hd)
                        dst = qn[:, 0, :].rearrange("p (h d) -> p h d", d=hd)
                        dve.wait_ge(sem(qk), at(qk, i, 1))
                        if not first(i):
                            dve.wait_ge(sem(normed), at(normed, i, 0))
                        dve.tensor_reduce(mean_n[:, 0, :], src, AX, ALU.add).then_inc(sem(steps), 1)
                        dve.wait_ge(sem(steps), at(steps, i, 1))
                        dve.tensor_scalar(mean_n[:, 1, :], mean_n[:, 0, :], 1.0 / hd, None, ALU.mult).then_inc(sem(steps), 1)
                        dve.wait_ge(sem(steps), at(steps, i, 2))
                        if not first(i):
                            dve.wait_ge(sem(qk_turned), at(qk_turned, i, 0))
                        dve.tensor_tensor(dst, src, mean_n[:, 1, :].unsqueeze(2).broadcast_to([P, 32, hd]), ALU.subtract)\
                            .then_inc(sem(steps), 1)
                        dve.wait_ge(sem(sqr), at(sqr, i, 1))
                        dve.tensor_reduce(ssq[:, :], stage[:, 0, :].rearrange("p (h d) -> p h d", d=hd), AX, ALU.add)\
                            .then_inc(sem(steps), 1)
                        dve.wait_ge(sem(rn), at(rn, i, 1))
                        dve.tensor_tensor(dst, dst, rnorm[:, :].unsqueeze(2).broadcast_to([P, 32, hd]), ALU.mult)\
                            .then_inc(sem(normed), 1)

                    def rotate_qk(i):
                        src = bank_p[0][:, :].rearrange("p (h r) -> p h r", r=8)
                        pair = bank_p[0][:, :].rearrange("p (h r two) -> p h r two", r=4, two=2)
                        turn = stage[:, 0, :].rearrange("p (h r two) -> p h r two", r=4, two=2)
                        dve.wait_ge(sem(qk), at(qk, i, 1))
                        if not first(i):
                            dve.wait_ge(sem(normed), at(normed, i, 0))
                            dve.wait_ge(sem(qk_turned), at(qk_turned, i, 0))
                        dve.tensor_tensor(qn[:, 0, :].rearrange("p (h r) -> p h r", r=8), src,
                                          ropes[:, i, 0:8].unsqueeze(1).broadcast_to([P, 64, 8]), ALU.mult)\
                            .then_inc(sem(steps), 1)
                        for n in range(2):
                            dve.tensor_tensor(turn[:, :, :, n], pair[:, :, :, 1 - n],
                                              ropes[:, i, 8 + 4 * n:12 + 4 * n].unsqueeze(1).broadcast_to([P, 64, 4]),
                                              ALU.mult).then_inc(sem(steps), 1)
                        dve.wait_ge(sem(steps), at(steps, i, 3))
                        dve.tensor_tensor(qn[:, 0, :], qn[:, 0, :], stage[:, 0, :], ALU.add).then_inc(sem(normed), 1)

                    def spread_v(i):
                        dve.wait_ge(sem(v), at(v, i, 1))
                        if not first(i):
                            dve.wait_ge(sem(pv), at(pv, i - 1, 1))
                        dve.tensor_tensor(v_pairs[:, :, :], bank_p[1][:, :].rearrange("p (b d) -> p b d", b=2),
                                          pair_mask[:, :].unsqueeze(1).broadcast_to([P, 2, DIM]), ALU.mult)\
                            .then_inc(sem(v_in), 1)

                    def shift(i, g):
                        dve.wait_ge(sem(scores), at(scores, i, g + 1))
                        if not first(i):
                            dve.wait_ge(sem(p_turned), at(p_turned, i - 1, g + 1))
                        src = bank_s[g % 2][:, :].rearrange("p (h k) -> p h k", h=8)
                        for n, (a, e) in enumerate(segs):
                            dve.tensor_reduce(smax[:, g, n, :], src[:, :, a:e], AX, ALU.max).then_inc(sem(smx), 1)
                        for n, (a, e) in enumerate(segs):
                            dve.wait_ge(sem(smx), at(smx, i, nseg * g + n + 1))
                            dve.tensor_tensor(E[:, g, :, a:e], src[:, :, a:e],
                                              smax[:, g, n, :].unsqueeze(2).broadcast_to([P, 8, e - a]), ALU.subtract)\
                                .then_inc(sem(sub), 1)

                    def weigh(i, g):
                        dve.wait_ge(sem(ex), at(ex, i, g + 1))
                        for n, (a, e) in enumerate(segs):
                            dve.tensor_reduce(ssum[:, g, n, :], E[:, g, :, a:e], AX, ALU.add).then_inc(sem(sm), 1)
                        dve.wait_ge(sem(sm), at(sm, i, nseg * (g + 1)))
                        if not first(i):
                            dve.wait_ge(sem(o_in), at(o_in, i, 0))
                        dve.reciprocal(srec[:, g, 0:nseg, :], ssum[:, g, 0:nseg, :]).then_inc(sem(rec), 1)
                        if split:
                            dve.wait_ge(sem(rec), at(rec, i, g + 1))
                            for n, (a, e) in enumerate(segs):
                                dve.tensor_tensor(E[:, g, :, a:e], E[:, g, :, a:e],
                                                  srec[:, g, n, :].unsqueeze(2).broadcast_to([P, 8, e - a]), ALU.mult)\
                                    .then_inc(sem(probs), 1)

                    def copy_o(i):
                        dve.wait_ge(sem(pv), at(pv, i, 1))
                        if not first(i):
                            dve.wait_ge(sem(o_turned), at(o_turned, i, 0))
                        if split:
                            dve.tensor_copy(o_sb[:, :], bank_o[:, 0:DIM]).then_inc(sem(o_in), 1)
                        else:
                            dve.wait_ge(sem(rec), at(rec, i, chunks))
                            dve.tensor_tensor(o_sb[:, :].rearrange("p (g h d) -> p g h d", g=chunks, h=8),
                                              bank_o[:, 0:DIM].rearrange("p (g h d) -> p g h d", g=chunks, h=8),
                                              srec[:, 0:chunks, 0, :].unsqueeze(3).broadcast_to([P, chunks, 8, hd]),
                                              ALU.mult).then_inc(sem(o_in), 1)

                    def add(i):
                        dve.wait_ge(sem(y), at(y, i, 1))
                        dve.scalar_tensor_tensor(x[:, i, :], bank_y[:, 0:DIM], tanh_g[:, layer:layer + 1], x[:, i, :],
                                                 ALU.mult, ALU.add).then_inc(sem(added), 1)

                    def tile(i):
                        (norm_qk if split else rotate_qk)(i)
                        if not (isinstance(i, int) and i < 2):
                            add(i - 2)
                        for g in range(chunks):
                            shift(i, g)
                        if not is_last(i):
                            dve_layernorm(dve, s, i + 1, None)
                        if not first(i):
                            copy_o(i - 1)
                        spread_v(i)
                        for g in range(chunks):
                            weigh(i, g)

                    dve_layernorm(dve, s, 0, None)
                    over_tiles(dve, tile, lead=2)
                    add(TILES - 2)
                    copy_o(TILES - 1)
                    add(TILES - 1)
            block_ends()

        def make_masks(pool, step, hd):
            n = P // hd
            hm = head_mask[:, 0:n]
            step(pool.memset(hm, 1.0))
            pm = pair_mask[:, :].rearrange("p (j two d) -> p j two d", two=2, d=hd)
            for half in range(2):
                for odd in range(2):
                    step(pool.memset(pm[half * SEQ:(half + 1) * SEQ, :, odd, :], 1.0 if half == odd else 0.0))
            step(pool.affine_select(out=hm, in_=hm, compare_op=ALU.is_ge, fill=0.0, base=0, pattern=[[-hd, n]],
                                    channel_multiplier=1))
            step(pool.affine_select(out=hm, in_=hm, compare_op=ALU.is_ge, fill=0.0, base=hd - 1, pattern=[[hd, n]],
                                    channel_multiplier=-1))

        def in_turn(eng, sem):
            done = [0]

            def step(ins):
                done[0] += 1
                ins.then_inc(sem, 1)
                eng.wait_ge(sem, done[0])
            return step

        def run_l0x():
            hd, main = 16, 48
            wq, wkv, wd, wo = aw(0, KC, DIM), aw(512, 16, 2, 16), aw(1024, 512), aw(1536, KC, DIM)
            made = ctx.enter_context(nc.semaphore("l0_masks"))
            cols = ctx.enter_context(nc.semaphore("l0_norm_cols"))
            with nc.Block() as block:
                @block.sync
                def _(sp):
                    k = "l0x"
                    load(sp, k, wq, io["L0_xattn_Wq"].rearrange("(k p) n -> p k n", p=P))
                    load(sp, k, attn_w[:, 512:768], io["L0_xattn_Wk"])
                    load(sp, k, attn_w[:, 768:1024], io["L0_xattn_Wv"])
                    load(sp, k, wd, io["L0_xattn_Wkv_dca"])
                    load(sp, k, wo, io["L0_xattn_Wo"].rearrange("(k p) n -> p k n", p=P))
                    load(sp, k, row_bias[:, :], io["L0_xattn_bq"].unsqueeze(0))
                    load(sp, k, out_bias[:, :], io["L0_xattn_bo"].unsqueeze(0))
                    for half, name in enumerate(("L0_xattn_bk", "L0_xattn_bv")):
                        src = io[name].rearrange("(h t d) -> t h d", t=2, d=hd)
                        for t in range(2):
                            load(sp, k, kv_bias[0:1, t, half * P:(half + 1) * P].rearrange("p (h d) -> p h d", d=hd),
                                 src[t:t + 1])
                    load(sp, k, kv_bias[1:2, :, :], io["L0_xattn_bkv_dca"].rearrange("(a t n) -> a t n", a=1, t=2))
                    for n, name in enumerate(("qn_w", "qn_b", "kn_w", "kn_b", "kn_dca_w", "kn_dca_b")):
                        load(sp, k, norm_rows[n:n + 1, :].rearrange("p (h d) -> p h d", d=hd),
                             io["L0_xattn_" + name].rearrange("(a b d) -> a b d", a=1, b=1).broadcast_to([1, P // hd, hd]))

                @block.gpsimd
                def _(pool):
                    step = in_turn(pool, made)
                    make_masks(pool, step, hd)
                    step(pool.memset(o_all[:, 1536:2304], 0.0))
                    step(pool.memset(key_side[:, :, :], 1.0))
                    step(pool.affine_select(out=key_side[:, :, :], in_=key_side[:, :, :], compare_op=ALU.is_ge, fill=0.0,
                                            base=main - 1, pattern=[[0, 2], [-1, SEQ]], channel_multiplier=SEQ))
                    step(pool.affine_select(out=key_side[:, :, :], in_=key_side[:, :, :], compare_op=ALU.is_ge, fill=0.0,
                                            base=SEQ - main, pattern=[[0, 2], [1, SEQ]], channel_multiplier=-SEQ))

                @block.tensor
                def _(pe):
                    pe.wait_ge(weights_in["l0x"], w_count["l0x"])
                    pe.transpose(bank_t[0][:, 0:6], norm_rows[:, :], ident[0:6, 0:6]).then_inc(cols, 1)

                @block.vector
                def _(dve):
                    dve.wait_ge(cols, 1)
                    dve.tensor_copy(norm_cols[:, :], bank_t[0][:, 0:6]).then_inc(cols, 1)
                    dve.wait_ge(cols, 2)
                    dve.tensor_scalar(norm_cols[:, 0:6:2], norm_cols[:, 0:6:2], float(hd) ** 0.5, None, ALU.mult)\
                        .then_inc(cols, 1)
            narrow_attention(0, "l0x", hd, wq, wo, [wkv[:, :, 0, :], wd[:, 0:DIM]], [wkv[:, :, 1, :], wd[:, DIM:2 * DIM]],
                             main)

        def run_l2x():
            hd = 8
            wq, wkv, wo = aw(0, KC, DIM), aw(512, 512), aw(1024, KC, DIM)
            made = ctx.enter_context(nc.semaphore("l2_masks"))
            r = ctx.enter_context(nc.semaphore("rope_steps"))
            sines = ctx.enter_context(nc.semaphore("rope_sines"))
            pi = PI
            with nc.Block() as block:
                @block.sync
                def _(sp):
                    k = "l2x"
                    load(sp, k, wq, io["L2_xattn_Wq"].rearrange("(k p) n -> p k n", p=P))
                    load(sp, k, wkv, io["L2_xattn_Wkv"])
                    load(sp, k, wo, io["L2_xattn_Wout"].rearrange("(k p) n -> p k n", p=P))
                    load(sp, k, out_bias[:, :], io["L2_xattn_bout"].unsqueeze(0))
                    load(sp, k, pos[:, :, :], io["fside_BxSx2_0"].rearrange("b s a -> (b s) a")
                         .rearrange("(n p) a -> p n a", p=P))

                @block.gpsimd
                def _(pool):
                    make_masks(pool, in_turn(pool, made), hd)

                @block.vector
                def _(dve):
                    ang, tmp, sin_in, cos_in = (ropes_w[:, n, :] for n in range(4))
                    step = in_turn(dve, r)

                    def wrapped(ap):
                        step(dve.tensor_scalar(tmp, ap, pi, -2 * pi, ALU.is_gt, ALU.mult))
                        step(dve.tensor_tensor(ap, ap, tmp, ALU.add))
                        step(dve.tensor_scalar(tmp, ap, -pi, 2 * pi, ALU.is_lt, ALU.mult))
                        step(dve.tensor_tensor(ap, ap, tmp, ALU.add))
                        step(dve.tensor_scalar(ap, ap, 3.1415925, -3.1415925, ALU.min, ALU.max))

                    dve.wait_ge(weights_in["l2x"], w_count["l2x"])
                    a4 = ang.rearrange("p (n a f) -> p n a f", a=2, f=2)
                    for f, freq in enumerate((1.0, 10000.0 ** -0.5)):
                        step(dve.tensor_scalar(a4[:, :, :, f], pos[:, :, :], freq, None, ALU.mult))
                    step(dve.tensor_scalar(tmp, ang, 1.0 / (2 * pi), None, ALU.mult))
                    step(dve.tensor_copy(ropes_i[:, :], tmp))
                    step(dve.tensor_copy(tmp, ropes_i[:, :]))
                    step(dve.scalar_tensor_tensor(ang, tmp, -6.28125, ang, ALU.mult, ALU.add))
                    step(dve.scalar_tensor_tensor(sin_in, tmp, -(2 * pi - 6.28125), ang, ALU.mult, ALU.add))
                    step(dve.tensor_scalar(cos_in, sin_in, pi / 2, None, ALU.add))
                    wrapped(sin_in)
                    wrapped(cos_in)
                    dve.wait_ge(sines, 2)
                    c4 = cos_in.rearrange("p (n r) -> p n r", r=4)
                    s4 = sin_in.rearrange("p (n r) -> p n r", r=4)
                    pair = ropes[:, :, 0:8].rearrange("p n (r two) -> p n r two", two=2)
                    step(dve.tensor_copy(pair[:, :, :, 0], c4))
                    step(dve.tensor_copy(pair[:, :, :, 1], c4))
                    step(dve.tensor_scalar(ropes[:, :, 8:12], s4, -1.0, None, ALU.mult))
                    step(dve.tensor_copy(ropes[:, :, 12:16], s4))

                @block.scalar
                def _(act):
                    act.wait_ge(r, 18)
                    act.activation(ropes_w[:, 2, :], ropes_w[:, 2, :], ACT.Sin).then_inc(sines, 1)
                    act.activation(ropes_w[:, 3, :], ropes_w[:, 3, :], ACT.Sin).then_inc(sines, 1)
            narrow_attention(2, "l2x", hd, wq, wo, [wkv[:, 0:DIM]], [wkv[:, DIM:2 * DIM]], SEQ)

        def run_l3f():
            key, hid = "l3f", 16
            w_in = fw(0, KC, EXPERTS + P)
            up_T = fw(512, DIM)
            raw_down, raw_router = fw(1024, DIM), ffn_w[0:EXPERTS, 1536:1536 + DIM]
            raw_up = fw(2048, KC, EXPERTS, hid)
            wt = ctx.enter_context(nc.semaphore("l3f_turned"))
            wk_ = ctx.enter_context(nc.semaphore("l3f_kept"))
            with nc.Block() as block:
                @block.sync
                def _(sp):
                    load(sp, key, raw_down, io["L3_ffn_down_w"].rearrange("e i h -> (e i) h"))
                    load(sp, key, raw_router, io["L3_ffn_router_w"])
                    for c in range(KC):
                        load(sp, key, raw_up[:, c, :, :],
                             io["L3_ffn_up_w"][:, c * P:(c + 1) * P, :].rearrange("e p i -> p e i"))

                @block.tensor
                def _(pe):
                    pe.wait_ge(weights_in[key], w_count[key])
                    for c in range(KC):
                        pe.transpose(bank_t[0][:, c * P:(c + 1) * P], raw_down[:, c * P:(c + 1) * P], ident[:, :])
                    for c in range(KC):
                        mm = pe.transpose(bank_t[0][:, DIM + c * P:DIM + (c + 1) * P],
                                          raw_up[:, c, :, :].rearrange("p e i -> p (e i)"), ident[:, :])
                    for c in range(KC):
                        mm = pe.transpose(bank_t[1][:, c * EXPERTS:(c + 1) * EXPERTS],
                                          raw_router[:, c * P:(c + 1) * P], ident[0:EXPERTS, 0:EXPERTS])
                    mm.then_inc(wt, 1)

                @block.vector
                def _(dve):
                    dve.wait_ge(wt, 1)
                    dve.tensor_copy(w_in[:, :, EXPERTS:EXPERTS + P],
                                    bank_t[0][:, 0:DIM].rearrange("p (k n) -> p k n", k=KC)).then_inc(wk_, 1)
                    dve.tensor_copy(w_in[:, :, 0:EXPERTS],
                                    bank_t[1][:, 0:KC * EXPERTS].rearrange("p (k n) -> p k n", k=KC)).then_inc(wk_, 1)
                    dve.tensor_copy(up_T, bank_t[0][:, DIM:2 * DIM]).then_inc(wk_, 1)

            s = ln_signals()
            S = counted
            proj = S("projected", 1)
            th_s = S("tanh_ready", 1)
            hid_s = S("hidden_half", 1)
            lg_in = S("logits_copied", 1)
            g_steps = S("gate_steps", 8)
            ex_s = S("exp_ready", 1)
            act_in = S("hidden_ready", 1)
            turned = S("hidden_turned", 1)
            hTr = S("hiddenT_ready", 1)
            down = S("down_ready", 1)
            added = S("expert_added", 1)
            gated = S("gates_ready", 1)
            es, er, nm = lead_t, g_first, g_second

            with nc.Block() as block:
                @block.tensor
                def _(pe):
                    def tile(i):
                        pe_turn_x(pe, s, i, bank_t[0])
                        pe.wait_ge(sem(s["xT"]), at(s["xT"], i, 1))
                        if not first(i):
                            pe.wait_ge(sem(act_in), at(act_in, i, 0))
                        for k in range(KC):
                            mm = pe.matmul(bank_p[0][:, 0:EXPERTS + P], xcT[:, k, :], w_in[:, k, :], start=(k == 0),
                                           stop=(k == KC - 1))
                        mm.then_inc(sem(proj), 1)
                        pe.wait_ge(sem(act_in), at(act_in, i, 1))
                        pe.transpose(bank_t[1][:, 0:P], hh[:, 0, 0:P], ident[:, :]).then_inc(sem(turned), 1)
                        pe.wait_ge(sem(hTr), at(hTr, i, 1))
                        if not first(i):
                            pe.wait_ge(sem(added), at(added, i, 0))
                        pe.matmul(bank_y[:, 0:DIM], hT[:, 0, 0, :], up_T, start=True, stop=True).then_inc(sem(down), 1)
                    over_tiles(pe, tile)

                @block.scalar
                def _(act):
                    def tile(i):
                        act.wait_ge(sem(s["turned"]), at(s["turned"], i, 1))
                        if not first(i):
                            act.wait_ge(sem(proj), at(proj, i, 0))
                        act.activation(xcT[:, 0:KC, :], bank_t[0][:, 0:KC * P].rearrange("p (a b) -> p a b", b=P),
                                       ACT.Copy).then_inc(sem(s["xT"]), 1)
                        act.wait_ge(sem(proj), at(proj, i, 1))
                        act.activation(th[:, 0, 0:P], bank_p[0][:, EXPERTS:EXPERTS + P], ACT.Tanh, scale=0.5)\
                            .then_inc(sem(th_s), 1)
                        act.wait_ge(sem(g_steps), at(g_steps, i, 2))
                        act.activation(pick[:, 0, :], lg[:, :], ACT.Exp, bias=nm[:, 0:1], accum_out=es[:, :])\
                            .then_inc(sem(ex_s), 1)
                        act.wait_ge(sem(turned), at(turned, i, 1))
                        act.activation(hT[:, 0, 0, :], bank_t[1][:, 0:P], ACT.Copy).then_inc(sem(hTr), 1)
                    over_tiles(act, tile)

                @block.gpsimd
                def _(pool):
                    over_tiles(pool, lambda i: pool_rstd(pool, s, i))

                @block.vector
                def _(dve):
                    def tile(i):
                        if not is_last(i):
                            dve_layernorm(dve, s, i + 1, None)
                        dve.wait_ge(sem(th_s), at(th_s, i, 1))
                        if not first(i):
                            dve.wait_ge(sem(turned), at(turned, i, 0))
                        dve.scalar_tensor_tensor(hh[:, 0, 0:P], th[:, 0, 0:P], 1.0, bank_p[0][:, EXPERTS:EXPERTS + P],
                                                 ALU.add, ALU.mult).then_inc(sem(hid_s), 1)
                        dve.tensor_copy(lg[:, :], bank_p[0][:, 0:EXPERTS]).then_inc(sem(lg_in), 1)
                        wait_apart(dve, sem(lg_in), at(lg_in, i, 1))
                        dve.max(top[:, :], lg[:, :]).then_inc(sem(g_steps), 1)
                        dve.wait_ge(sem(g_steps), at(g_steps, i, 1))
                        dve.tensor_scalar(nm[:, :], top[:, 0:1], -1.0, None, ALU.mult).then_inc(sem(g_steps), 1)
                        dve.max_index(top_i[:, :], top[:, :], lg[:, :]).then_inc(sem(g_steps), 1)
                        dve.wait_ge(sem(g_steps), at(g_steps, i, 3))
                        dve.tensor_copy(top_f[:, :], top_i[:, 0:2]).then_inc(sem(g_steps), 1)
                        dve.wait_ge(sem(ex_s), at(ex_s, i, 1))
                        dve.reciprocal(er[:, :], es[:, :]).then_inc(sem(g_steps), 1)
                        dve.wait_ge(sem(g_steps), at(g_steps, i, 5))
                        dve.tensor_scalar(er[:, :], er[:, :], half_g[:, 3:4], None, ALU.mult).then_inc(sem(g_steps), 1)
                        dve.tensor_scalar(gate[:, :], iota8[:, :], top_f[:, 0:1], None, ALU.is_equal).then_inc(sem(g_steps), 1)
                        dve.wait_ge(sem(g_steps), at(g_steps, i, 7))
                        dve.scalar_tensor_tensor(gate[:, :], iota8[:, :], top_f[:, 1:2], gate[:, :], ALU.is_equal,
                                                 ALU.add).then_inc(sem(g_steps), 1)
                        dve.wait_ge(sem(g_steps), at(g_steps, i, 8))
                        dve.scalar_tensor_tensor(gate[:, :], gate[:, :], er[:, 0:1], pick[:, 0, :], ALU.mult, ALU.mult)\
                            .then_inc(sem(gated), 1)
                        dve.wait_ge(sem(gated), at(gated, i, 1))
                        dve.tensor_tensor(hh[:, 0, 0:P].rearrange("p (e i) -> p e i", e=EXPERTS),
                                          hh[:, 0, 0:P].rearrange("p (e i) -> p e i", e=EXPERTS),
                                          gate[:, :].unsqueeze(2).broadcast_to([P, EXPERTS, hid]), ALU.mult)\
                            .then_inc(sem(act_in), 1)
                        dve.wait_ge(sem(down), at(down, i, 1))
                        dve.tensor_tensor(x[:, i, :], bank_y[:, 0:DIM], x[:, i, :], ALU.add).then_inc(sem(added), 1)

                    dve_layernorm(dve, s, 0, None)
                    over_tiles(dve, tile)
            block_ends()

        def moe_loads(sp, layer, key, gate_w, up_w, down_w, router_w, hid):
            fk = hid // 2 if hid > P else hid
            fc = hid // fk
            wgu = ffn_w[:, 0:KC * EXPERTS * 2 * hid].rearrange("p (k e g f) -> p k e g f", k=KC, e=EXPERTS, g=2)
            wd = ffn_w[0:fk, KC * EXPERTS * 2 * hid:KC * EXPERTS * 2 * hid + fc * EXPERTS * DIM]\
                .rearrange("p (c e d) -> p c e d", c=fc, e=EXPERTS)
            load(sp, key, router[:, layer, :, :], router_w.rearrange("(k p) e -> p k e", p=P))
            for k in range(KC):
                load(sp, key, wgu[:, k, :, 0, :], gate_w[:, k * P:(k + 1) * P, :].rearrange("e p f -> p e f"))
                load(sp, key, wgu[:, k, :, 1, :], up_w[:, k * P:(k + 1) * P, :].rearrange("e p f -> p e f"))
            for c in range(fc):
                load(sp, key, wd[:, c, :, :], down_w[:, c * fk:(c + 1) * fk, :].rearrange("e p d -> p e d"))

        MOE = {
            "l0f": (0, 128, "L0_ffn_wi_0", "L0_ffn_wi_1", "L0_ffn_wo", "L0_ffn_w_gate"),
            "l1f": (1, 176, "L1_ffn_Wg", "L1_ffn_Wu", "L1_ffn_Wd", "L1_ffn_Wr"),
            "l2f": (2, 256, "L2_ffn_Wg", "L2_ffn_Wu", "L2_ffn_Wd", "L2_ffn_Wr"),
        }

        def run_moe(key):
            layer, hid, g, u, d, r = MOE[key]
            with nc.Block() as block:
                @block.sync
                def _(sp):
                    moe_loads(sp, layer, key, io[g], io[u], io[d], io[r], hid)
            moe_part(layer, key, hid, lambda: w_count[key])

        run = {"l0x": run_l0x, "l1x": run_l1x, "l2x": run_l2x, "l3x": run_l3x, "l3f": run_l3f}
        for key in parts:
            run[key]() if key in run else run_moe(key)

        with nc.Block() as block:
            @block.sync
            def _(sp):
                sp.dma_start(out.rearrange("b s d -> (b s) d").rearrange("(n p) d -> p n d", p=P), x[:, :, :])\
                    .then_inc(out_stored, 16)
                sp.wait_ge(out_stored, 16)


PARTS = ("l0x", "l0f", "l1x", "l1f", "l2x", "l2f", "l3x", "l3f")


def kernel(**inputs):
    import numpy as np
    from concourse import bacc
    from concourse.bass_utils import run_bass_kernel_spmd

    nc = bacc.Bacc("TRN2", target_bir_lowering=False, num_devices=1)
    arrays, io = {}, {}
    for name, value in inputs.items():
        a = np.ascontiguousarray(value)
        if a.dtype == np.bool_:
            a = a.view(np.uint8)
        arrays[f"in_{name}_dram"] = a
        io[name] = nc.dram_tensor(f"in_{name}_dram", a.shape, mybir.dt.from_np(a.dtype), kind="ExternalInput").ap()
    out = nc.dram_tensor("out_0_dram", (BATCH, SEQ, DIM), F32, kind="ExternalOutput").ap()
    flamingo_kernel(nc, io, out, PARTS)
    r = run_bass_kernel_spmd(nc, [arrays], core_ids=[0])
    return r.results[0]["out_0_dram"]
```

```python
from contextlib import ExitStack

import concourse.bass as bass
from concourse import mybir

F32 = mybir.dt.float32
U32 = mybir.dt.uint32
I32 = mybir.dt.int32
U8 = mybir.dt.uint8
ALU = mybir.AluOpType
ACT = mybir.ActivationFunctionType
AX = mybir.AxisListType.X

P = 128
PI = 3.141592653589793
BATCH, SEQ, DIM, CTX = 32, 64, 256, 128
TILES = BATCH * SEQ // P
KC = DIM // P
EXPERTS = 8
LN_EPS = 1e-5
CHUNK_HEADS = 8


def sem(signal):
    return signal[0]


def per(signal):
    return signal[1]


def at(signal, tile, n):
    return tile * signal[1] + (signal[2] + n)


def over_tiles(eng, body, tail=1):
    body(0)
    with eng.Fori(1, TILES - tail) as i:
        body(i)
    for i in range(TILES - tail, TILES):
        body(i)


def first(i):
    return isinstance(i, int) and i == 0


def within(i, n):
    return isinstance(i, int) and i >= TILES - n


def is_last(i):
    return isinstance(i, int) and i == TILES - 1


def flamingo_kernel(nc, io, out, parts):
    ctx = ExitStack()
    with ctx:
        signals, in_use = {}, []

        def sb(name, shape, dt=F32):
            return ctx.enter_context(nc.sbuf_tensor(name, shape, dt))

        def ps(name):
            return ctx.enter_context(nc.psum_tensor(name, [P, 512], F32))

        def counted(name, n):
            if name not in signals:
                signals[name] = [ctx.enter_context(nc.semaphore(name)), 0, 0]
            signals[name][1] = n
            in_use.append(signals[name])
            return signals[name]

        def block_ends():
            for one in in_use:
                one[2] += TILES * one[1]
            del in_use[:]

        x = sb("x", [P, TILES, DIM])
        attn_w = sb("attn_w", [P, 18432])
        ffn_w = sb("ffn_w", [P, 12288])
        ident = sb("ident", [P, P])
        ones = sb("ones", [P, P])
        gates_raw = sb("gates_raw", [P, 8])
        tanh_g = sb("tanh_g", [P, 8])
        half_g = sb("half_g", [P, 4])
        quarter_g = sb("quarter_g", [P, 4])
        minus_half = sb("minus_half", [P, 32])
        ln_eps = sb("ln_eps", [P, 1])
        rms_eps = sb("rms_eps", [P, 4])
        head_eps = sb("head_eps", [P, 32])
        iota8 = sb("iota8", [P, EXPERTS])
        small = {
            "st": sb("st", [P, 6]), "mv": sb("mv", [P, 2]), "rstd": sb("rstd", [P, 1]),
            "var": sb("var", [P, 1]),
        }
        xn = sb("xn", [P, DIM])
        xcT = sb("xcT", [P, 3, P])
        c_tok = sb("c_tok", [P, CTX])
        c_even = sb("c_even", [P, 2, CTX])
        c_odd = sb("c_odd", [P, 2, CTX])
        bank_t = [ps("bank_t0"), ps("bank_t1")]
        bank_p = [ps("bank_p0"), ps("bank_p1")]
        bank_s = [ps("bank_s0"), ps("bank_s1")]
        bank_o = ps("bank_o")
        bank_y = ps("bank_y")

        weights_in = {n: ctx.enter_context(nc.semaphore(f"w_{n}")) for n in
                      ("first", "l0x", "l0f", "l1x", "l1f", "l2x", "l2f", "l3x", "l3f")}
        w_count = {n: 0 for n in weights_in}
        setup = ctx.enter_context(nc.semaphore("setup"))
        gates_tanh = ctx.enter_context(nc.semaphore("gates_tanh"))
        stood_apart = ctx.enter_context(nc.semaphore("stood_apart"))
        gates_scaled = ctx.enter_context(nc.semaphore("gates_scaled"))
        out_stored = ctx.enter_context(nc.semaphore("out_stored"))

        def load(sp, key, dst, src):
            sp.dma_start(dst, src).then_inc(weights_in[key], 16)
            w_count[key] += 16

        ctx_rows = io["ctx_1024"].rearrange("b s c -> (b s) c").rearrange("(n p) c -> n p c", p=P)
        ctx_by_row = io["ctx_1024"].rearrange("(n b) s c -> n s b c", b=2)

        def aw(off, *shape):
            n = 1
            for s in shape:
                n *= s
            ap = attn_w[:, off:off + n]
            if len(shape) == 2:
                return ap.rearrange("p (a b) -> p a b", a=shape[0])
            if len(shape) == 3:
                return ap.rearrange("p (a b c) -> p a b c", a=shape[0], b=shape[1])
            return ap

        def fw(off, *shape):
            n = 1
            for s in shape:
                n *= s
            ap = ffn_w[:, off:off + n]
            if len(shape) == 2:
                return ap.rearrange("p (a b) -> p a b", a=shape[0])
            if len(shape) == 3:
                return ap.rearrange("p (a b c) -> p a b c", a=shape[0], b=shape[1])
            return ap

        def wait_apart(eng, sem, value):
            eng.wait_ge(sem, value)
            eng.sem_inc(stood_apart, 1)

        def ln_signals():
            S = counted
            return dict(stats=S("ln_stats", 1), var=S("ln_var", 1), aggr=S("ln_aggr", 1), rstd=S("ln_rstd", 1), xn=S("xn_ready", 1),
                        turned=S("x_turned", 1), xT=S("xT_ready", 1))

        def ln_stats(dve, s, i):
            if not first(i):
                dve.wait_ge(sem(s["xn"]), at(s["xn"], i, 0))
            dve.bn_stats(small["st"][:, :], x[:, i, :]).then_inc(sem(s["stats"]), 1)
            wait_apart(dve, sem(s["stats"]), at(s["stats"], i, 1))
            dve.bn_aggr(small["mv"][:, :], small["st"][:, :]).then_inc(sem(s["aggr"]), 1)

        def ln_apply(dve, s, i):
            dve.wait_ge(sem(s["rstd"]), at(s["rstd"], i, 1))
            if not first(i):
                dve.wait_ge(sem(s["turned"]), at(s["turned"], i, 0))
            dve.tensor_scalar(xn[:, :], x[:, i, :], small["mv"][:, 0:1], small["rstd"][:, 0:1],
                              ALU.subtract, ALU.mult).then_inc(sem(s["xn"]), 1)

        def dve_layernorm(dve, s, i):
            ln_stats(dve, s, i)
            ln_apply(dve, s, i)

        def pool_rstd(pool, s, i):
            pool.wait_ge(sem(s["aggr"]), at(s["aggr"], i, 1))
            if not first(i):
                pool.wait_ge(sem(s["xn"]), at(s["xn"], i, 0))
            pool.tensor_tensor(small["var"][:, :], small["mv"][:, 1:2], ln_eps[:, :], ALU.add)\
                .then_inc(sem(s["var"]), 1)
            pool.wait_ge(sem(s["var"]), at(s["var"], i, 1))
            pool.tensor_tensor(small["rstd"][:, :], small["var"][:, :], minus_half[:, 0:1], ALU.pow)\
                .then_inc(sem(s["rstd"]), 1)

        def pe_turn_x(pe, s, i, bank, c_in=None, bank_free=None):
            pe.wait_ge(sem(s["xn"]), at(s["xn"], i, 1))
            if bank_free is not None:
                bank_free()
            for k in range(KC):
                mm = pe.transpose(bank[:, k * P:(k + 1) * P], xn[:, k * P:(k + 1) * P], ident[:, :])
            if c_in is not None:
                c_in()
                mm = pe.transpose(bank[:, 2 * P:3 * P], c_tok[:, :], ident[:, :])
            mm.then_inc(sem(s["turned"]), 1)

        with nc.Block() as block:
            @block.sync
            def _(sp):
                sp.dma_start(x[:, :, :], io["x"].rearrange("b s d -> (b s) d").rearrange("(n p) d -> p n d", p=P))\
                    .then_inc(weights_in["first"], 16)
                sp.dma_start(gates_raw[:, 0:4], io["g_xattn"].rearrange("(a g) -> a g", a=1).broadcast_to([P, 4]))\
                    .then_inc(weights_in["first"], 16)
                sp.dma_start(gates_raw[:, 4:8], io["g_ffn"].rearrange("(a g) -> a g", a=1).broadcast_to([P, 4]))\
                    .then_inc(weights_in["first"], 16)

            @block.gpsimd
            def _(pool):
                pool.memset(ident[:, :], 0.0).then_inc(setup, 1)
                pool.memset(ones[:, :], 1.0).then_inc(setup, 1)
                pool.memset(c_even[:, :, :], 0.0).then_inc(setup, 1)
                pool.memset(c_odd[:, :, :], 0.0).then_inc(setup, 1)
                pool.memset(minus_half[:, :], -0.5).then_inc(setup, 1)
                pool.memset(ln_eps[:, :], LN_EPS).then_inc(setup, 1)
                pool.memset(rms_eps[:, :], P * LN_EPS).then_inc(setup, 1)
                pool.memset(head_eps[:, :], 16 * 1e-6).then_inc(setup, 1)
                pool.iota(iota8[:, :], [[1, EXPERTS]], base=0, channel_multiplier=0,
                          allow_small_or_imprecise_dtypes=True).then_inc(setup, 1)
                pool.wait_ge(setup, 9)
                pool.affine_select(out=ident[:, :], in_=ident[:, :], compare_op=ALU.not_equal, fill=1.0, base=0,
                                   pattern=[[-1, P]], channel_multiplier=1).then_inc(setup, 1)

            @block.scalar
            def _(act):
                act.wait_ge(weights_in["first"], 48)
                act.activation(tanh_g[:, :], gates_raw[:, :], ACT.Tanh).then_inc(gates_tanh, 1)

            @block.vector
            def _(dve):
                dve.wait_ge(gates_tanh, 1)
                dve.tensor_scalar(half_g[:, :], tanh_g[:, 4:8], 0.5, None, ALU.mult).then_inc(gates_scaled, 1)
                dve.tensor_scalar(quarter_g[:, :], tanh_g[:, 4:8], 0.25, None, ALU.mult).then_inc(gates_scaled, 1)

        lg = sb("lg", [P, EXPERTS])
        top = sb("top", [P, 8])
        top_i = sb("top_i", [P, 8], U32)
        top_f = sb("top_f", [P, 2])
        lead = sb("lead", [P, 1])
        lead_t = sb("lead_t", [P, 1])
        g_first = sb("g_first", [P, 1])
        g_second = sb("g_second", [P, 1])
        pick = sb("pick", [P, 2, EXPERTS])
        gate = sb("gate", [P, EXPERTS])
        th = sb("th", [P, 2, 256])
        hh = sb("hh", [P, 2, 256])
        hT = sb("hT", [P, 2, 2, P])

        def moe_part(layer, key, hid, loads):
            fk = hid // 2 if hid > P else hid
            fc = hid // fk
            wgu = fw(0, KC * EXPERTS, 2 * hid)
            wd = fw(KC * EXPERTS * 2 * hid, fc * EXPERTS, DIM)
            wr = router[:, layer, :, :]
            s = ln_signals()
            S = counted
            logits = S("logits_ready", 1)
            lg_in = S("logits_copied", 1)
            g_steps = S("gate_steps", 8)
            gated = S("gates_ready", 1)
            lead_s = S("lead_tanh", 1)
            gu = S("gate_up_ready", EXPERTS)
            tanh = S("tanh_ready", EXPERTS)
            hid1 = S("hidden_half", EXPERTS)
            hid2 = S("hidden_ready", EXPERTS)
            turned = S("hidden_turned", EXPERTS)
            hTr = S("hiddenT_ready", EXPERTS)
            down = S("down_ready", EXPERTS)
            added = S("expert_added", EXPERTS)
            nw = loads()

            with nc.Block() as block:
                @block.tensor
                def _(pe):
                    pe.wait_ge(weights_in[key], nw)

                    def turn_x(i):
                        pe_turn_x(pe, s, i, bank_s[1], bank_free=None if first(i) else
                                  (lambda: pe.wait_ge(sem(s["xT"]), at(s["xT"], i, 0))))

                    def route(i):
                        pe.wait_ge(sem(s["xT"]), at(s["xT"], i, 1))
                        if not first(i):
                            pe.wait_ge(sem(lg_in), at(lg_in, i, 0))
                        for k in range(KC):
                            mm = pe.matmul(bank_s[0][:, 0:EXPERTS], xcT[:, k, :], wr[:, k, :],
                                           start=(k == 0), stop=(k == KC - 1))
                        mm.then_inc(sem(logits), 1)

                    def gate_up(i, e):
                        if not (first(i) and e < 2):
                            pe.wait_ge(sem(hid2), at(hid2, i, e - 1))
                        for k in range(KC):
                            mm = pe.matmul(bank_p[e % 2][:, 0:2 * hid], xcT[:, k, :], wgu[:, k * EXPERTS + e, :],
                                           start=(k == 0), stop=(k == KC - 1))
                        mm.then_inc(sem(gu), 1)

                    def turn_h(i, e):
                        pe.wait_ge(sem(hid2), at(hid2, i, e + 1))
                        if not (first(i) and e < 2):
                            pe.wait_ge(sem(hTr), at(hTr, i, e - 1))
                        for c in range(fc):
                            mm = pe.transpose(bank_t[e % 2][0:fk, c * P:(c + 1) * P],
                                              hh[:, e % 2, c * fk:(c + 1) * fk], ident[:, :])
                        mm.then_inc(sem(turned), 1)

                    def down_e(i, e):
                        pe.wait_ge(sem(hTr), at(hTr, i, e + 1))
                        if not (first(i) and e < 2):
                            pe.wait_ge(sem(added), at(added, i, e - 1))
                        b = (bank_o, bank_y)[e % 2]
                        for c in range(fc):
                            mm = pe.matmul(b[:, 0:DIM], hT[0:fk, e % 2, c, :], wd[0:fk, c * EXPERTS + e, :],
                                           start=(c == 0), stop=(c == fc - 1))
                        mm.then_inc(sem(down), 1)

                    def tile(i):
                        route(i)
                        for e in range(EXPERTS):
                            gate_up(i, e)
                            if e >= 1:
                                turn_h(i, e - 1)
                            elif not first(i):
                                turn_h(i - 1, EXPERTS - 1)
                            if e >= 2:
                                down_e(i, e - 2)
                            elif not first(i):
                                down_e(i - 1, EXPERTS - 2 + e)
                            if e == EXPERTS - 1 and not is_last(i):
                                turn_x(i + 1)

                    turn_x(0)
                    over_tiles(pe, tile)
                    turn_h(TILES - 1, EXPERTS - 1)
                    down_e(TILES - 1, EXPERTS - 2)
                    down_e(TILES - 1, EXPERTS - 1)

                @block.scalar
                def _(act):
                    load_next(act, key)

                    def xT_in(i):
                        act.wait_ge(sem(s["turned"]), at(s["turned"], i, 1))
                        if not first(i):
                            act.wait_ge(sem(gu), at(gu, i, 0))
                        act.activation(xcT[:, 0:KC, :], bank_s[1][:, 0:KC * P].rearrange("p (a b) -> p a b", b=P),
                                       ACT.Copy).then_inc(sem(s["xT"]), 1)

                    def tanh_e(i, e):
                        act.wait_ge(sem(gu), at(gu, i, e + 1))
                        if not (first(i) and e < 2):
                            act.wait_ge(sem(hid1), at(hid1, i, e - 1))
                        act.activation(th[:, e % 2, 0:hid], bank_p[e % 2][:, 0:hid], ACT.Tanh, scale=0.5)\
                            .then_inc(sem(tanh), 1)

                    def hT_in(i, e):
                        act.wait_ge(sem(turned), at(turned, i, e + 1))
                        if not (first(i) and e < 2):
                            act.wait_ge(sem(down), at(down, i, e - 1))
                        act.activation(hT[0:fk, e % 2, 0:fc, :],
                                       bank_t[e % 2][0:fk, 0:fc * P].rearrange("p (a b) -> p a b", b=P),
                                       ACT.Copy).then_inc(sem(hTr), 1)

                    def lead_in(i):
                        act.wait_ge(sem(g_steps), at(g_steps, i, 4))
                        act.activation(lead_t[:, :], lead[:, :], ACT.Tanh, scale=0.5).then_inc(sem(lead_s), 1)

                    def tile(i):
                        for e in range(EXPERTS):
                            tanh_e(i, e)
                            if e == 1:
                                lead_in(i)
                            if e >= 1:
                                hT_in(i, e - 1)
                            elif not first(i):
                                hT_in(i - 1, EXPERTS - 1)
                            if e == EXPERTS - 1 and not is_last(i):
                                xT_in(i + 1)

                    xT_in(0)
                    over_tiles(act, tile)
                    hT_in(TILES - 1, EXPERTS - 1)

                @block.gpsimd
                def _(pool):
                    over_tiles(pool, lambda i: pool_rstd(pool, s, i))

                @block.vector
                def _(dve):
                    def hidden(i, e):
                        dve.wait_ge(sem(tanh), at(tanh, i, e + 1))
                        if not (first(i) and e < 2):
                            dve.wait_ge(sem(turned), at(turned, i, e - 1))
                        if not (first(i) and e == 0):
                            dve.wait_ge(sem(hid2), at(hid2, i, e))
                        g, u = bank_p[e % 2][:, 0:hid], bank_p[e % 2][:, hid:2 * hid]
                        dve.scalar_tensor_tensor(th[:, e % 2, 0:hid], th[:, e % 2, 0:hid], 1.0, g,
                                                 ALU.add, ALU.mult).then_inc(sem(hid1), 1)
                        dve.wait_ge(sem(hid1), at(hid1, i, e + 1))
                        dve.tensor_tensor(hh[:, e % 2, 0:hid], th[:, e % 2, 0:hid], u, ALU.mult)\
                            .then_inc(sem(hid2), 1)

                    def gates(i):
                        dve.wait_ge(sem(logits), at(logits, i, 1))
                        if not first(i):
                            dve.wait_ge(sem(added), at(added, i, 0))
                        dve.tensor_copy(lg[:, :], bank_s[0][:, 0:EXPERTS]).then_inc(sem(lg_in), 1)
                        wait_apart(dve, sem(lg_in), at(lg_in, i, 1))
                        dve.max(top[:, :], lg[:, :]).then_inc(sem(g_steps), 1)
                        wait_apart(dve, sem(g_steps), at(g_steps, i, 1))
                        dve.max_index(top_i[:, :], top[:, :], lg[:, :]).then_inc(sem(g_steps), 1)
                        dve.wait_ge(sem(g_steps), at(g_steps, i, 2))
                        dve.tensor_copy(top_f[:, :], top_i[:, 0:2]).then_inc(sem(g_steps), 1)
                        dve.tensor_tensor(lead[:, :], top[:, 0:1], top[:, 1:2], ALU.subtract).then_inc(sem(g_steps), 1)
                        dve.wait_ge(sem(lead_s), at(lead_s, i, 1))
                        dve.tensor_scalar(g_first[:, :], lead_t[:, :], 1.0, quarter_g[:, layer:layer + 1],
                                          ALU.add, ALU.mult).then_inc(sem(g_steps), 1)
                        dve.wait_ge(sem(g_steps), at(g_steps, i, 5))
                        dve.tensor_scalar(g_second[:, :], g_first[:, :], half_g[:, layer:layer + 1], -1.0,
                                          ALU.subtract, ALU.mult).then_inc(sem(g_steps), 1)
                        dve.wait_ge(sem(g_steps), at(g_steps, i, 6))
                        dve.tensor_scalar(pick[:, 0, :], iota8[:, :], top_f[:, 0:1], g_first[:, 0:1],
                                          ALU.is_equal, ALU.mult).then_inc(sem(g_steps), 1)
                        dve.tensor_scalar(pick[:, 1, :], iota8[:, :], top_f[:, 1:2], g_second[:, 0:1],
                                          ALU.is_equal, ALU.mult).then_inc(sem(g_steps), 1)
                        dve.wait_ge(sem(g_steps), at(g_steps, i, 8))
                        dve.tensor_tensor(gate[:, :], pick[:, 0, :], pick[:, 1, :], ALU.add).then_inc(sem(gated), 1)

                    def add(i, e):
                        dve.wait_ge(sem(down), at(down, i, e + 1))
                        if e == 0:
                            dve.wait_ge(sem(gated), at(gated, i, 1))
                        else:
                            dve.wait_ge(sem(added), at(added, i, e))
                        b = (bank_o, bank_y)[e % 2]
                        dve.scalar_tensor_tensor(x[:, i, :], b[:, 0:DIM], gate[:, e:e + 1], x[:, i, :],
                                                 ALU.mult, ALU.add).then_inc(sem(added), 1)

                    def tile(i):
                        for e in range(EXPERTS):
                            hidden(i, e)
                            if e >= 2:
                                add(i, e - 2)
                            elif not first(i):
                                add(i - 1, EXPERTS - 2 + e)
                            if e == 1:
                                gates(i)
                            if e == 3 and not is_last(i):
                                dve_layernorm(dve, s, i + 1)

                    dve_layernorm(dve, s, 0)
                    over_tiles(dve, tile)
                    add(TILES - 1, EXPERTS - 2)
                    add(TILES - 1, EXPERTS - 1)
            block_ends()

        router = sb("router", [P, 4, KC, EXPERTS])


        stage = sb("stage", [P, 2, 512])
        qn = sb("qn", [P, 2, 512])
        ssq = sb("ssq", [P, 32])
        ssq_e = sb("ssq_e", [P, 32])
        rnorm = sb("rnorm", [P, 32])
        qk_all = sb("qk_all", [P, 4096])
        qT = qk_all[:, 0:2048].rearrange("p (h t) -> p h t", h=16)
        kT = qk_all[:, 2048:4096].rearrange("p (h t) -> p h t", h=16)
        smax = sb("smax", [P, 4, 2, 8])
        E = sb("E", [P, 4, 8, SEQ])
        ssum = sb("ssum", [P, 4, 2, 8])
        srec = sb("srec", [P, 4, 2, 8])
        PT = sb("PT", [P, 4, 4, P])
        o_all = sb("o_all", [P, 2304])
        OT = o_all[:, 0:2048].rearrange("p (h t) -> p h t", h=16)
        gcol = sb("gcol", [P, 3])

        def load_context(sp, i, s, turned):
            if not first(i):
                sp.wait_ge(sem(turned), at(turned, i, 0))
            sp.dma_start(c_tok[:, :], ctx_rows[i]).then_inc(sem(s["c"]), 16)

        def load_context_rows(sp, i, s, rows_used):
            if not first(i):
                sp.wait_ge(sem(rows_used), at(rows_used, i, 0))
            sp.dma_start(c_even[0:SEQ, :, :], ctx_by_row[i]).then_inc(sem(s["ce"]), 16)
            sp.dma_start(c_odd[SEQ:P, :, :], ctx_by_row[i]).then_inc(sem(s["co"]), 16)

        def load_contexts(sp, s, rows_used):
            def tile(i):
                if not is_last(i):
                    load_context(sp, i + 1, s, s["turned"])
                load_context_rows(sp, i, s, rows_used)
            load_context(sp, 0, s, s["turned"])
            over_tiles(sp, tile)

        def absorb_part(key, pairs, wq, wk, wv, wo, m_out, w2_out):
            S = counted
            jobs = 1 if wq is None else 2
            turned, copied, mul, kept = (S(n, jobs) for n in ("w_turned", "w_copied", "w_multiplied", "w_kept"))
            banks_w = (bank_t[0], bank_s[0])
            banks_wq = (bank_t[1], bank_s[1])
            banks_w2 = (bank_p[0], bank_o)
            banks_m = (bank_p[1], bank_y)
            wT, wqT = qn, stage

            with nc.Block() as block:
                @block.tensor
                def _(pe):
                    def turn(j):
                        if j >= 2:
                            pe.wait_ge(sem(copied), at(copied, j - 1, 0))
                        shared = wq is not None
                        for a, (w, h) in enumerate(((wk, j), (wv, j)) if shared else ((wv, 2 * j), (wv, 2 * j + 1))):
                            mm = pe.transpose(banks_w[j % 2][:, a * P:(a + 1) * P], w[:, h * P:(h + 1) * P], ident[:, :])
                        mm.then_inc(sem(turned), 1)
                        if shared:
                            for a in range(2):
                                for k in range(KC):
                                    h = 2 * j + a
                                    mm = pe.transpose(banks_wq[j % 2][:, (a * KC + k) * P:(a * KC + k + 1) * P],
                                                      wq[:, k, h * P:(h + 1) * P], ident[:, :])
                            mm.then_inc(sem(turned), 1)

                    def multiply(j):
                        pe.wait_ge(sem(copied), at(copied, j, jobs))
                        if j >= 2:
                            pe.wait_ge(sem(kept), at(kept, j - 1, 0))
                        for a in range(2):
                            v = 1 if wq is not None else a
                            mm = pe.matmul(banks_w2[j % 2][:, a * DIM:(a + 1) * DIM], wT[:, j % 2, v * P:(v + 1) * P],
                                           wo[:, 2 * j + a, :], start=True, stop=True)
                        mm.then_inc(sem(mul), 1)
                        if wq is not None:
                            for n in range(2 * KC):
                                mm = pe.matmul(banks_m[j % 2][:, n * P:(n + 1) * P], wqT[:, j % 2, n * P:(n + 1) * P],
                                               wT[:, j % 2, 0:P], start=True, stop=True)
                            mm.then_inc(sem(mul), 1)

                    pe.wait_ge(weights_in[key], w_count[key])
                    turn(0)
                    for j in range(pairs):
                        if j + 1 < pairs:
                            turn(j + 1)
                        multiply(j)

                @block.scalar
                def _(act):
                    for j in range(pairs):
                        act.wait_ge(sem(turned), at(turned, j, 1))
                        if j >= 2:
                            act.wait_ge(sem(mul), at(mul, j - 1, 0))
                        act.activation(wT[:, j % 2, 0:2 * P], banks_w[j % 2][:, 0:2 * P], ACT.Copy)\
                            .then_inc(sem(copied), 1)
                        if wq is not None:
                            act.wait_ge(sem(turned), at(turned, j, 2))
                            act.activation(wqT[:, j % 2, :], banks_wq[j % 2][:, :], ACT.Copy).then_inc(sem(copied), 1)

                @block.vector
                def _(dve):
                    for j in range(pairs):
                        dve.wait_ge(sem(mul), at(mul, j, 1))
                        dve.tensor_copy(w2_out[:, 2 * j:2 * j + 2, :],
                                        banks_w2[j % 2][:, :].rearrange("p (a d) -> p a d", a=2)).then_inc(sem(kept), 1)
                        if wq is not None:
                            dve.wait_ge(sem(mul), at(mul, j, 2))
                            dve.tensor_copy(m_out[:, :, 2 * j:2 * j + 2, :].rearrange("p k a c -> p a k c"),
                                            banks_m[j % 2][:, :].rearrange("p (a k c) -> p a k c", a=2, k=KC))\
                                .then_inc(sem(kept), 1)
            for one in in_use:
                one[2] += pairs * one[1]
            del in_use[:]

        def normed_attention(layer, key, wq, wk, w2, score_scale):
            jobs = 8
            s = ln_signals()
            S = counted
            s["c"], s["ce"], s["co"] = S("c_loaded", 16), S("c_even_loaded", 16), S("c_odd_loaded", 16)
            proj, sq, sqs, sqe, rn, normed, qk_turned, qkT = (S(n, jobs) for n in (
                "projected", "squared", "squares_summed", "norm_eps", "norm_ready", "qk_normed", "qk_turned", "qkT_ready"))
            scores, smx, sub, ex, sm, rec, probs, p_turned, pT = (S(n, 2) for n in (
                "scores_ready", "score_max", "scores_shifted", "exp_ready", "exp_sum", "sum_inverse", "probs_ready",
                "probs_turned", "probsT_ready"))
            pv, oT = S("pv_ready", 4), S("pvT_copied", 4)
            y, added = S("y_ready", 1), S("y_added", 1)
            banks_o = [bank_o, bank_s[0], bank_o, bank_s[1]]

            with nc.Block() as block:
                @block.sync
                def _(sp):
                    load_contexts(sp, s, pv)

                @block.tensor
                def _(pe):
                    def turn_x(i):
                        pe_turn_x(pe, s, i, bank_t[0], c_in=lambda: pe.wait_ge(sem(s["c"]), at(s["c"], i, 16)),
                                  bank_free=None if first(i) else
                                  (lambda: pe.wait_ge(sem(qkT), at(qkT, i, -1))))

                    def project(i, j):
                        if j == 0:
                            pe.wait_ge(sem(s["xT"]), at(s["xT"], i, 1))
                        cols = slice(j // 2 * 512, (j // 2 + 1) * 512)
                        if j % 2 == 0:
                            for k in range(KC):
                                mm = pe.matmul(bank_p[0][:, :], xcT[:, k, :], wq[:, k, cols], start=(k == 0),
                                               stop=(k == KC - 1))
                        else:
                            mm = pe.matmul(bank_p[1][:, :], xcT[:, 2, :], wk[:, cols], start=True, stop=True)
                        mm.then_inc(sem(proj), 1)

                    def turn(i, j):
                        pe.wait_ge(sem(normed), at(normed, i, j + 1))
                        if j >= 2:
                            pe.wait_ge(sem(qkT), at(qkT, i, j - 1))
                        for h in range(4):
                            mm = pe.transpose(bank_t[j % 2][:, h * P:(h + 1) * P], qn[:, j % 2, h * P:(h + 1) * P],
                                              ident[:, :])
                        mm.then_inc(sem(qk_turned), 1)

                    def score(i, g):
                        pe.wait_ge(sem(qkT), at(qkT, i, 4 * g + 4))
                        for h in range(8):
                            for b in range(2):
                                rows = slice(b * SEQ, (b + 1) * SEQ)
                                mm = pe.matmul(bank_s[g][rows, h * SEQ:(h + 1) * SEQ], qT[:, 8 * g + h, rows],
                                               kT[:, 8 * g + h, rows], start=True, stop=True)
                        mm.then_inc(sem(scores), 1)

                    def turn_probs(i, g):
                        pe.wait_ge(sem(probs), at(probs, i, g + 1))
                        for a in range(4):
                            mm = pe.transpose(bank_s[g][:, a * P:(a + 1) * P],
                                              E[:, g, 2 * a:2 * a + 2, :].rearrange("p a b -> p (a b)"), ident[:, :])
                        mm.then_inc(sem(p_turned), 1)

                    def values(i, g, b):
                        if b == 0:
                            pe.wait_ge(sem(pT), at(pT, i, g + 1))
                        if g == 0 and b == 0:
                            pe.wait_ge(sem(s["ce"]), at(s["ce"], i, 16))
                            pe.wait_ge(sem(s["co"]), at(s["co"], i, 16))
                        for a, c in enumerate((c_even, c_odd)):
                            mm = pe.matmul(banks_o[2 * g + b][:, a * 256:(a + 1) * 256], c[:, b, :],
                                           PT[:, g, :, b * SEQ:(b + 1) * SEQ], start=True, stop=True)
                        mm.then_inc(sem(pv), 1)

                    def sum_heads(i, q):
                        if q == 0 and not first(i):
                            pe.wait_ge(sem(added), at(added, i, 0))
                        if q % 2 == 0:
                            pe.wait_ge(sem(oT), at(oT, i, q + 2))
                        for h in range(4 * q, 4 * q + 4):
                            mm = pe.matmul(bank_y[:, 0:DIM], OT[:, h, :], w2[:, h, :], start=(h == 0), stop=(h == 15))
                        if q == 3:
                            mm.then_inc(sem(y), 1)

                    def tile(i):
                        project(i, 0)
                        project(i, 1)
                        if not first(i):
                            sum_heads(i - 1, 0)
                            sum_heads(i - 1, 1)
                        turn(i, 0)
                        project(i, 2)
                        turn(i, 1)
                        project(i, 3)
                        turn(i, 2)
                        project(i, 4)
                        if not first(i):
                            turn_probs(i - 1, 1)
                        turn(i, 3)
                        project(i, 5)
                        if not first(i):
                            values(i - 1, 1, 0)
                        score(i, 0)
                        if not first(i):
                            values(i - 1, 1, 1)
                        turn(i, 4)
                        project(i, 6)
                        turn(i, 5)
                        project(i, 7)
                        if not first(i):
                            sum_heads(i - 1, 2)
                        turn_probs(i, 0)
                        if not first(i):
                            sum_heads(i - 1, 3)
                        turn(i, 6)
                        turn(i, 7)
                        if not is_last(i):
                            turn_x(i + 1)
                        values(i, 0, 0)
                        values(i, 0, 1)
                        score(i, 1)

                    turn_x(0)
                    over_tiles(pe, tile)
                    sum_heads(TILES - 1, 0)
                    sum_heads(TILES - 1, 1)
                    turn_probs(TILES - 1, 1)
                    values(TILES - 1, 1, 0)
                    values(TILES - 1, 1, 1)
                    sum_heads(TILES - 1, 2)
                    sum_heads(TILES - 1, 3)

                @block.scalar
                def _(act):
                    load_next(act, key)

                    def copy_x(i):
                        act.wait_ge(sem(s["turned"]), at(s["turned"], i, 1))
                        if not first(i):
                            act.wait_ge(sem(proj), at(proj, i, 0))
                        act.activation(xcT[:, :, :], bank_t[0][:, 0:3 * P].rearrange("p (a b) -> p a b", b=P),
                                       ACT.Copy).then_inc(sem(s["xT"]), 1)

                    def square(i, j):
                        act.wait_ge(sem(proj), at(proj, i, j + 1))
                        if not (first(i) and j < 2):
                            act.wait_ge(sem(sqs), at(sqs, i, j - 1))
                        act.activation(stage[:, j % 2, :], bank_p[j % 2][:, :], ACT.Square).then_inc(sem(sq), 1)

                    def copy_qk(i, j):
                        act.wait_ge(sem(qk_turned), at(qk_turned, i, j + 1))
                        src = bank_t[j % 2][:, :].rearrange("p (h t) -> p h t", h=4)
                        heads = slice(j // 2 * 4, j // 2 * 4 + 4)
                        if j % 2 == 0:
                            act.activation(qT[:, heads, :], src, ACT.Copy).then_inc(sem(qkT), 1)
                        else:
                            act.activation(kT[:, heads, :], src, ACT.Copy, scale=gcol[:, 2:3]).then_inc(sem(qkT), 1)

                    def exps(i, g):
                        act.wait_ge(sem(sub), at(sub, i, g + 1))
                        act.activation(E[:, g, :, :], E[:, g, :, :], ACT.Exp, scale=score_scale).then_inc(sem(ex), 1)

                    def copy_probs(i, g):
                        act.wait_ge(sem(p_turned), at(p_turned, i, g + 1))
                        act.activation(PT[:, g, :, :], bank_s[g][:, :].rearrange("p (a t) -> p a t", a=4), ACT.Copy)\
                            .then_inc(sem(pT), 1)

                    def tile(i):
                        square(i, 0)
                        square(i, 1)
                        if not first(i):
                            exps(i - 1, 1)
                        copy_qk(i, 0)
                        square(i, 2)
                        copy_qk(i, 1)
                        square(i, 3)
                        copy_qk(i, 2)
                        square(i, 4)
                        if not first(i):
                            copy_probs(i - 1, 1)
                        copy_qk(i, 3)
                        square(i, 5)
                        exps(i, 0)
                        for j in range(4, 6):
                            copy_qk(i, j)
                            square(i, j + 2)
                        copy_probs(i, 0)
                        copy_qk(i, 6)
                        copy_qk(i, 7)
                        if not is_last(i):
                            copy_x(i + 1)

                    copy_x(0)
                    over_tiles(act, tile)
                    exps(TILES - 1, 1)
                    copy_probs(TILES - 1, 1)

                @block.gpsimd
                def _(pool):
                    def tile(i):
                        for j in range(jobs):
                            c = slice(4 * j, 4 * j + 4)
                            pool.wait_ge(sem(sqs), at(sqs, i, j + 1))
                            pool.tensor_tensor(ssq_e[:, c], ssq[:, c], rms_eps[:, 0:4], ALU.add).then_inc(sem(sqe), 1)
                            pool.wait_ge(sem(sqe), at(sqe, i, j + 1))
                            pool.tensor_tensor(rnorm[:, c], ssq_e[:, c], minus_half[:, 0:4], ALU.pow).then_inc(sem(rn), 1)
                            if j == 1 and not is_last(i):
                                pool_rstd(pool, s, i + 1)
                    pool_rstd(pool, s, 0)
                    over_tiles(pool, tile)

                @block.vector
                def _(dve):
                    def sum_squares(i, j):
                        dve.wait_ge(sem(sq), at(sq, i, j + 1))
                        if not first(i):
                            dve.wait_ge(sem(normed), at(normed, i, j))
                        dve.tensor_reduce(ssq[:, 4 * j:4 * j + 4], stage[:, j % 2, :].rearrange("p (h d) -> p h d", h=4),
                                          AX, ALU.add).then_inc(sem(sqs), 1)

                    def norm(i, j):
                        dve.wait_ge(sem(rn), at(rn, i, j + 1))
                        if j >= 2:
                            dve.wait_ge(sem(qk_turned), at(qk_turned, i, j - 1))
                        dve.tensor_tensor(qn[:, j % 2, :].rearrange("p (h d) -> p h d", h=4),
                                          bank_p[j % 2][:, :].rearrange("p (h d) -> p h d", h=4),
                                          rnorm[:, 4 * j:4 * j + 4].unsqueeze(2).broadcast_to([P, 4, P]), ALU.mult)\
                            .then_inc(sem(normed), 1)

                    def shift(i, g):
                        dve.wait_ge(sem(scores), at(scores, i, g + 1))
                        src = bank_s[g][:, :].rearrange("p (h k) -> p h k", h=8)
                        dve.tensor_reduce(smax[:, g, 0, :], src, AX, ALU.max).then_inc(sem(smx), 1)
                        dve.wait_ge(sem(smx), at(smx, i, g + 1))
                        dve.tensor_tensor(E[:, g, :, :], src, smax[:, g, 0, :].unsqueeze(2).broadcast_to([P, 8, SEQ]),
                                          ALU.subtract).then_inc(sem(sub), 1)

                    def weigh(i, g):
                        dve.wait_ge(sem(ex), at(ex, i, g + 1))
                        dve.tensor_reduce(ssum[:, g, 0, :], E[:, g, :, :], AX, ALU.add).then_inc(sem(sm), 1)
                        dve.wait_ge(sem(sm), at(sm, i, g + 1))
                        dve.reciprocal(srec[:, g, 0, :], ssum[:, g, 0, :]).then_inc(sem(rec), 1)
                        dve.wait_ge(sem(rec), at(rec, i, g + 1))
                        dve.tensor_tensor(E[:, g, :, :], E[:, g, :, :],
                                          srec[:, g, 0, :].unsqueeze(2).broadcast_to([P, 8, SEQ]), ALU.mult)\
                            .then_inc(sem(probs), 1)

                    def copy_pv(i, g, b):
                        n = 2 * g + b
                        dve.wait_ge(sem(pv), at(pv, i, n + 1))
                        for a in range(2):
                            ins = dve.tensor_copy(OT[:, 8 * g + a:8 * g + 8:2, b * SEQ:(b + 1) * SEQ],
                                                  banks_o[n][:, a * 256:(a + 1) * 256].rearrange("p (h t) -> p h t", h=4))
                        ins.then_inc(sem(oT), 1)

                    def add(i):
                        dve.wait_ge(sem(y), at(y, i, 1))
                        dve.scalar_tensor_tensor(x[:, i, :], bank_y[:, 0:DIM], tanh_g[:, layer:layer + 1], x[:, i, :],
                                                 ALU.mult, ALU.add).then_inc(sem(added), 1)

                    def tile(i):
                        sum_squares(i, 0)
                        if not first(i):
                            shift(i - 1, 1)
                        norm(i, 0)
                        sum_squares(i, 1)
                        if not is_last(i):
                            ln_stats(dve, s, i + 1)
                        norm(i, 1)
                        sum_squares(i, 2)
                        if not is_last(i):
                            ln_apply(dve, s, i + 1)
                        norm(i, 2)
                        sum_squares(i, 3)
                        if not first(i):
                            weigh(i - 1, 1)
                        norm(i, 3)
                        sum_squares(i, 4)
                        if not first(i):
                            copy_pv(i - 1, 1, 0)
                        norm(i, 4)
                        sum_squares(i, 5)
                        shift(i, 0)
                        norm(i, 5)
                        if not first(i):
                            copy_pv(i - 1, 1, 1)
                        sum_squares(i, 6)
                        weigh(i, 0)
                        norm(i, 6)
                        sum_squares(i, 7)
                        norm(i, 7)
                        if not first(i):
                            add(i - 1)
                        copy_pv(i, 0, 0)
                        copy_pv(i, 0, 1)

                    dve_layernorm(dve, s, 0)
                    over_tiles(dve, tile)
                    shift(TILES - 1, 1)
                    weigh(TILES - 1, 1)
                    copy_pv(TILES - 1, 1, 0)
                    copy_pv(TILES - 1, 1, 1)
                    add(TILES - 1)
            block_ends()

        def masked_attention(layer, key, m, w2, score_scale):
            jobs = 4
            s = ln_signals()
            S = counted
            s["c"], s["ce"], s["co"] = S("c_loaded", 16), S("c_even_loaded", 16), S("c_odd_loaded", 16)
            proj = S("projected", jobs)
            qkT = S("qkT_ready", jobs)
            scores = S("scores_ready", 2)
            masked, recv = (S(n, 2) for n in ("scores_masked", "sum_inverse_valid"))
            smx, sub, ex, sm, rec, probs = (S(n, 2) for n in (
                "score_max", "scores_shifted", "exp_ready", "exp_sum", "sum_inverse", "probs_ready"))
            p_turned = S("probs_turned", 2)
            pT = S("probsT_ready", 2)
            pv = S("pv_ready", 4)
            oT = S("pvT_copied", 4)
            y = S("y_ready", 1)
            added = S("y_added", 1)
            banks_o = [bank_o, bank_p[1], bank_t[0], bank_t[1]]

            with nc.Block() as block:
                @block.sync
                def _(sp):
                    load_contexts(sp, s, pv)

                @block.tensor
                def _(pe):
                    def turn_x(i):
                        pe_turn_x(pe, s, i, bank_p[0], c_in=lambda: pe.wait_ge(sem(s["c"]), at(s["c"], i, 16)),
                                  bank_free=None if first(i) else
                                  (lambda: pe.wait_ge(sem(qkT), at(qkT, i - 1, 3))))

                    def project(i, j):
                        if j >= 2:
                            pe.wait_ge(sem(qkT), at(qkT, i, j - 1))
                        for h in range(4):
                            for k in range(KC):
                                mm = pe.matmul(bank_p[j % 2][:, h * P:(h + 1) * P], m[:, k, 4 * j + h, :],
                                               xcT[:, k, :], start=(k == 0), stop=(k == KC - 1))
                        mm.then_inc(sem(proj), 1)

                    def score(i, g):
                        pe.wait_ge(sem(qkT), at(qkT, i, 2 * g + 2))
                        if not first(i):
                            pe.wait_ge(sem(sub), at(sub, i - 1, g + 1))
                        for h in range(8):
                            for b in range(2):
                                rows = slice(b * SEQ, (b + 1) * SEQ)
                                mm = pe.matmul(bank_s[g][rows, h * SEQ:(h + 1) * SEQ], qT[:, 8 * g + h, rows],
                                               xcT[:, 2, rows], start=True, stop=True)
                        mm.then_inc(sem(scores), 1)

                    def front(i):
                        pe.wait_ge(sem(s["xT"]), at(s["xT"], i, 1))
                        for j in range(jobs):
                            project(i, j)
                            if j == 2:
                                score(i, 0)

                    def values(i, g, b):
                        if b == 0:
                            pe.wait_ge(sem(pT), at(pT, i, g + 1))
                        n = 2 * g + b
                        if n == 0:
                            pe.wait_ge(sem(s["ce"]), at(s["ce"], i, 16))
                            pe.wait_ge(sem(s["co"]), at(s["co"], i, 16))
                        for a, c in enumerate((c_even, c_odd)):
                            mm = pe.matmul(banks_o[n][:, a * 256:(a + 1) * 256], c[:, b, :],
                                           PT[:, g, :, b * SEQ:(b + 1) * SEQ], start=True, stop=True)
                        mm.then_inc(sem(pv), 1)

                    def turn_probs(i):
                        for g in range(2):
                            pe.wait_ge(sem(probs), at(probs, i, g + 1))
                            for a in range(4):
                                mm = pe.transpose(bank_t[g][:, a * P:(a + 1) * P],
                                                  E[:, g, 2 * a:2 * a + 2, :].rearrange("p a b -> p (a b)"), ident[:, :])
                            mm.then_inc(sem(p_turned), 1)

                    def back(i):
                        for g in range(2):
                            for b in range(2):
                                values(i, g, b)
                        for g in range(2):
                            pe.wait_ge(sem(oT), at(oT, i, 2 * g + 2))
                            if g == 0 and not first(i):
                                pe.wait_ge(sem(added), at(added, i, 0))
                            for h in range(8):
                                mm = pe.matmul(bank_y[:, 0:DIM], OT[:, 8 * g + h, :], w2[:, 8 * g + h, :],
                                               start=(g == 0 and h == 0), stop=(g == 1 and h == 7))
                        mm.then_inc(sem(y), 1)

                    def tile(i):
                        front(i)
                        if not first(i):
                            turn_probs(i - 1)
                        score(i, 1)
                        if not is_last(i):
                            turn_x(i + 1)
                        if not first(i):
                            back(i - 1)

                    turn_x(0)
                    over_tiles(pe, tile)
                    turn_probs(TILES - 1)
                    back(TILES - 1)

                @block.scalar
                def _(act):
                    load_next(act, key)

                    def copy_x(i):
                        act.wait_ge(sem(s["turned"]), at(s["turned"], i, 1))
                        if not first(i):
                            act.wait_ge(sem(scores), at(scores, i, 0))
                        act.activation(xcT[:, :, :], bank_p[0][:, 0:3 * P].rearrange("p (a b) -> p a b", b=P),
                                       ACT.Copy).then_inc(sem(s["xT"]), 1)

                    def copy_q(i, j):
                        act.wait_ge(sem(proj), at(proj, i, j + 1))
                        if j == 0 and not first(i):
                            act.wait_ge(sem(scores), at(scores, i, 0))
                        act.activation(qT[:, 4 * j:4 * j + 4, :], bank_p[j % 2][:, :].rearrange("p (h t) -> p h t", h=4),
                                       ACT.Copy).then_inc(sem(qkT), 1)

                    def copy_probs(i):
                        for g in range(2):
                            act.wait_ge(sem(p_turned), at(p_turned, i, g + 1))
                            act.activation(PT[:, g, :, :], bank_t[g][:, :].rearrange("p (a t) -> p a t", a=4), ACT.Copy)\
                                .then_inc(sem(pT), 1)

                    def exps(i):
                        for g in range(2):
                            act.wait_ge(sem(sub), at(sub, i, g + 1))
                            act.activation(E[:, g, :, :], E[:, g, :, :], ACT.Exp, scale=score_scale).then_inc(sem(ex), 1)

                    def tile(i):
                        for j in range(jobs):
                            copy_q(i, j)
                        if not first(i):
                            copy_probs(i - 1)
                        if not is_last(i):
                            copy_x(i + 1)
                        exps(i)

                    copy_x(0)
                    over_tiles(act, tile)
                    copy_probs(TILES - 1)

                @block.gpsimd
                def _(pool):
                    def tile(i):
                        if not within(i, 2):
                            pool_rstd(pool, s, i + 2)
                    pool_rstd(pool, s, 0)
                    pool_rstd(pool, s, 1)
                    over_tiles(pool, tile, tail=2)

                @block.vector
                def _(dve):
                    def shift(i, g):
                        dve.wait_ge(sem(scores), at(scores, i, g + 1))
                        if not first(i):
                            dve.wait_ge(sem(p_turned), at(p_turned, i - 1, g + 1))
                        src = E[:, g, :, :]
                        dve.tensor_tensor(src, bank_s[g][:, :].rearrange("p (h k) -> p h k", h=8),
                                          mask_add[:, i, :].unsqueeze(1).broadcast_to([P, 8, SEQ]), ALU.add)\
                            .then_inc(sem(masked), 1)
                        dve.wait_ge(sem(masked), at(masked, i, g + 1))
                        dve.tensor_reduce(smax[:, g, 0, :], src, AX, ALU.max).then_inc(sem(smx), 1)
                        dve.wait_ge(sem(smx), at(smx, i, g + 1))
                        dve.tensor_tensor(E[:, g, :, :], src, smax[:, g, 0, :].unsqueeze(2).broadcast_to([P, 8, SEQ]),
                                          ALU.subtract).then_inc(sem(sub), 1)

                    def weigh(i, g):
                        dve.wait_ge(sem(ex), at(ex, i, g + 1))
                        dve.tensor_reduce(ssum[:, g, 0, :], E[:, g, :, :], AX, ALU.add).then_inc(sem(sm), 1)
                        dve.wait_ge(sem(sm), at(sm, i, g + 1))
                        dve.reciprocal(srec[:, g, 0, :], ssum[:, g, 0, :]).then_inc(sem(rec), 1)
                        dve.wait_ge(sem(rec), at(rec, i, g + 1))
                        dve.tensor_tensor(srec[:, g, 0, :], srec[:, g, 0, :], mask_any[:, i, :].broadcast_to([P, 8]),
                                          ALU.mult).then_inc(sem(recv), 1)
                        dve.wait_ge(sem(recv), at(recv, i, g + 1))
                        dve.tensor_tensor(E[:, g, :, :], E[:, g, :, :],
                                          srec[:, g, 0, :].unsqueeze(2).broadcast_to([P, 8, SEQ]), ALU.mult)\
                            .then_inc(sem(probs), 1)

                    def copy_pv(i, n):
                        g, b = n // 2, n % 2
                        dve.wait_ge(sem(pv), at(pv, i, n + 1))
                        if n == 0 and not first(i):
                            dve.wait_ge(sem(y), at(y, i, 0))
                        for a in range(2):
                            ins = dve.tensor_copy(OT[:, 8 * g + a:8 * g + 8:2, b * SEQ:(b + 1) * SEQ],
                                                  banks_o[n][:, a * 256:(a + 1) * 256].rearrange("p (h t) -> p h t", h=4))
                        ins.then_inc(sem(oT), 1)

                    def add(i):
                        dve.wait_ge(sem(y), at(y, i, 1))
                        dve.scalar_tensor_tensor(x[:, i, :], bank_y[:, 0:DIM], tanh_g[:, layer:layer + 1], x[:, i, :],
                                                 ALU.mult, ALU.add).then_inc(sem(added), 1)

                    def tile(i):
                        if not within(i, 2):
                            ln_stats(dve, s, i + 2)
                        shift(i, 0)
                        if not first(i):
                            copy_pv(i - 1, 0)
                            copy_pv(i - 1, 1)
                        shift(i, 1)
                        if not within(i, 2):
                            ln_apply(dve, s, i + 2)
                        if not first(i):
                            copy_pv(i - 1, 2)
                            copy_pv(i - 1, 3)
                        weigh(i, 0)
                        weigh(i, 1)
                        if not first(i):
                            add(i - 1)

                    dve_layernorm(dve, s, 0)
                    dve_layernorm(dve, s, 1)
                    over_tiles(dve, tile, tail=2)
                    for n in range(4):
                        copy_pv(TILES - 1, n)
                    add(TILES - 1)
            block_ends()

        mask_add = sb("mask_add", [P, TILES, SEQ])
        mask_u8 = sb("mask_u8", [P, TILES, SEQ], U8)
        mask_any = sb("mask_any", [P, TILES, 1])

        def run_l1x():
            wq, wk, wv = aw(0, KC, 2048), aw(4096, 2048), aw(6144, 2048)
            wo, w2 = aw(8192, 16, DIM), aw(12288, 16, DIM)
            scaled = ctx.enter_context(nc.semaphore("l1_gain"))
            with nc.Block() as block:
                @block.vector
                def _(dve):
                    dve.wait_ge(weights_in["l1x"], w_count["l1x"])
                    dve.tensor_tensor(gcol[:, 2:3], gcol[:, 0:1], gcol[:, 1:2], ALU.mult).then_inc(scaled, 1)
            absorb_part("l1x", 8, None, None, wv, wo, None, w2)
            normed_attention(1, "l1x", wq, wk, w2, float(P) ** 0.5)

        def run_l3x():
            wq, wk, wv = aw(0, KC, 2048), aw(4096, 1024), aw(5120, 1024)
            wo, m, w2 = aw(6144, 16, DIM), aw(10240, KC * 16, P), aw(14336, 16, DIM)
            m = m.rearrange("p (k h) c -> p k h c", k=KC)
            made = ctx.enter_context(nc.semaphore("mask_made"))
            with nc.Block() as block:
                @block.vector
                def _(dve):
                    dve.wait_ge(weights_in["l3x"], w_count["l3x"])
                    dve.tensor_copy(mask_add[:, :, :], mask_u8[:, :, :]).then_inc(made, 1)
                    dve.wait_ge(made, 1)
                    dve.tensor_reduce(mask_any[:, :, 0], mask_add[:, :, :], AX, ALU.max).then_inc(made, 1)
                    dve.wait_ge(made, 2)
                    dve.tensor_scalar(mask_add[:, :, :], mask_add[:, :, :], 1.0, 1e30, ALU.subtract, ALU.mult)\
                        .then_inc(made, 1)
            absorb_part("l3x", 8, wq, wk, wv, wo, m, w2)
            masked_attention(3, "l3x", m, w2, float(P) ** -0.5)

        head_mask = sb("head_mask", [P, 16])
        pair_mask = sb("pair_mask", [P, DIM])
        qkT_n = o_all[:, 0:512].rearrange("p (a t) -> p a t", a=4)
        v_pairs = o_all[:, 512:1024].rearrange("p (b d) -> p b d", b=2)
        o_sb = o_all[:, 1024:1280]
        oT_n = o_all[:, 1280:1536].rearrange("p (k t) -> p k t", k=KC)
        c_parts = o_all[:, 1536:2304].rearrange("p (n k r t) -> p n k r t", n=2, k=3, r=2)
        key_side = sb("key_side", [2, 2, SEQ])
        kv_bias = attn_w[0:2, 2048:2560].rearrange("p (n d) -> p n d", n=2)
        row_bias = attn_w[0:1, 2560:2816]
        out_bias = attn_w[0:1, 2816:3072]
        norm_rows = attn_w[0:6, 3072:3200]
        norm_cols = sb("norm_cols", [P, 6])
        mean_n = sb("mean_n", [P, 2, 32])
        ropes = sb("ropes", [P, TILES, 16])
        ropes_w = attn_w[:, 4096:4352].rearrange("p (n a) -> p n a", n=4)
        ropes_i = attn_w[:, 4352:4416].bitcast(I32)
        pos = sb("pos", [P, TILES, 2])

        def narrow_attention(layer, key, hd, wq, wo, k_weights, v_weights, keys_main):
            split = keys_main < SEQ
            heads = DIM // hd
            in_half = P // hd
            chunks = heads // 8
            segs = [(0, keys_main), (keys_main, SEQ)] if split else [(0, SEQ)]
            score_scale = float(hd) ** -0.5
            kb = qk_all[:, 0:2 * 2 * in_half * SEQ].rearrange("p (f b h t) -> p f b h t", f=2, b=2, h=in_half)
            s = ln_signals()
            S = counted
            s["c"] = S("c_loaded", 16)
            c_split = S("context_split", 2 * len(segs))
            qk = S("qk_projected", 1)
            v = S("v_projected", 1)
            v_in = S("v_spread", 1)
            steps = S("qk_steps", 4 if split else 3)
            sqr, sqe, rn = (S(n, 1 if split else 0) for n in ("squared", "norm_eps", "norm_ready"))
            normed = S("qk_normed", 1)
            qk_turned = S("qk_turned", 1)
            qkT = S("qkT_ready", 3 if split else 1)
            spread = [S("keys_spread_low", 2), S("keys_spread_high", 2)]
            scores = S("scores_ready", chunks)
            nseg = len(segs)
            smx, sub = (S(n, chunks * nseg) for n in ("score_max", "scores_shifted"))
            ex = S("exp_ready", chunks)
            sm, probs = (S(n, chunks * nseg if split else m) for n, m in (("exp_sum", 1), ("probs_ready", 0)))
            rec = S("sum_inverse", chunks if split else 1)
            p_turned = S("probs_turned", chunks)
            pT = S("probsT_ready", chunks)
            pv = S("pv_ready", 1)
            o_in = S("pv_copied", 1)
            o_turned = S("pv_turned", 1)
            oT = S("pvT_ready", 1)
            y = S("y_ready", 1)
            added = S("y_added", 1)

            def spread_keys(eng, i, f):
                eng.wait_ge(sem(qkT), at(qkT, i, per(qkT)))
                if not first(i):
                    eng.wait_ge(sem(scores), at(scores, i, 0))
                for b in range(2):
                    eng.tensor_tensor(
                        kb[:, f, b, :, :],
                        qkT_n[:, 2 + f, b * SEQ:(b + 1) * SEQ].unsqueeze(1).broadcast_to([P, in_half, SEQ]),
                        head_mask[:, 0:in_half].unsqueeze(2).broadcast_to([P, in_half, SEQ]), ALU.mult)\
                        .then_inc(sem(spread[f]), 1)

            with nc.Block() as block:
                @block.sync
                def _(sp):
                    over_tiles(sp, lambda i: load_context(sp, i, s, s["turned"]))

                @block.tensor
                def _(pe):
                    def keys_of(part, b=None):
                        return c_parts[:, part, 0 if b is None else 1 + b, :, :].rearrange("p r t -> p (r t)")

                    def turn_x(i, o_before=False):
                        pe_turn_x(pe, s, i, bank_t[0], c_in=lambda: pe.wait_ge(sem(s["c"]), at(s["c"], i, 16)),
                                  bank_free=(lambda: pe.wait_ge(sem(oT), at(oT, i - 3, 1))) if o_before else None)

                    def project_qk(i):
                        pe.wait_ge(sem(s["xT"]), at(s["xT"], i, 1))
                        for k in range(KC):
                            pe.matmul(bank_p[0][:, 0:DIM], xcT[:, k, :], wq[:, k, :], start=(k == 0),
                                      stop=(not split and k == KC - 1))
                        if split:
                            pe.matmul(bank_p[0][:, 0:DIM], ones[0:1, :], row_bias[:, :], start=False, stop=True)
                        pe.wait_ge(sem(c_split), at(c_split, i, per(c_split)))
                        for n, w in enumerate(k_weights):
                            mm = pe.matmul(bank_p[0][:, DIM:2 * DIM], keys_of(n), w, start=(n == 0),
                                           stop=(not split and n == len(k_weights) - 1))
                        if split:
                            mm = pe.matmul(bank_p[0][:, DIM:2 * DIM], key_side[:, :, :], kv_bias[:, 0, :],
                                           start=False, stop=True)
                        mm.then_inc(sem(qk), 1)

                    def project_v(i):
                        if not first(i):
                            pe.wait_ge(sem(v_in), at(v_in, i, 0))
                        for b in range(2):
                            o = bank_p[1][:, b * DIM:(b + 1) * DIM]
                            for n, w in enumerate(v_weights):
                                mm = pe.matmul(o, keys_of(n, b), w, start=(n == 0),
                                               stop=(not split and n == len(v_weights) - 1))
                            if split:
                                mm = pe.matmul(o, key_side[:, :, :], kv_bias[:, 1, :], start=False, stop=True)
                        mm.then_inc(sem(v), 1)

                    def turn_qk(i):
                        pe.wait_ge(sem(normed), at(normed, i, 1))
                        for a in range(4):
                            mm = pe.transpose(bank_t[1][:, a * P:(a + 1) * P], qn[:, 0, a * P:(a + 1) * P], ident[:, :])
                        mm.then_inc(sem(qk_turned), 1)

                    def score(i):
                        for g in range(chunks):
                            f, h0 = g * 8 // in_half, g * 8 % in_half
                            pe.wait_ge(sem(spread[f]), at(spread[f], i, 2))
                            if g >= 2:
                                pe.wait_ge(sem(sub), at(sub, i, nseg * (g - 1)))
                            for b in range(2):
                                rows = slice(b * SEQ, (b + 1) * SEQ)
                                mm = pe.matmul(bank_s[g % 2][rows, :], qkT_n[:, f, rows], kb[:, f, b, h0:h0 + 8, :],
                                               start=True, stop=True)
                            mm.then_inc(sem(scores), 1)

                    def turn_probs(i, g):
                        if split:
                            pe.wait_ge(sem(probs), at(probs, i, nseg * (g + 1)))
                        else:
                            pe.wait_ge(sem(ex), at(ex, i, g + 1))
                        if g >= 2:
                            pe.wait_ge(sem(pT), at(pT, i, g - 1))
                        else:
                            pe.wait_ge(sem(sub), at(sub, i, nseg * (chunks - 1 + g)))
                        for a in range(4):
                            mm = pe.transpose(bank_s[g % 2][:, a * P:(a + 1) * P],
                                              E[:, g, 2 * a:2 * a + 2, :].rearrange("p a b -> p (a b)"), ident[:, :])
                        mm.then_inc(sem(p_turned), 1)

                    def weigh_values(i, g):
                        pe.wait_ge(sem(pT), at(pT, i, g + 1))
                        if g == 0:
                            pe.wait_ge(sem(v_in), at(v_in, i, 1))
                        for a in range(4):
                            c = slice((8 * g + 2 * a) * hd, (8 * g + 2 * a + 2) * hd)
                            for b in range(2):
                                rows = slice(b * SEQ, (b + 1) * SEQ)
                                mm = pe.matmul(bank_o[rows, c], PT[:, g, a, rows], v_pairs[:, b, c],
                                               start=True, stop=True)
                        if g == chunks - 1:
                            mm.then_inc(sem(pv), 1)

                    def values(i):
                        for g in range(chunks):
                            weigh_values(i, g)

                    def turn_o(i):
                        pe.wait_ge(sem(o_in), at(o_in, i, 1))
                        for k in range(KC):
                            mm = pe.transpose(bank_t[0][:, k * P:(k + 1) * P], o_sb[:, k * P:(k + 1) * P], ident[:, :])
                        mm.then_inc(sem(o_turned), 1)

                    def project_o(i):
                        pe.wait_ge(sem(oT), at(oT, i, 1))
                        if not first(i):
                            pe.wait_ge(sem(added), at(added, i, 0))
                        for k in range(KC):
                            pe.matmul(bank_y[:, 0:DIM], oT_n[:, k, :], wo[:, k, :], start=(k == 0), stop=False)
                        pe.matmul(bank_y[:, 0:DIM], ones[0:1, :], out_bias[:, :], start=False, stop=True)\
                            .then_inc(sem(y), 1)

                    def tile(i):
                        if not first(i):
                            values(i - 1)
                        score(i)
                        if not first(i):
                            turn_o(i - 1)
                        if not within(i, 1):
                            project_v(i + 1)
                            turn_qk(i + 1)
                        if not within(i, 2):
                            turn_x(i + 2, o_before=not first(i))
                        if not first(i):
                            project_o(i - 1)
                        if not within(i, 2):
                            project_qk(i + 2)
                        for g in range(chunks):
                            turn_probs(i, g)

                    turn_x(0)
                    project_qk(0)
                    project_v(0)
                    turn_x(1)
                    turn_qk(0)
                    project_qk(1)
                    over_tiles(pe, tile, tail=3)
                    values(TILES - 1)
                    turn_o(TILES - 1)
                    project_o(TILES - 1)

                @block.scalar
                def _(act):
                    load_next(act, key)

                    def front(i):
                        act.wait_ge(sem(s["turned"]), at(s["turned"], i, 1))
                        if not first(i):
                            act.wait_ge(sem(v), at(v, i, 0))
                        act.activation(xcT[:, :, :], bank_t[0][:, 0:3 * P].rearrange("p (a b) -> p a b", b=P),
                                       ACT.Copy).then_inc(sem(s["xT"]), 1)
                        src = bank_t[0][:, 2 * P:3 * P].rearrange("p (b t) -> p b t", b=2)
                        for n, (a, e) in enumerate(segs):
                            act.activation(c_parts[:, n, 0, :, a:e], src[:, :, a:e], ACT.Copy).then_inc(sem(c_split), 1)
                            act.activation(c_parts[:, n, 1:3, :, a:e],
                                           src[:, :, a:e].unsqueeze(2).broadcast_to([P, 2, 2, e - a]), ACT.Copy)\
                                .then_inc(sem(c_split), 1)

                    def square(i):
                        if split:
                            act.wait_ge(sem(steps), at(steps, i, 3))
                            act.activation(stage[:, 0, :], qn[:, 0, :], ACT.Square).then_inc(sem(sqr), 1)

                    def turned_qk(i):
                        act.wait_ge(sem(qk_turned), at(qk_turned, i, 1))
                        if not first(i):
                            act.wait_ge(sem(scores), at(scores, i, 0))
                        if not split:
                            act.activation(qkT_n[:, :, :], bank_t[1][:, :].rearrange("p (a t) -> p a t", a=4), ACT.Copy)\
                                .then_inc(sem(qkT), 1)
                            return
                        act.activation(qkT_n[:, 0:2, :], bank_t[1][:, 0:2 * P].rearrange("p (a t) -> p a t", a=2),
                                       ACT.Identity, scale=norm_cols[:, 0:1], bias=norm_cols[:, 1:2]).then_inc(sem(qkT), 1)
                        src = bank_t[1][:, 2 * P:4 * P].rearrange("p (f t) -> p f t", t=SEQ)
                        dst = qkT_n[:, 2:4, :].rearrange("p f (b t) -> p (f b) t", b=2)
                        for n, (a, e) in enumerate(segs):
                            act.activation(dst[:, :, a:e], src[:, :, a:e], ACT.Identity,
                                           scale=norm_cols[:, 2 + 2 * n:3 + 2 * n], bias=norm_cols[:, 3 + 2 * n:4 + 2 * n])\
                                .then_inc(sem(qkT), 1)

                    def exps(i, g):
                        act.wait_ge(sem(sub), at(sub, i, nseg * (g + 1)))
                        act.activation(E[:, g, :, :], E[:, g, :, :], ACT.Exp, scale=score_scale).then_inc(sem(ex), 1)

                    def copy_probs(i, g):
                        act.wait_ge(sem(p_turned), at(p_turned, i, g + 1))
                        act.activation(PT[:, g, :, :], bank_s[g % 2][:, :].rearrange("p (a t) -> p a t", a=4), ACT.Copy)\
                            .then_inc(sem(pT), 1)

                    def copy_oT(i):
                        act.wait_ge(sem(o_turned), at(o_turned, i, 1))
                        act.activation(oT_n[:, :, :], bank_t[0][:, 0:KC * P].rearrange("p (a b) -> p a b", b=P), ACT.Copy)\
                            .then_inc(sem(oT), 1)

                    def tile(i):
                        for g in range(chunks - 1):
                            exps(i, g)
                        if not first(i):
                            copy_oT(i - 1)
                        exps(i, chunks - 1)
                        if not within(i, 1):
                            turned_qk(i + 1)
                        if not within(i, 2):
                            front(i + 2)
                        for g in range(chunks // 2):
                            copy_probs(i, g)
                        if not within(i, 2):
                            square(i + 2)
                        for g in range(chunks // 2, chunks):
                            copy_probs(i, g)

                    front(0)
                    square(0)
                    front(1)
                    turned_qk(0)
                    square(1)
                    over_tiles(act, tile, tail=3)
                    copy_oT(TILES - 1)

                @block.gpsimd
                def _(pool):
                    def norm(i):
                        pool.wait_ge(sem(steps), at(steps, i, 4))
                        pool.tensor_tensor(ssq_e[:, :], ssq[:, :], head_eps[:, :], ALU.add).then_inc(sem(sqe), 1)
                        pool.wait_ge(sem(sqe), at(sqe, i, 1))
                        pool.tensor_tensor(rnorm[:, :], ssq_e[:, :], minus_half[:, 0:32], ALU.pow).then_inc(sem(rn), 1)

                    def tile(i):
                        if not within(i, 3):
                            pool_rstd(pool, s, i + 3)
                        if not within(i, 1):
                            spread_keys(pool, i + 1, 1)
                        if split and not within(i, 2):
                            norm(i + 2)

                    for i in range(3):
                        pool_rstd(pool, s, i)
                    if split:
                        norm(0)
                    spread_keys(pool, 0, 1)
                    if split:
                        norm(1)
                    over_tiles(pool, tile, tail=3)

                @block.vector
                def _(dve):
                    def centre_qk(i):
                        src = bank_p[0][:, :].rearrange("p (h d) -> p h d", d=hd)
                        dve.wait_ge(sem(qk), at(qk, i, 1))
                        if not first(i):
                            dve.wait_ge(sem(normed), at(normed, i, 0))
                        dve.tensor_reduce(mean_n[:, 0, :], src, AX, ALU.add).then_inc(sem(steps), 1)
                        dve.wait_ge(sem(steps), at(steps, i, 1))
                        dve.tensor_scalar(mean_n[:, 1, :], mean_n[:, 0, :], 1.0 / hd, None, ALU.mult).then_inc(sem(steps), 1)
                        dve.wait_ge(sem(steps), at(steps, i, 2))
                        if not first(i):
                            dve.wait_ge(sem(qk_turned), at(qk_turned, i, 0))
                        dve.tensor_tensor(qn[:, 0, :].rearrange("p (h d) -> p h d", d=hd), src,
                                          mean_n[:, 1, :].unsqueeze(2).broadcast_to([P, 32, hd]), ALU.subtract)\
                            .then_inc(sem(steps), 1)

                    def sum_squares(i):
                        dve.wait_ge(sem(sqr), at(sqr, i, 1))
                        dve.tensor_reduce(ssq[:, :], stage[:, 0, :].rearrange("p (h d) -> p h d", d=hd), AX, ALU.add)\
                            .then_inc(sem(steps), 1)

                    def scale_qk(i):
                        dst = qn[:, 0, :].rearrange("p (h d) -> p h d", d=hd)
                        dve.wait_ge(sem(rn), at(rn, i, 1))
                        dve.tensor_tensor(dst, dst, rnorm[:, :].unsqueeze(2).broadcast_to([P, 32, hd]), ALU.mult)\
                            .then_inc(sem(normed), 1)

                    def rotate_qk(i):
                        src = bank_p[0][:, :].rearrange("p (h r) -> p h r", r=8)
                        pair = bank_p[0][:, :].rearrange("p (h r two) -> p h r two", r=4, two=2)
                        turn = stage[:, 0, :].rearrange("p (h r two) -> p h r two", r=4, two=2)
                        dve.wait_ge(sem(qk), at(qk, i, 1))
                        if not first(i):
                            dve.wait_ge(sem(normed), at(normed, i, 0))
                            dve.wait_ge(sem(qk_turned), at(qk_turned, i, 0))
                        dve.tensor_tensor(qn[:, 0, :].rearrange("p (h r) -> p h r", r=8), src,
                                          ropes[:, i, 0:8].unsqueeze(1).broadcast_to([P, 64, 8]), ALU.mult)\
                            .then_inc(sem(steps), 1)
                        for n in range(2):
                            dve.tensor_tensor(turn[:, :, :, n], pair[:, :, :, 1 - n],
                                              ropes[:, i, 8 + 4 * n:12 + 4 * n].unsqueeze(1).broadcast_to([P, 64, 4]),
                                              ALU.mult).then_inc(sem(steps), 1)
                        dve.wait_ge(sem(steps), at(steps, i, 3))
                        dve.tensor_tensor(qn[:, 0, :], qn[:, 0, :], stage[:, 0, :], ALU.add).then_inc(sem(normed), 1)

                    def spread_v(i):
                        dve.wait_ge(sem(v), at(v, i, 1))
                        if not first(i):
                            dve.wait_ge(sem(pv), at(pv, i - 1, 1))
                        dve.tensor_tensor(v_pairs[:, :, :], bank_p[1][:, :].rearrange("p (b d) -> p b d", b=2),
                                          pair_mask[:, :].unsqueeze(1).broadcast_to([P, 2, DIM]), ALU.mult)\
                            .then_inc(sem(v_in), 1)

                    def shift(i, g):
                        dve.wait_ge(sem(scores), at(scores, i, g + 1))
                        src = bank_s[g % 2][:, :].rearrange("p (h k) -> p h k", h=8)
                        for n, (a, e) in enumerate(segs):
                            dve.tensor_reduce(smax[:, g, n, :], src[:, :, a:e], AX, ALU.max).then_inc(sem(smx), 1)
                        for n, (a, e) in enumerate(segs):
                            dve.wait_ge(sem(smx), at(smx, i, nseg * g + n + 1))
                            dve.tensor_tensor(E[:, g, :, a:e], src[:, :, a:e],
                                              smax[:, g, n, :].unsqueeze(2).broadcast_to([P, 8, e - a]), ALU.subtract)\
                                .then_inc(sem(sub), 1)

                    def weigh(i, g):
                        dve.wait_ge(sem(ex), at(ex, i, g + 1))
                        for n, (a, e) in enumerate(segs):
                            dve.tensor_reduce(ssum[:, g, n, :], E[:, g, :, a:e], AX, ALU.add).then_inc(sem(sm), 1)
                        dve.wait_ge(sem(sm), at(sm, i, nseg * (g + 1)))
                        dve.reciprocal(srec[:, g, 0:nseg, :], ssum[:, g, 0:nseg, :]).then_inc(sem(rec), 1)
                        dve.wait_ge(sem(rec), at(rec, i, g + 1))
                        for n, (a, e) in enumerate(segs):
                            dve.tensor_tensor(E[:, g, :, a:e], E[:, g, :, a:e],
                                              srec[:, g, n, :].unsqueeze(2).broadcast_to([P, 8, e - a]), ALU.mult)\
                                .then_inc(sem(probs), 1)

                    def sum_exps(i):
                        dve.wait_ge(sem(ex), at(ex, i, chunks))
                        dve.tensor_reduce(ssum[:, 0:chunks, 0, :], E[:, 0:chunks, :, :], AX, ALU.add).then_inc(sem(sm), 1)
                        dve.wait_ge(sem(sm), at(sm, i, 1))
                        dve.reciprocal(srec[:, 0:chunks, 0, :], ssum[:, 0:chunks, 0, :]).then_inc(sem(rec), 1)

                    def copy_o(i):
                        dve.wait_ge(sem(pv), at(pv, i, 1))
                        if split:
                            dve.tensor_copy(o_sb[:, :], bank_o[:, 0:DIM]).then_inc(sem(o_in), 1)
                        else:
                            dve.wait_ge(sem(rec), at(rec, i, 1))
                            dve.tensor_tensor(o_sb[:, :].rearrange("p (g h d) -> p g h d", g=chunks, h=8),
                                              bank_o[:, 0:DIM].rearrange("p (g h d) -> p g h d", g=chunks, h=8),
                                              srec[:, 0:chunks, 0, :].unsqueeze(3).broadcast_to([P, chunks, 8, hd]),
                                              ALU.mult).then_inc(sem(o_in), 1)

                    def add(i):
                        dve.wait_ge(sem(y), at(y, i, 1))
                        dve.scalar_tensor_tensor(x[:, i, :], bank_y[:, 0:DIM], tanh_g[:, layer:layer + 1], x[:, i, :],
                                                 ALU.mult, ALU.add).then_inc(sem(added), 1)

                    def tile(i):
                        if not within(i, 3):
                            ln_stats(dve, s, i + 3)
                        if not first(i):
                            copy_o(i - 1)
                        spread_v(i)
                        shift(i, 0)
                        shift(i, 1)
                        if split and not within(i, 1):
                            scale_qk(i + 1)
                        for g in range(2, chunks):
                            shift(i, g)
                        if split:
                            weigh(i, 0)
                            weigh(i, 1)
                        else:
                            sum_exps(i)
                        if not within(i, 1):
                            spread_keys(dve, i + 1, 0)
                        if not within(i, 2):
                            (centre_qk if split else rotate_qk)(i + 2)
                        if not first(i):
                            add(i - 1)
                        if not within(i, 3):
                            ln_apply(dve, s, i + 3)
                        if split and not within(i, 2):
                            sum_squares(i + 2)

                    for i in range(3):
                        dve_layernorm(dve, s, i)
                        if i == 0:
                            (centre_qk if split else rotate_qk)(0)
                            if split:
                                sum_squares(0)
                    if split:
                        scale_qk(0)
                    (centre_qk if split else rotate_qk)(1)
                    if split:
                        sum_squares(1)
                    spread_keys(dve, 0, 0)
                    over_tiles(dve, tile, tail=3)
                    copy_o(TILES - 1)
                    add(TILES - 1)
            block_ends()

        def make_masks(pool, step, hd):
            n = P // hd
            hm = head_mask[:, 0:n]
            step(pool.memset(hm, 1.0))
            pm = pair_mask[:, :].rearrange("p (j two d) -> p j two d", two=2, d=hd)
            for half in range(2):
                for odd in range(2):
                    step(pool.memset(pm[half * SEQ:(half + 1) * SEQ, :, odd, :], 1.0 if half == odd else 0.0))
            step(pool.affine_select(out=hm, in_=hm, compare_op=ALU.is_ge, fill=0.0, base=0, pattern=[[-hd, n]],
                                    channel_multiplier=1))
            step(pool.affine_select(out=hm, in_=hm, compare_op=ALU.is_ge, fill=0.0, base=hd - 1, pattern=[[hd, n]],
                                    channel_multiplier=-1))

        def in_turn(eng, sem):
            done = [0]

            def step(ins):
                done[0] += 1
                ins.then_inc(sem, 1)
                eng.wait_ge(sem, done[0])
            return step

        def run_l0x():
            hd, main = 16, 48
            wq, wkv, wd, wo = aw(0, KC, DIM), aw(512, 16, 2, 16), aw(1024, 512), aw(1536, KC, DIM)
            made = ctx.enter_context(nc.semaphore("l0_masks"))
            cols = ctx.enter_context(nc.semaphore("l0_norm_cols"))
            with nc.Block() as block:
                @block.gpsimd
                def _(pool):
                    step = in_turn(pool, made)
                    make_masks(pool, step, hd)
                    step(pool.memset(o_all[:, 1536:2304], 0.0))
                    step(pool.memset(key_side[:, :, :], 1.0))
                    step(pool.affine_select(out=key_side[:, :, :], in_=key_side[:, :, :], compare_op=ALU.is_ge, fill=0.0,
                                            base=main - 1, pattern=[[0, 2], [-1, SEQ]], channel_multiplier=SEQ))
                    step(pool.affine_select(out=key_side[:, :, :], in_=key_side[:, :, :], compare_op=ALU.is_ge, fill=0.0,
                                            base=SEQ - main, pattern=[[0, 2], [1, SEQ]], channel_multiplier=-SEQ))

                @block.tensor
                def _(pe):
                    pe.wait_ge(weights_in["l0x"], w_count["l0x"])
                    pe.transpose(bank_t[0][:, 0:6], norm_rows[:, :], ident[0:6, 0:6]).then_inc(cols, 1)

                @block.vector
                def _(dve):
                    dve.wait_ge(cols, 1)
                    dve.tensor_copy(norm_cols[:, :], bank_t[0][:, 0:6]).then_inc(cols, 1)
                    dve.wait_ge(cols, 2)
                    dve.tensor_scalar(norm_cols[:, 0:6:2], norm_cols[:, 0:6:2], float(hd) ** 0.5, None, ALU.mult)\
                        .then_inc(cols, 1)
            narrow_attention(0, "l0x", hd, wq, wo, [wkv[:, :, 0, :], wd[:, 0:DIM]], [wkv[:, :, 1, :], wd[:, DIM:2 * DIM]],
                             main)

        def run_l2x():
            hd = 8
            wq, wkv, wo = aw(0, KC, DIM), aw(512, 512), aw(1024, KC, DIM)
            made = ctx.enter_context(nc.semaphore("l2_masks"))
            r = ctx.enter_context(nc.semaphore("rope_steps"))
            sines = ctx.enter_context(nc.semaphore("rope_sines"))
            pi = PI
            with nc.Block() as block:
                @block.gpsimd
                def _(pool):
                    make_masks(pool, in_turn(pool, made), hd)

                @block.vector
                def _(dve):
                    ang, tmp, sin_in, cos_in = (ropes_w[:, n, :] for n in range(4))
                    step = in_turn(dve, r)

                    def wrapped(ap):
                        step(dve.tensor_scalar(tmp, ap, pi, -2 * pi, ALU.is_gt, ALU.mult))
                        step(dve.tensor_tensor(ap, ap, tmp, ALU.add))
                        step(dve.tensor_scalar(tmp, ap, -pi, 2 * pi, ALU.is_lt, ALU.mult))
                        step(dve.tensor_tensor(ap, ap, tmp, ALU.add))
                        step(dve.tensor_scalar(ap, ap, 3.1415925, -3.1415925, ALU.min, ALU.max))

                    dve.wait_ge(weights_in["l2x"], w_count["l2x"])
                    a4 = ang.rearrange("p (n a f) -> p n a f", a=2, f=2)
                    for f, freq in enumerate((1.0, 10000.0 ** -0.5)):
                        step(dve.tensor_scalar(a4[:, :, :, f], pos[:, :, :], freq, None, ALU.mult))
                    step(dve.tensor_scalar(tmp, ang, 1.0 / (2 * pi), None, ALU.mult))
                    step(dve.tensor_copy(ropes_i[:, :], tmp))
                    step(dve.tensor_copy(tmp, ropes_i[:, :]))
                    step(dve.scalar_tensor_tensor(ang, tmp, -6.28125, ang, ALU.mult, ALU.add))
                    step(dve.scalar_tensor_tensor(sin_in, tmp, -(2 * pi - 6.28125), ang, ALU.mult, ALU.add))
                    step(dve.tensor_scalar(cos_in, sin_in, pi / 2, None, ALU.add))
                    wrapped(sin_in)
                    wrapped(cos_in)
                    dve.wait_ge(sines, 2)
                    c4 = cos_in.rearrange("p (n r) -> p n r", r=4)
                    s4 = sin_in.rearrange("p (n r) -> p n r", r=4)
                    pair = ropes[:, :, 0:8].rearrange("p n (r two) -> p n r two", two=2)
                    step(dve.tensor_copy(pair[:, :, :, 0], c4))
                    step(dve.tensor_copy(pair[:, :, :, 1], c4))
                    step(dve.tensor_scalar(ropes[:, :, 8:12], s4, -1.0, None, ALU.mult))
                    step(dve.tensor_copy(ropes[:, :, 12:16], s4))

                @block.scalar
                def _(act):
                    act.wait_ge(r, 18)
                    act.activation(ropes_w[:, 2, :], ropes_w[:, 2, :], ACT.Sin).then_inc(sines, 1)
                    act.activation(ropes_w[:, 3, :], ropes_w[:, 3, :], ACT.Sin).then_inc(sines, 1)
            narrow_attention(2, "l2x", hd, wq, wo, [wkv[:, 0:DIM]], [wkv[:, DIM:2 * DIM]], SEQ)

        def run_l3f():
            key, hid = "l3f", 16
            w_in = fw(0, KC, EXPERTS + P)
            up_T = fw(512, DIM)
            raw_down, raw_router = fw(1024, DIM), ffn_w[0:EXPERTS, 1536:1536 + DIM]
            raw_up = fw(2048, KC, EXPERTS, hid)
            wt = ctx.enter_context(nc.semaphore("l3f_turned"))
            wk_ = ctx.enter_context(nc.semaphore("l3f_kept"))
            with nc.Block() as block:
                @block.tensor
                def _(pe):
                    pe.wait_ge(weights_in[key], w_count[key])
                    for c in range(KC):
                        pe.transpose(bank_t[0][:, c * P:(c + 1) * P], raw_down[:, c * P:(c + 1) * P], ident[:, :])
                    for c in range(KC):
                        mm = pe.transpose(bank_t[0][:, DIM + c * P:DIM + (c + 1) * P],
                                          raw_up[:, c, :, :].rearrange("p e i -> p (e i)"), ident[:, :])
                    for c in range(KC):
                        mm = pe.transpose(bank_t[1][:, c * EXPERTS:(c + 1) * EXPERTS],
                                          raw_router[:, c * P:(c + 1) * P], ident[0:EXPERTS, 0:EXPERTS])
                    mm.then_inc(wt, 1)

                @block.vector
                def _(dve):
                    dve.wait_ge(wt, 1)
                    dve.tensor_copy(w_in[:, :, EXPERTS:EXPERTS + P],
                                    bank_t[0][:, 0:DIM].rearrange("p (k n) -> p k n", k=KC)).then_inc(wk_, 1)
                    dve.tensor_copy(w_in[:, :, 0:EXPERTS],
                                    bank_t[1][:, 0:KC * EXPERTS].rearrange("p (k n) -> p k n", k=KC)).then_inc(wk_, 1)
                    dve.tensor_copy(up_T, bank_t[0][:, DIM:2 * DIM]).then_inc(wk_, 1)

            s = ln_signals()
            S = counted
            proj = S("projected", 1)
            th_s = S("tanh_ready", 1)
            hid_s = S("hidden_half", 1)
            lg_in = S("logits_copied", 1)
            g_steps = S("gate_steps", 8)
            ex_s = S("exp_ready", 1)
            act_in = S("hidden_ready", 1)
            turned = S("hidden_turned", 1)
            hTr = S("hiddenT_ready", 1)
            down = S("down_ready", 1)
            added = S("expert_added", 1)
            gated = S("gates_ready", 1)
            es, er, nm = lead_t, g_first, g_second

            with nc.Block() as block:
                @block.tensor
                def _(pe):
                    def tile(i):
                        pe_turn_x(pe, s, i, bank_t[0])
                        pe.wait_ge(sem(s["xT"]), at(s["xT"], i, 1))
                        if not first(i):
                            pe.wait_ge(sem(act_in), at(act_in, i, 0))
                        for k in range(KC):
                            mm = pe.matmul(bank_p[0][:, 0:EXPERTS + P], xcT[:, k, :], w_in[:, k, :], start=(k == 0),
                                           stop=(k == KC - 1))
                        mm.then_inc(sem(proj), 1)
                        pe.wait_ge(sem(act_in), at(act_in, i, 1))
                        pe.transpose(bank_t[1][:, 0:P], hh[:, 0, 0:P], ident[:, :]).then_inc(sem(turned), 1)
                        pe.wait_ge(sem(hTr), at(hTr, i, 1))
                        if not first(i):
                            pe.wait_ge(sem(added), at(added, i, 0))
                        pe.matmul(bank_y[:, 0:DIM], hT[:, 0, 0, :], up_T, start=True, stop=True).then_inc(sem(down), 1)
                    over_tiles(pe, tile)

                @block.scalar
                def _(act):
                    load_next(act, key)

                    def tile(i):
                        act.wait_ge(sem(s["turned"]), at(s["turned"], i, 1))
                        if not first(i):
                            act.wait_ge(sem(proj), at(proj, i, 0))
                        act.activation(xcT[:, 0:KC, :], bank_t[0][:, 0:KC * P].rearrange("p (a b) -> p a b", b=P),
                                       ACT.Copy).then_inc(sem(s["xT"]), 1)
                        act.wait_ge(sem(proj), at(proj, i, 1))
                        act.activation(th[:, 0, 0:P], bank_p[0][:, EXPERTS:EXPERTS + P], ACT.Tanh, scale=0.5)\
                            .then_inc(sem(th_s), 1)
                        act.wait_ge(sem(g_steps), at(g_steps, i, 2))
                        act.activation(pick[:, 0, :], lg[:, :], ACT.Exp, bias=nm[:, 0:1], accum_out=es[:, :])\
                            .then_inc(sem(ex_s), 1)
                        act.wait_ge(sem(turned), at(turned, i, 1))
                        act.activation(hT[:, 0, 0, :], bank_t[1][:, 0:P], ACT.Copy).then_inc(sem(hTr), 1)
                    over_tiles(act, tile)

                @block.gpsimd
                def _(pool):
                    over_tiles(pool, lambda i: pool_rstd(pool, s, i))

                @block.vector
                def _(dve):
                    def tile(i):
                        if not is_last(i):
                            dve_layernorm(dve, s, i + 1)
                        dve.wait_ge(sem(th_s), at(th_s, i, 1))
                        if not first(i):
                            dve.wait_ge(sem(turned), at(turned, i, 0))
                        dve.scalar_tensor_tensor(hh[:, 0, 0:P], th[:, 0, 0:P], 1.0, bank_p[0][:, EXPERTS:EXPERTS + P],
                                                 ALU.add, ALU.mult).then_inc(sem(hid_s), 1)
                        dve.tensor_copy(lg[:, :], bank_p[0][:, 0:EXPERTS]).then_inc(sem(lg_in), 1)
                        wait_apart(dve, sem(lg_in), at(lg_in, i, 1))
                        dve.max(top[:, :], lg[:, :]).then_inc(sem(g_steps), 1)
                        dve.wait_ge(sem(g_steps), at(g_steps, i, 1))
                        dve.tensor_scalar(nm[:, :], top[:, 0:1], -1.0, None, ALU.mult).then_inc(sem(g_steps), 1)
                        dve.max_index(top_i[:, :], top[:, :], lg[:, :]).then_inc(sem(g_steps), 1)
                        dve.wait_ge(sem(g_steps), at(g_steps, i, 3))
                        dve.tensor_copy(top_f[:, :], top_i[:, 0:2]).then_inc(sem(g_steps), 1)
                        dve.wait_ge(sem(ex_s), at(ex_s, i, 1))
                        dve.reciprocal(er[:, :], es[:, :]).then_inc(sem(g_steps), 1)
                        dve.wait_ge(sem(g_steps), at(g_steps, i, 5))
                        dve.tensor_scalar(er[:, :], er[:, :], half_g[:, 3:4], None, ALU.mult).then_inc(sem(g_steps), 1)
                        dve.tensor_scalar(gate[:, :], iota8[:, :], top_f[:, 0:1], None, ALU.is_equal).then_inc(sem(g_steps), 1)
                        dve.wait_ge(sem(g_steps), at(g_steps, i, 7))
                        dve.scalar_tensor_tensor(gate[:, :], iota8[:, :], top_f[:, 1:2], gate[:, :], ALU.is_equal,
                                                 ALU.add).then_inc(sem(g_steps), 1)
                        dve.wait_ge(sem(g_steps), at(g_steps, i, 8))
                        dve.scalar_tensor_tensor(gate[:, :], gate[:, :], er[:, 0:1], pick[:, 0, :], ALU.mult, ALU.mult)\
                            .then_inc(sem(gated), 1)
                        dve.wait_ge(sem(gated), at(gated, i, 1))
                        dve.tensor_tensor(hh[:, 0, 0:P].rearrange("p (e i) -> p e i", e=EXPERTS),
                                          hh[:, 0, 0:P].rearrange("p (e i) -> p e i", e=EXPERTS),
                                          gate[:, :].unsqueeze(2).broadcast_to([P, EXPERTS, hid]), ALU.mult)\
                            .then_inc(sem(act_in), 1)
                        dve.wait_ge(sem(down), at(down, i, 1))
                        dve.tensor_tensor(x[:, i, :], bank_y[:, 0:DIM], x[:, i, :], ALU.add).then_inc(sem(added), 1)

                    dve_layernorm(dve, s, 0)
                    over_tiles(dve, tile)
            block_ends()

        def moe_loads(sp, layer, key, gate_w, up_w, down_w, router_w, hid):
            fk = hid // 2 if hid > P else hid
            fc = hid // fk
            wgu = ffn_w[:, 0:KC * EXPERTS * 2 * hid].rearrange("p (k e g f) -> p k e g f", k=KC, e=EXPERTS, g=2)
            wd = ffn_w[0:fk, KC * EXPERTS * 2 * hid:KC * EXPERTS * 2 * hid + fc * EXPERTS * DIM]\
                .rearrange("p (c e d) -> p c e d", c=fc, e=EXPERTS)
            load(sp, key, router[:, layer, :, :], router_w.rearrange("(k p) e -> p k e", p=P))
            for k in range(KC):
                load(sp, key, wgu[:, k, :, 0, :], gate_w[:, k * P:(k + 1) * P, :].rearrange("e p f -> p e f"))
                load(sp, key, wgu[:, k, :, 1, :], up_w[:, k * P:(k + 1) * P, :].rearrange("e p f -> p e f"))
            for c in range(fc):
                load(sp, key, wd[:, c, :, :], down_w[:, c * fk:(c + 1) * fk, :].rearrange("e p d -> p e d"))

        MOE = {
            "l0f": (0, 128, "L0_ffn_wi_0", "L0_ffn_wi_1", "L0_ffn_wo", "L0_ffn_w_gate"),
            "l1f": (1, 176, "L1_ffn_Wg", "L1_ffn_Wu", "L1_ffn_Wd", "L1_ffn_Wr"),
            "l2f": (2, 256, "L2_ffn_Wg", "L2_ffn_Wu", "L2_ffn_Wd", "L2_ffn_Wr"),
        }

        def run_moe(key):
            layer, hid = MOE[key][:2]
            moe_part(layer, key, hid, lambda: w_count[key])

        def load_moe(sp, key):
            layer, hid, g, u, d, r = MOE[key]
            moe_loads(sp, layer, key, io[g], io[u], io[d], io[r], hid)

        def load_l0x(sp):
            hd = 16
            wq, wd, wo = aw(0, KC, DIM), aw(1024, 512), aw(1536, KC, DIM)
            k = "l0x"
            load(sp, k, wq, io["L0_xattn_Wq"].rearrange("(k p) n -> p k n", p=P))
            load(sp, k, attn_w[:, 512:768], io["L0_xattn_Wk"])
            load(sp, k, attn_w[:, 768:1024], io["L0_xattn_Wv"])
            load(sp, k, wd, io["L0_xattn_Wkv_dca"])
            load(sp, k, wo, io["L0_xattn_Wo"].rearrange("(k p) n -> p k n", p=P))
            load(sp, k, row_bias[:, :], io["L0_xattn_bq"].unsqueeze(0))
            load(sp, k, out_bias[:, :], io["L0_xattn_bo"].unsqueeze(0))
            for half, name in enumerate(("L0_xattn_bk", "L0_xattn_bv")):
                src = io[name].rearrange("(h t d) -> t h d", t=2, d=hd)
                for t in range(2):
                    load(sp, k, kv_bias[0:1, t, half * P:(half + 1) * P].rearrange("p (h d) -> p h d", d=hd),
                         src[t:t + 1])
            load(sp, k, kv_bias[1:2, :, :], io["L0_xattn_bkv_dca"].rearrange("(a t n) -> a t n", a=1, t=2))
            for n, name in enumerate(("qn_w", "qn_b", "kn_w", "kn_b", "kn_dca_w", "kn_dca_b")):
                load(sp, k, norm_rows[n:n + 1, :].rearrange("p (h d) -> p h d", d=hd),
                     io["L0_xattn_" + name].rearrange("(a b d) -> a b d", a=1, b=1).broadcast_to([1, P // hd, hd]))

        def load_l1x(sp):
            wq, wk, wv = aw(0, KC, 2048), aw(4096, 2048), aw(6144, 2048)
            wo, w2 = aw(8192, 16, DIM), aw(12288, 16, DIM)
            load(sp, "l1x", wq, io["L1_xattn_Wq"].rearrange("(k p) n -> p k n", p=P))
            load(sp, "l1x", wk, io["L1_xattn_Wk"])
            load(sp, "l1x", wv, io["L1_xattn_Wv"])
            load(sp, "l1x", wo, io["L1_xattn_Wo"].rearrange("(h p) d -> p h d", p=P))
            load(sp, "l1x", gcol[:, 0:1], io["L1_xattn_gq"].rearrange("(p a) -> p a", a=1))
            load(sp, "l1x", gcol[:, 1:2], io["L1_xattn_gk"].rearrange("(p a) -> p a", a=1))

        def load_l2x(sp):
            wq, wkv, wo = aw(0, KC, DIM), aw(512, 512), aw(1024, KC, DIM)
            k = "l2x"
            load(sp, k, wq, io["L2_xattn_Wq"].rearrange("(k p) n -> p k n", p=P))
            load(sp, k, wkv, io["L2_xattn_Wkv"])
            load(sp, k, wo, io["L2_xattn_Wout"].rearrange("(k p) n -> p k n", p=P))
            load(sp, k, out_bias[:, :], io["L2_xattn_bout"].unsqueeze(0))
            load(sp, k, pos[:, :, :], io["fside_BxSx2_0"].rearrange("b s a -> (b s) a")
                 .rearrange("(n p) a -> p n a", p=P))

        def load_l3x(sp):
            wq, wk, wv = aw(0, KC, 2048), aw(4096, 1024), aw(5120, 1024)
            wo = aw(6144, 16, DIM)
            load(sp, "l3x", wq, io["L3_xattn_Wq"].rearrange("(k p) n -> p k n", p=P))
            load(sp, "l3x", wk, io["L3_xattn_Wk"])
            load(sp, "l3x", wv, io["L3_xattn_Wv"])
            load(sp, "l3x", wo, io["L3_xattn_Wo"].rearrange("(h p) d -> p h d", p=P))
            rows = io["mask_BxS2_bf1"].rearrange("(n b) k -> b n k", b=2)
            for b in range(2):
                load(sp, "l3x", mask_u8[b * SEQ:(b + 1) * SEQ, :, :],
                     rows[b:b + 1].broadcast_to([SEQ, TILES, SEQ]))

        def load_l3f(sp):
            key, hid = "l3f", 16
            raw_down, raw_router = fw(1024, DIM), ffn_w[0:EXPERTS, 1536:1536 + DIM]
            raw_up = fw(2048, KC, EXPERTS, hid)
            load(sp, key, raw_down, io["L3_ffn_down_w"].rearrange("e i h -> (e i) h"))
            load(sp, key, raw_router, io["L3_ffn_router_w"])
            for c in range(KC):
                load(sp, key, raw_up[:, c, :, :],
                     io["L3_ffn_up_w"][:, c * P:(c + 1) * P, :].rearrange("e p i -> p e i"))

        loaders = {"l0x": load_l0x, "l1x": load_l1x, "l2x": load_l2x, "l3x": load_l3x, "l3f": load_l3f}

        def load_part(queue, key):
            if key in loaders:
                loaders[key](queue)
            elif key is not None:
                load_moe(queue, key)

        def load_next(queue, key):
            n = parts.index(key) + 1
            if n < len(parts) and not (key[2] == parts[n][2]):
                load_part(queue, parts[n])
                loaded.append(parts[n])

        loaded = []

        def weights_of(key):
            if key not in loaded:
                with nc.Block() as block:
                    @block.sync
                    def _(sp):
                        load_part(sp, key)

        run = {"l0x": run_l0x, "l1x": run_l1x, "l2x": run_l2x, "l3x": run_l3x, "l3f": run_l3f}
        for key in parts:
            weights_of(key)
            run[key]() if key in run else run_moe(key)

        with nc.Block() as block:
            @block.sync
            def _(sp):
                sp.dma_start(out.rearrange("b s d -> (b s) d").rearrange("(n p) d -> p n d", p=P), x[:, :, :])\
                    .then_inc(out_stored, 16)
                sp.wait_ge(out_stored, 16)


PARTS = ("l0x", "l0f", "l1x", "l1f", "l2x", "l2f", "l3x", "l3f")


def kernel(**inputs):
    import numpy as np
    from concourse import bacc
    from concourse.bass_utils import run_bass_kernel_spmd

    nc = bacc.Bacc("TRN2", target_bir_lowering=False, num_devices=1)
    arrays, io = {}, {}
    for name, value in inputs.items():
        a = np.ascontiguousarray(value)
        if a.dtype == np.bool_:
            a = a.view(np.uint8)
        arrays[f"in_{name}_dram"] = a
        io[name] = nc.dram_tensor(f"in_{name}_dram", a.shape, mybir.dt.from_np(a.dtype), kind="ExternalInput").ap()
    out = nc.dram_tensor("out_0_dram", (BATCH, SEQ, DIM), F32, kind="ExternalOutput").ap()
    flamingo_kernel(nc, io, out, PARTS)
    r = run_bass_kernel_spmd(nc, [arrays], core_ids=[0])
    return r.results[0]["out_0_dram"]
```

```python
from contextlib import ExitStack

import concourse.bass as bass
from concourse import mybir

F32 = mybir.dt.float32
U32 = mybir.dt.uint32
I32 = mybir.dt.int32
U8 = mybir.dt.uint8
ALU = mybir.AluOpType
ACT = mybir.ActivationFunctionType
AX = mybir.AxisListType.X

P = 128
PI = 3.141592653589793
BATCH, SEQ, DIM, CTX = 32, 64, 256, 128
TILES = BATCH * SEQ // P
KC = DIM // P
GROUP = 512 // P
GROUPS = TILES // GROUP
EXPERTS = 8
LN_EPS = 1e-5
CHUNK_HEADS = 8


def sem(signal):
    return signal[0]


def per(signal):
    return signal[1]


def at(signal, tile, n):
    return tile * signal[1] + (signal[2] + n)


def over_tiles(eng, body, tail=1, n=TILES):
    body(0)
    with eng.Fori(1, n - tail) as i:
        body(i)
    for i in range(n - tail, n):
        body(i)


def first(i):
    return isinstance(i, int) and i == 0


def within(i, n):
    return isinstance(i, int) and i >= TILES - n


def is_last(i):
    return isinstance(i, int) and i == TILES - 1


def flamingo_kernel(nc, io, out, parts):
    ctx = ExitStack()
    with ctx:
        signals, in_use = {}, []

        def sb(name, shape, dt=F32):
            return ctx.enter_context(nc.sbuf_tensor(name, shape, dt))

        def ps(name):
            return ctx.enter_context(nc.psum_tensor(name, [P, 512], F32))

        def counted(name, n):
            if name not in signals:
                signals[name] = [ctx.enter_context(nc.semaphore(name)), 0, 0]
            signals[name][1] = n
            in_use.append(signals[name])
            return signals[name]

        def block_ends(n=TILES):
            for one in in_use:
                one[2] += n * one[1]
            del in_use[:]

        x = sb("x", [P, TILES, DIM])
        attn_w = sb("attn_w", [P, 18432])
        ffn_w = sb("ffn_w", [P, 12288])
        ident = sb("ident", [P, P])
        ones = sb("ones", [P, P])
        gates_raw = sb("gates_raw", [P, 8])
        tanh_g = sb("tanh_g", [P, 8])
        half_g = sb("half_g", [P, 4])
        quarter_g = sb("quarter_g", [P, 4])
        minus_half = sb("minus_half", [P, 32])
        ln_eps = sb("ln_eps", [P, 1])
        rms_eps = sb("rms_eps", [P, 4])
        head_eps = sb("head_eps", [P, 32])
        iota8 = sb("iota8", [P, EXPERTS])
        small = {
            "st": sb("st", [P, 6]), "mv": sb("mv", [P, 2]), "rstd": sb("rstd", [P, 1]),
            "var": sb("var", [P, 1]),
        }
        xn = sb("xn", [P, DIM])
        xcT = sb("xcT", [P, 3, P])
        c_tok = sb("c_tok", [P, CTX])
        c_even = sb("c_even", [P, 2, CTX])
        c_odd = sb("c_odd", [P, 2, CTX])
        bank_t = [ps("bank_t0"), ps("bank_t1")]
        bank_p = [ps("bank_p0"), ps("bank_p1")]
        bank_s = [ps("bank_s0"), ps("bank_s1")]
        bank_o = ps("bank_o")
        bank_y = ps("bank_y")

        weights_in = {n: ctx.enter_context(nc.semaphore(f"w_{n}")) for n in
                      ("first", "l0x", "l0f", "l1x", "l1f", "l2x", "l2f", "l3x", "l3f")}
        w_count = {n: 0 for n in weights_in}
        setup = ctx.enter_context(nc.semaphore("setup"))
        gates_tanh = ctx.enter_context(nc.semaphore("gates_tanh"))
        stood_apart = ctx.enter_context(nc.semaphore("stood_apart"))
        gates_scaled = ctx.enter_context(nc.semaphore("gates_scaled"))
        out_stored = ctx.enter_context(nc.semaphore("out_stored"))

        def load(sp, key, dst, src):
            sp.dma_start(dst, src).then_inc(weights_in[key], 16)
            w_count[key] += 16

        ctx_rows = io["ctx_1024"].rearrange("b s c -> (b s) c").rearrange("(n p) c -> n p c", p=P)
        ctx_by_row = io["ctx_1024"].rearrange("(n b) s c -> n s b c", b=2)

        def aw(off, *shape):
            n = 1
            for s in shape:
                n *= s
            ap = attn_w[:, off:off + n]
            if len(shape) == 2:
                return ap.rearrange("p (a b) -> p a b", a=shape[0])
            if len(shape) == 3:
                return ap.rearrange("p (a b c) -> p a b c", a=shape[0], b=shape[1])
            return ap

        def fw(off, *shape):
            n = 1
            for s in shape:
                n *= s
            ap = ffn_w[:, off:off + n]
            if len(shape) == 2:
                return ap.rearrange("p (a b) -> p a b", a=shape[0])
            if len(shape) == 3:
                return ap.rearrange("p (a b c) -> p a b c", a=shape[0], b=shape[1])
            return ap

        def wait_apart(eng, sem, value):
            eng.wait_ge(sem, value)
            eng.sem_inc(stood_apart, 1)

        def ln_signals():
            S = counted
            return dict(stats=S("ln_stats", 1), var=S("ln_var", 1), aggr=S("ln_aggr", 1), rstd=S("ln_rstd", 1), xn=S("xn_ready", 1),
                        turned=S("x_turned", 1), xT=S("xT_ready", 1))

        def ln_stats(dve, s, i):
            if not first(i):
                dve.wait_ge(sem(s["xn"]), at(s["xn"], i, 0))
            dve.bn_stats(small["st"][:, :], x[:, i, :]).then_inc(sem(s["stats"]), 1)
            wait_apart(dve, sem(s["stats"]), at(s["stats"], i, 1))
            dve.bn_aggr(small["mv"][:, :], small["st"][:, :]).then_inc(sem(s["aggr"]), 1)

        def ln_apply(dve, s, i):
            dve.wait_ge(sem(s["rstd"]), at(s["rstd"], i, 1))
            if not first(i):
                dve.wait_ge(sem(s["turned"]), at(s["turned"], i, 0))
            dve.tensor_scalar(xn[:, :], x[:, i, :], small["mv"][:, 0:1], small["rstd"][:, 0:1],
                              ALU.subtract, ALU.mult).then_inc(sem(s["xn"]), 1)

        def dve_layernorm(dve, s, i):
            ln_stats(dve, s, i)
            ln_apply(dve, s, i)

        def pool_rstd(pool, s, i):
            pool.wait_ge(sem(s["aggr"]), at(s["aggr"], i, 1))
            if not first(i):
                pool.wait_ge(sem(s["xn"]), at(s["xn"], i, 0))
            pool.tensor_tensor(small["var"][:, :], small["mv"][:, 1:2], ln_eps[:, :], ALU.add)\
                .then_inc(sem(s["var"]), 1)
            pool.wait_ge(sem(s["var"]), at(s["var"], i, 1))
            pool.tensor_tensor(small["rstd"][:, :], small["var"][:, :], minus_half[:, 0:1], ALU.pow)\
                .then_inc(sem(s["rstd"]), 1)

        def pe_turn_x(pe, s, i, bank, c_in=None, bank_free=None):
            pe.wait_ge(sem(s["xn"]), at(s["xn"], i, 1))
            if bank_free is not None:
                bank_free()
            for k in range(KC):
                mm = pe.transpose(bank[:, k * P:(k + 1) * P], xn[:, k * P:(k + 1) * P], ident[:, :])
            if c_in is not None:
                c_in()
                mm = pe.transpose(bank[:, 2 * P:3 * P], c_tok[:, :], ident[:, :])
            mm.then_inc(sem(s["turned"]), 1)

        with nc.Block() as block:
            @block.sync
            def _(sp):
                sp.dma_start(x[:, :, :], io["x"].rearrange("b s d -> (b s) d").rearrange("(n p) d -> p n d", p=P))\
                    .then_inc(weights_in["first"], 16)
                sp.dma_start(gates_raw[:, 0:4], io["g_xattn"].rearrange("(a g) -> a g", a=1).broadcast_to([P, 4]))\
                    .then_inc(weights_in["first"], 16)
                sp.dma_start(gates_raw[:, 4:8], io["g_ffn"].rearrange("(a g) -> a g", a=1).broadcast_to([P, 4]))\
                    .then_inc(weights_in["first"], 16)

            @block.gpsimd
            def _(pool):
                pool.memset(ident[:, :], 0.0).then_inc(setup, 1)
                pool.memset(ones[:, :], 1.0).then_inc(setup, 1)
                pool.memset(c_even[:, :, :], 0.0).then_inc(setup, 1)
                pool.memset(c_odd[:, :, :], 0.0).then_inc(setup, 1)
                pool.memset(minus_half[:, :], -0.5).then_inc(setup, 1)
                pool.memset(ln_eps[:, :], LN_EPS).then_inc(setup, 1)
                pool.memset(rms_eps[:, :], P * LN_EPS).then_inc(setup, 1)
                pool.memset(head_eps[:, :], 16 * 1e-6).then_inc(setup, 1)
                pool.iota(iota8[:, :], [[1, EXPERTS]], base=0, channel_multiplier=0,
                          allow_small_or_imprecise_dtypes=True).then_inc(setup, 1)
                pool.wait_ge(setup, 9)
                pool.affine_select(out=ident[:, :], in_=ident[:, :], compare_op=ALU.not_equal, fill=1.0, base=0,
                                   pattern=[[-1, P]], channel_multiplier=1).then_inc(setup, 1)

            @block.scalar
            def _(act):
                act.wait_ge(weights_in["first"], 48)
                act.activation(tanh_g[:, :], gates_raw[:, :], ACT.Tanh).then_inc(gates_tanh, 1)

            @block.vector
            def _(dve):
                dve.wait_ge(gates_tanh, 1)
                dve.tensor_scalar(half_g[:, :], tanh_g[:, 4:8], 0.5, None, ALU.mult).then_inc(gates_scaled, 1)
                dve.tensor_scalar(quarter_g[:, :], tanh_g[:, 4:8], 0.25, None, ALU.mult).then_inc(gates_scaled, 1)

        lg = sb("lg", [P, EXPERTS])
        top = sb("top", [P, 8])
        top_i = sb("top_i", [P, 8], U32)
        top_f = sb("top_f", [P, 2])
        lead = sb("lead", [P, 1])
        lead_t = sb("lead_t", [P, 1])
        g_first = sb("g_first", [P, 1])
        g_second = sb("g_second", [P, 1])
        pick = sb("pick", [P, 2, EXPERTS])
        gate = sb("gate", [P, EXPERTS])
        th = sb("th", [P, 2, 256])
        hh = sb("hh", [P, 2, 256])
        hT = sb("hT", [P, 2, 2, P])

        def expert_units(hid):
            if hid % P == 0:
                chunks = hid // P
                units = [(u * 2 * P, P) for u in range(EXPERTS * chunks)]
                downs = [[(e * chunks + c, 0, P, (c * EXPERTS + e) * DIM) for c in range(chunks)] for e in range(EXPERTS)]
                return units, downs
            body, rest = hid - SEQ, SEQ
            units, downs = [], []
            for pair in range(EXPERTS // 2):
                off = pair * 4 * hid
                units += [(off, 2 * rest), (off + 4 * rest, body), (off + 4 * rest + 2 * body, body)]
                for odd in range(2):
                    e = 2 * pair + odd
                    downs.append([(3 * pair, odd * rest, rest, (EXPERTS + pair) * DIM), (3 * pair + 1 + odd, 0, body, e * DIM)])
            return units, downs

        def moe_part(layer, key, hid, nw):
            units, downs = expert_units(hid)
            n_units = len(units)
            last_unit = [d[-1][0] for d in downs]
            user = [max(e for e in range(EXPERTS) if u in [d[0] for d in downs[e]]) for u in range(n_units)]
            wgu = [ffn_w[:, k * EXPERTS * 2 * hid:(k + 1) * EXPERTS * 2 * hid] for k in range(KC)]
            wd = ffn_w[:, KC * EXPERTS * 2 * hid:]
            wr = router[:, layer, :, :]
            x_g = x[:, :, :].rearrange("p (g t) d -> p g t d", t=GROUP)
            xn_g = o_all[:, 0:1024].rearrange("p (t d) -> p t d", t=GROUP)
            xT_g = qk_all[:, 0:1024].rearrange("p (k t) -> p k t", k=KC)
            tanh_g4 = PT[:, :, :, :].rearrange("p u a t -> p u (a t)")
            hidden_T = E[:, :, :, :].rearrange("p u a t -> p u (a t)")
            banks_g, banks_u = (bank_p[0], bank_s[0]), (bank_p[1], bank_s[1])
            banks_y = (bank_o, bank_y)
            S = counted
            stats, aggr, xn_s = (S(n, GROUP) for n in ("ln_stats", "ln_aggr", "xn_ready"))
            var, rstd, turned, xT_s = S("ln_var", 1), S("ln_rstd", 1), S("x_turned", 1), S("xT_ready", KC)
            logits, lg_in = S("logits_ready", 1), S("logits_copied", 1)
            g_max, g_steps, lead_s, gated = S("gate_max", GROUP), S("gate_steps", GROUP + 8), S("lead_tanh", 1), S("gates_ready", 1)
            gu, tanh, hid1, hid2 = (S(n, n_units) for n in ("gate_up_ready", "tanh_ready", "hidden_half", "hidden_ready"))
            down, added = S("down_ready", 2 * EXPERTS), S("expert_added", GROUP * EXPERTS)

            def last(g):
                return isinstance(g, int) and g == GROUPS - 1

            with nc.Block() as block:
                @block.tensor
                def _(pe):
                    pe.wait_ge(weights_in[key], nw)

                    def turn_x(g):
                        pe.wait_ge(sem(xn_s), at(xn_s, g, GROUP))
                        if not first(g):
                            pe.wait_ge(sem(lg_in), at(lg_in, g, 0))
                        for k in range(KC):
                            for t in range(GROUP):
                                mm = pe.transpose(bank_t[k][:, t * P:(t + 1) * P], xn_g[:, t, k * P:(k + 1) * P],
                                                  ident[:, :])
                        mm.then_inc(sem(turned), 1)

                    def route(g):
                        pe.wait_ge(sem(xT_s), at(xT_s, g, KC))
                        for t in range(GROUP):
                            for k in range(KC):
                                mm = pe.matmul(bank_t[0][:, t * EXPERTS:(t + 1) * EXPERTS],
                                               xT_g[:, k, t * P:(t + 1) * P], wr[:, k, :], start=(k == 0),
                                               stop=(k == KC - 1))
                        mm.then_inc(sem(logits), 1)

                    def gate_up(g, u):
                        off, rows = units[u]
                        if not (first(g) and u < 2):
                            pe.wait_ge(sem(hid2), at(hid2, g, u - 1))
                        for a, b in enumerate((banks_g[u % 2], banks_u[u % 2])):
                            for k in range(KC):
                                mm = pe.matmul(b[0:rows, :], wgu[k][:, off + a * rows:off + (a + 1) * rows],
                                               xT_g[:, k, :], start=(k == 0), stop=(k == KC - 1))
                        mm.then_inc(sem(gu), 1)

                    def down_e(g, e):
                        pe.wait_ge(sem(hid2), at(hid2, g, last_unit[e] + 1))
                        for t in range(GROUP):
                            if t % 2 == 0 and not (first(g) and e == 0):
                                pe.wait_ge(sem(added), at(added, g, GROUP * (e - 1) + t + 2))
                            o = banks_y[t // 2][:, t % 2 * DIM:(t % 2 + 1) * DIM]
                            for n, (u, r, rows, off) in enumerate(downs[e]):
                                mm = pe.matmul(o, hidden_T[r:r + rows, u % 4, t * P:(t + 1) * P],
                                               wd[r:r + rows, off:off + DIM], start=(n == 0), stop=(n == len(downs[e]) - 1))
                            if t % 2 == 1:
                                mm.then_inc(sem(down), 1)

                    def group(g):
                        for u in range(n_units):
                            gate_up(g, u)
                            if u == n_units - 3 and not last(g):
                                turn_x(g + 1)
                            if u == 0 and not first(g):
                                down_e(g - 1, EXPERTS - 1)
                            for e in range(EXPERTS):
                                if last_unit[e] == u - 1:
                                    down_e(g, e)
                        if not last(g):
                            route(g + 1)

                    turn_x(0)
                    route(0)
                    over_tiles(pe, group, n=GROUPS)
                    down_e(GROUPS - 1, EXPERTS - 1)

                @block.scalar
                def _(act):
                    load_next(act, key)

                    def copy_x(g):
                        act.wait_ge(sem(turned), at(turned, g, 1))
                        if not first(g):
                            act.wait_ge(sem(gu), at(gu, g, 0))
                        for k in range(KC):
                            act.activation(xT_g[:, k, :], bank_t[k][:, :], ACT.Copy).then_inc(sem(xT_s), 1)

                    def lead_in(g):
                        act.wait_ge(sem(g_steps), at(g_steps, g, GROUP + 2))
                        act.activation(leads_t, leads, ACT.Tanh, scale=0.5).then_inc(sem(lead_s), 1)

                    def group(g):
                        for u in range(n_units):
                            rows = units[u][1]
                            act.wait_ge(sem(gu), at(gu, g, u + 1))
                            act.activation(tanh_g4[0:rows, u % 4, :], banks_g[u % 2][0:rows, :], ACT.Tanh, scale=0.5)\
                                .then_inc(sem(tanh), 1)
                            if u == 0:
                                lead_in(g)
                        if not last(g):
                            copy_x(g + 1)

                    copy_x(0)
                    over_tiles(act, group, n=GROUPS)

                @block.gpsimd
                def _(pool):
                    def group(g):
                        pool.wait_ge(sem(aggr), at(aggr, g, GROUP))
                        if not first(g):
                            pool.wait_ge(sem(xn_s), at(xn_s, g, 0))
                        pool.tensor_tensor(vars_g, mvs[:, :, 1], ln_eps[:, :].broadcast_to([P, GROUP]), ALU.add)\
                            .then_inc(sem(var), 1)
                        pool.wait_ge(sem(var), at(var, g, 1))
                        pool.tensor_tensor(rstds, vars_g, minus_half[:, 0:GROUP], ALU.pow).then_inc(sem(rstd), 1)
                    over_tiles(pool, group, n=GROUPS)

                @block.vector
                def _(dve):
                    def ln_stats_g(g):
                        if not first(g):
                            dve.wait_ge(sem(xn_s), at(xn_s, g, 0))
                        for t in range(GROUP):
                            dve.bn_stats(sts[:, t, :], x_g[:, g, t, :]).then_inc(sem(stats), 1)
                        for t in range(GROUP):
                            wait_apart(dve, sem(stats), at(stats, g, t + 1))
                            dve.bn_aggr(mvs[:, t, :], sts[:, t, :]).then_inc(sem(aggr), 1)

                    def ln_apply_g(g):
                        dve.wait_ge(sem(rstd), at(rstd, g, 1))
                        if not first(g):
                            dve.wait_ge(sem(turned), at(turned, g, 0))
                        for t in range(GROUP):
                            dve.tensor_scalar(xn_g[:, t, :], x_g[:, g, t, :], mvs[:, t, 0:1], rstds[:, t:t + 1],
                                              ALU.subtract, ALU.mult).then_inc(sem(xn_s), 1)

                    def hidden(g, u):
                        rows = units[u][1]
                        th = tanh_g4[0:rows, u % 4, :]
                        dve.wait_ge(sem(tanh), at(tanh, g, u + 1))
                        dve.scalar_tensor_tensor(th, th, 1.0, banks_g[u % 2][0:rows, :], ALU.add, ALU.mult)\
                            .then_inc(sem(hid1), 1)
                        dve.wait_ge(sem(hid1), at(hid1, g, u + 1))
                        if not (first(g) and u < 4):
                            e = user[u - 4]
                            dve.wait_ge(sem(down), at(down, g, 2 * (e + 1) - (2 * EXPERTS if u < 4 else 0)))
                        dve.tensor_tensor(hidden_T[0:rows, u % 4, :], th, banks_u[u % 2][0:rows, :], ALU.mult)\
                            .then_inc(sem(hid2), 1)

                    def gate_max(g):
                        dve.wait_ge(sem(logits), at(logits, g, 1))
                        if not first(g):
                            dve.wait_ge(sem(added), at(added, g, 0))
                        dve.tensor_copy(lgs[:, :, :], bank_t[0][:, 0:GROUP * EXPERTS].rearrange("p (t e) -> p t e", t=GROUP))\
                            .then_inc(sem(lg_in), 1)
                        wait_apart(dve, sem(lg_in), at(lg_in, g, 1))
                        for t in range(GROUP):
                            dve.max(tops[:, t, :], lgs[:, t, :]).then_inc(sem(g_max), 1)
                        for t in range(GROUP):
                            wait_apart(dve, sem(g_max), at(g_max, g, t + 1))
                            dve.max_index(tops_i[:, t, :], tops[:, t, :], lgs[:, t, :]).then_inc(sem(g_steps), 1)
                        dve.tensor_tensor(leads, tops[:, :, 0], tops[:, :, 1], ALU.subtract).then_inc(sem(g_steps), 1)
                        dve.wait_ge(sem(g_steps), at(g_steps, g, GROUP))
                        dve.tensor_copy(tops_f[:, :, :], tops_i[:, :, 0:2]).then_inc(sem(g_steps), 1)

                    def gates(g):
                        done = [GROUP + 2]

                        def step(ins):
                            done[0] += 1
                            ins.then_inc(sem(g_steps), 1)

                        def after(n):
                            dve.wait_ge(sem(g_steps), at(g_steps, g, GROUP + 2 + n))
                        dve.wait_ge(sem(lead_s), at(lead_s, g, 1))
                        step(dve.tensor_scalar(firsts, leads_t, 1.0, quarter_g[:, layer:layer + 1], ALU.add, ALU.mult))
                        after(1)
                        step(dve.tensor_scalar(seconds, firsts, half_g[:, layer:layer + 1], -1.0, ALU.subtract, ALU.mult))
                        experts = iota8[:, :].unsqueeze(1).broadcast_to([P, GROUP, EXPERTS])
                        for n in range(2):
                            step(dve.tensor_tensor(picks[:, n, :, :], experts,
                                                   tops_f[:, :, n:n + 1].broadcast_to([P, GROUP, EXPERTS]), ALU.is_equal))
                        for n, weight in enumerate((firsts, seconds)):
                            after(3 + n)
                            step(dve.tensor_tensor(picks[:, n, :, :], picks[:, n, :, :],
                                                   weight.unsqueeze(2).broadcast_to([P, GROUP, EXPERTS]), ALU.mult))
                        after(6)
                        dve.tensor_tensor(gates_g[:, :, :], picks[:, 0, :, :], picks[:, 1, :, :], ALU.add)\
                            .then_inc(sem(gated), 1)

                    def add(g, e):
                        for t in range(GROUP):
                            dve.wait_ge(sem(down), at(down, g, 2 * e + t // 2 + 1))
                            if e == 0:
                                dve.wait_ge(sem(gated), at(gated, g, 1))
                            else:
                                dve.wait_ge(sem(added), at(added, g, GROUP * (e - 1) + t + 1))
                            dve.scalar_tensor_tensor(x_g[:, g, t, :], banks_y[t // 2][:, t % 2 * DIM:(t % 2 + 1) * DIM],
                                                     gates_g[:, t, e:e + 1], x_g[:, g, t, :], ALU.mult, ALU.add)\
                                .then_inc(sem(added), 1)

                    def group(g):
                        for u in range(n_units):
                            hidden(g, u)
                            if u == 0 and not first(g):
                                add(g - 1, EXPERTS - 1)
                            if u == 0:
                                gate_max(g)
                                gates(g)
                            for e in range(EXPERTS):
                                if last_unit[e] == u - 1:
                                    add(g, e)
                            if u == n_units - 6 and not last(g):
                                ln_stats_g(g + 1)
                            if u == n_units - 5 and not last(g):
                                ln_apply_g(g + 1)

                    ln_stats_g(0)
                    ln_apply_g(0)
                    over_tiles(dve, group, n=GROUPS)
                    add(GROUPS - 1, EXPERTS - 1)
            block_ends(GROUPS)

        router = sb("router", [P, 4, KC, EXPERTS])


        stage = sb("stage", [P, 2, 512])
        qn = sb("qn", [P, 2, 512])
        ssq = sb("ssq", [P, 32])
        ssq_e = sb("ssq_e", [P, 32])
        rnorm = sb("rnorm", [P, 32])
        qk_all = sb("qk_all", [P, 4096])
        qT = qk_all[:, 0:2048].rearrange("p (h t) -> p h t", h=16)
        kT = qk_all[:, 2048:4096].rearrange("p (h t) -> p h t", h=16)
        smax = sb("smax", [P, 4, 2, 8])
        E = sb("E", [P, 4, 8, SEQ])
        ssum = sb("ssum", [P, 4, 2, 8])
        srec = sb("srec", [P, 4, 2, 8])
        PT = sb("PT", [P, 4, 4, P])
        o_all = sb("o_all", [P, 2304])
        OT = o_all[:, 0:2048].rearrange("p (h t) -> p h t", h=16)
        gcol = sb("gcol", [P, 3])
        def group_view(off, *shape):
            n = 1
            for d in shape:
                n *= d
            ap = o_all[:, 1024 + off:1024 + off + n]
            if len(shape) == 2:
                return ap.rearrange("p (t a) -> p t a", t=shape[0])
            return ap
        lgs, tops, gates_g = (group_view(32 * n, GROUP, EXPERTS) for n in range(3))
        tops_i = o_all[:, 1120:1152].bitcast(U32).rearrange("p (t a) -> p t a", t=GROUP)
        picks = o_all[:, 1152:1216].rearrange("p (n t e) -> p n t e", n=2, t=GROUP)
        tops_f, mvs, sts = group_view(192, GROUP, 2), group_view(200, GROUP, 2), group_view(208, GROUP, 6)
        leads, leads_t, firsts, seconds, vars_g, rstds = (group_view(232 + 4 * n, GROUP) for n in range(6))

        def load_context(sp, i, s, turned):
            if not first(i):
                sp.wait_ge(sem(turned), at(turned, i, 0))
            sp.dma_start(c_tok[:, :], ctx_rows[i]).then_inc(sem(s["c"]), 16)

        def load_context_rows(sp, i, s, rows_used):
            if not first(i):
                sp.wait_ge(sem(rows_used), at(rows_used, i, 0))
            sp.dma_start(c_even[0:SEQ, :, :], ctx_by_row[i]).then_inc(sem(s["ce"]), 16)
            sp.dma_start(c_odd[SEQ:P, :, :], ctx_by_row[i]).then_inc(sem(s["co"]), 16)

        def load_contexts(sp, s, rows_used):
            def tile(i):
                if not is_last(i):
                    load_context(sp, i + 1, s, s["turned"])
                load_context_rows(sp, i, s, rows_used)
            load_context(sp, 0, s, s["turned"])
            over_tiles(sp, tile)

        def absorb_part(key, pairs, wq, wk, wv, wo, m_out, w2_out):
            S = counted
            jobs = 1 if wq is None else 2
            turned, copied, mul, kept = (S(n, jobs) for n in ("w_turned", "w_copied", "w_multiplied", "w_kept"))
            banks_w = (bank_t[0], bank_s[0])
            banks_wq = (bank_t[1], bank_s[1])
            banks_w2 = (bank_p[0], bank_o)
            banks_m = (bank_p[1], bank_y)
            wT, wqT = qn, stage

            with nc.Block() as block:
                @block.tensor
                def _(pe):
                    def turn(j):
                        if j >= 2:
                            pe.wait_ge(sem(copied), at(copied, j - 1, 0))
                        shared = wq is not None
                        for a, (w, h) in enumerate(((wk, j), (wv, j)) if shared else ((wv, 2 * j), (wv, 2 * j + 1))):
                            mm = pe.transpose(banks_w[j % 2][:, a * P:(a + 1) * P], w[:, h * P:(h + 1) * P], ident[:, :])
                        mm.then_inc(sem(turned), 1)
                        if shared:
                            for a in range(2):
                                for k in range(KC):
                                    h = 2 * j + a
                                    mm = pe.transpose(banks_wq[j % 2][:, (a * KC + k) * P:(a * KC + k + 1) * P],
                                                      wq[:, k, h * P:(h + 1) * P], ident[:, :])
                            mm.then_inc(sem(turned), 1)

                    def multiply(j):
                        pe.wait_ge(sem(copied), at(copied, j, jobs))
                        if j >= 2:
                            pe.wait_ge(sem(kept), at(kept, j - 1, 0))
                        for a in range(2):
                            v = 1 if wq is not None else a
                            mm = pe.matmul(banks_w2[j % 2][:, a * DIM:(a + 1) * DIM], wT[:, j % 2, v * P:(v + 1) * P],
                                           wo[:, 2 * j + a, :], start=True, stop=True)
                        mm.then_inc(sem(mul), 1)
                        if wq is not None:
                            for n in range(2 * KC):
                                mm = pe.matmul(banks_m[j % 2][:, n * P:(n + 1) * P], wqT[:, j % 2, n * P:(n + 1) * P],
                                               wT[:, j % 2, 0:P], start=True, stop=True)
                            mm.then_inc(sem(mul), 1)

                    pe.wait_ge(weights_in[key], w_count[key])
                    turn(0)
                    for j in range(pairs):
                        if j + 1 < pairs:
                            turn(j + 1)
                        multiply(j)

                @block.scalar
                def _(act):
                    for j in range(pairs):
                        act.wait_ge(sem(turned), at(turned, j, 1))
                        if j >= 2:
                            act.wait_ge(sem(mul), at(mul, j - 1, 0))
                        act.activation(wT[:, j % 2, 0:2 * P], banks_w[j % 2][:, 0:2 * P], ACT.Copy)\
                            .then_inc(sem(copied), 1)
                        if wq is not None:
                            act.wait_ge(sem(turned), at(turned, j, 2))
                            act.activation(wqT[:, j % 2, :], banks_wq[j % 2][:, :], ACT.Copy).then_inc(sem(copied), 1)

                @block.vector
                def _(dve):
                    for j in range(pairs):
                        dve.wait_ge(sem(mul), at(mul, j, 1))
                        dve.tensor_copy(w2_out[:, 2 * j:2 * j + 2, :],
                                        banks_w2[j % 2][:, :].rearrange("p (a d) -> p a d", a=2)).then_inc(sem(kept), 1)
                        if wq is not None:
                            dve.wait_ge(sem(mul), at(mul, j, 2))
                            dve.tensor_copy(m_out[:, :, 2 * j:2 * j + 2, :].rearrange("p k a c -> p a k c"),
                                            banks_m[j % 2][:, :].rearrange("p (a k c) -> p a k c", a=2, k=KC))\
                                .then_inc(sem(kept), 1)
            block_ends(pairs)

        def normed_attention(layer, key, wq, wk, w2, score_scale):
            jobs = 8
            s = ln_signals()
            S = counted
            s["c"], s["ce"], s["co"] = S("c_loaded", 16), S("c_even_loaded", 16), S("c_odd_loaded", 16)
            proj, sq, sqs, sqe, rn, normed, qk_turned, qkT = (S(n, jobs) for n in (
                "projected", "squared", "squares_summed", "norm_eps", "norm_ready", "qk_normed", "qk_turned", "qkT_ready"))
            scores, smx, sub, ex, sm, rec, probs, p_turned, pT = (S(n, 2) for n in (
                "scores_ready", "score_max", "scores_shifted", "exp_ready", "exp_sum", "sum_inverse", "probs_ready",
                "probs_turned", "probsT_ready"))
            pv, oT = S("pv_ready", 4), S("pvT_copied", 4)
            y, added = S("y_ready", 1), S("y_added", 1)
            banks_o = [bank_o, bank_s[0], bank_o, bank_s[1]]

            with nc.Block() as block:
                @block.sync
                def _(sp):
                    load_contexts(sp, s, pv)

                @block.tensor
                def _(pe):
                    def turn_x(i):
                        pe_turn_x(pe, s, i, bank_t[0], c_in=lambda: pe.wait_ge(sem(s["c"]), at(s["c"], i, 16)),
                                  bank_free=None if first(i) else
                                  (lambda: pe.wait_ge(sem(qkT), at(qkT, i, -1))))

                    def project(i, j):
                        if j == 0:
                            pe.wait_ge(sem(s["xT"]), at(s["xT"], i, 1))
                        cols = slice(j // 2 * 512, (j // 2 + 1) * 512)
                        if j % 2 == 0:
                            for k in range(KC):
                                mm = pe.matmul(bank_p[0][:, :], xcT[:, k, :], wq[:, k, cols], start=(k == 0),
                                               stop=(k == KC - 1))
                        else:
                            mm = pe.matmul(bank_p[1][:, :], xcT[:, 2, :], wk[:, cols], start=True, stop=True)
                        mm.then_inc(sem(proj), 1)

                    def turn(i, j):
                        pe.wait_ge(sem(normed), at(normed, i, j + 1))
                        if j >= 2:
                            pe.wait_ge(sem(qkT), at(qkT, i, j - 1))
                        for h in range(4):
                            mm = pe.transpose(bank_t[j % 2][:, h * P:(h + 1) * P], qn[:, j % 2, h * P:(h + 1) * P],
                                              ident[:, :])
                        mm.then_inc(sem(qk_turned), 1)

                    def score(i, g):
                        pe.wait_ge(sem(qkT), at(qkT, i, 4 * g + 4))
                        for h in range(8):
                            for b in range(2):
                                rows = slice(b * SEQ, (b + 1) * SEQ)
                                mm = pe.matmul(bank_s[g][rows, h * SEQ:(h + 1) * SEQ], qT[:, 8 * g + h, rows],
                                               kT[:, 8 * g + h, rows], start=True, stop=True)
                        mm.then_inc(sem(scores), 1)

                    def turn_probs(i, g):
                        pe.wait_ge(sem(probs), at(probs, i, g + 1))
                        for a in range(4):
                            mm = pe.transpose(bank_s[g][:, a * P:(a + 1) * P],
                                              E[:, g, 2 * a:2 * a + 2, :].rearrange("p a b -> p (a b)"), ident[:, :])
                        mm.then_inc(sem(p_turned), 1)

                    def values(i, g, b):
                        if b == 0:
                            pe.wait_ge(sem(pT), at(pT, i, g + 1))
                        if g == 0 and b == 0:
                            pe.wait_ge(sem(s["ce"]), at(s["ce"], i, 16))
                            pe.wait_ge(sem(s["co"]), at(s["co"], i, 16))
                        for a, c in enumerate((c_even, c_odd)):
                            mm = pe.matmul(banks_o[2 * g + b][:, a * 256:(a + 1) * 256], c[:, b, :],
                                           PT[:, g, :, b * SEQ:(b + 1) * SEQ], start=True, stop=True)
                        mm.then_inc(sem(pv), 1)

                    def sum_heads(i, q):
                        if q == 0 and not first(i):
                            pe.wait_ge(sem(added), at(added, i, 0))
                        if q % 2 == 0:
                            pe.wait_ge(sem(oT), at(oT, i, q + 2))
                        for h in range(4 * q, 4 * q + 4):
                            mm = pe.matmul(bank_y[:, 0:DIM], OT[:, h, :], w2[:, h, :], start=(h == 0), stop=(h == 15))
                        if q == 3:
                            mm.then_inc(sem(y), 1)

                    def tile(i):
                        project(i, 0)
                        project(i, 1)
                        if not first(i):
                            sum_heads(i - 1, 0)
                            sum_heads(i - 1, 1)
                        turn(i, 0)
                        project(i, 2)
                        turn(i, 1)
                        project(i, 3)
                        turn(i, 2)
                        project(i, 4)
                        if not first(i):
                            turn_probs(i - 1, 1)
                        turn(i, 3)
                        project(i, 5)
                        if not first(i):
                            values(i - 1, 1, 0)
                        score(i, 0)
                        if not first(i):
                            values(i - 1, 1, 1)
                        turn(i, 4)
                        project(i, 6)
                        turn(i, 5)
                        project(i, 7)
                        if not first(i):
                            sum_heads(i - 1, 2)
                        turn_probs(i, 0)
                        if not first(i):
                            sum_heads(i - 1, 3)
                        turn(i, 6)
                        turn(i, 7)
                        if not is_last(i):
                            turn_x(i + 1)
                        values(i, 0, 0)
                        values(i, 0, 1)
                        score(i, 1)

                    turn_x(0)
                    over_tiles(pe, tile)
                    sum_heads(TILES - 1, 0)
                    sum_heads(TILES - 1, 1)
                    turn_probs(TILES - 1, 1)
                    values(TILES - 1, 1, 0)
                    values(TILES - 1, 1, 1)
                    sum_heads(TILES - 1, 2)
                    sum_heads(TILES - 1, 3)

                @block.scalar
                def _(act):
                    load_next(act, key)

                    def copy_x(i):
                        act.wait_ge(sem(s["turned"]), at(s["turned"], i, 1))
                        if not first(i):
                            act.wait_ge(sem(proj), at(proj, i, 0))
                        act.activation(xcT[:, :, :], bank_t[0][:, 0:3 * P].rearrange("p (a b) -> p a b", b=P),
                                       ACT.Copy).then_inc(sem(s["xT"]), 1)

                    def square(i, j):
                        act.wait_ge(sem(proj), at(proj, i, j + 1))
                        if not (first(i) and j < 2):
                            act.wait_ge(sem(sqs), at(sqs, i, j - 1))
                        act.activation(stage[:, j % 2, :], bank_p[j % 2][:, :], ACT.Square).then_inc(sem(sq), 1)

                    def copy_qk(i, j):
                        act.wait_ge(sem(qk_turned), at(qk_turned, i, j + 1))
                        src = bank_t[j % 2][:, :].rearrange("p (h t) -> p h t", h=4)
                        heads = slice(j // 2 * 4, j // 2 * 4 + 4)
                        if j % 2 == 0:
                            act.activation(qT[:, heads, :], src, ACT.Copy).then_inc(sem(qkT), 1)
                        else:
                            act.activation(kT[:, heads, :], src, ACT.Copy, scale=gcol[:, 2:3]).then_inc(sem(qkT), 1)

                    def exps(i, g):
                        act.wait_ge(sem(sub), at(sub, i, g + 1))
                        act.activation(E[:, g, :, :], E[:, g, :, :], ACT.Exp, scale=score_scale).then_inc(sem(ex), 1)

                    def copy_probs(i, g):
                        act.wait_ge(sem(p_turned), at(p_turned, i, g + 1))
                        act.activation(PT[:, g, :, :], bank_s[g][:, :].rearrange("p (a t) -> p a t", a=4), ACT.Copy)\
                            .then_inc(sem(pT), 1)

                    def tile(i):
                        square(i, 0)
                        square(i, 1)
                        if not first(i):
                            exps(i - 1, 1)
                        copy_qk(i, 0)
                        square(i, 2)
                        copy_qk(i, 1)
                        square(i, 3)
                        copy_qk(i, 2)
                        square(i, 4)
                        if not first(i):
                            copy_probs(i - 1, 1)
                        copy_qk(i, 3)
                        square(i, 5)
                        exps(i, 0)
                        for j in range(4, 6):
                            copy_qk(i, j)
                            square(i, j + 2)
                        copy_probs(i, 0)
                        copy_qk(i, 6)
                        copy_qk(i, 7)
                        if not is_last(i):
                            copy_x(i + 1)

                    copy_x(0)
                    over_tiles(act, tile)
                    exps(TILES - 1, 1)
                    copy_probs(TILES - 1, 1)

                @block.gpsimd
                def _(pool):
                    def tile(i):
                        for j in range(jobs):
                            c = slice(4 * j, 4 * j + 4)
                            pool.wait_ge(sem(sqs), at(sqs, i, j + 1))
                            pool.tensor_tensor(ssq_e[:, c], ssq[:, c], rms_eps[:, 0:4], ALU.add).then_inc(sem(sqe), 1)
                            pool.wait_ge(sem(sqe), at(sqe, i, j + 1))
                            pool.tensor_tensor(rnorm[:, c], ssq_e[:, c], minus_half[:, 0:4], ALU.pow).then_inc(sem(rn), 1)
                            if j == 1 and not is_last(i):
                                pool_rstd(pool, s, i + 1)
                    pool_rstd(pool, s, 0)
                    over_tiles(pool, tile)

                @block.vector
                def _(dve):
                    def sum_squares(i, j):
                        dve.wait_ge(sem(sq), at(sq, i, j + 1))
                        if not first(i):
                            dve.wait_ge(sem(normed), at(normed, i, j))
                        dve.tensor_reduce(ssq[:, 4 * j:4 * j + 4], stage[:, j % 2, :].rearrange("p (h d) -> p h d", h=4),
                                          AX, ALU.add).then_inc(sem(sqs), 1)

                    def norm(i, j):
                        dve.wait_ge(sem(rn), at(rn, i, j + 1))
                        if j >= 2:
                            dve.wait_ge(sem(qk_turned), at(qk_turned, i, j - 1))
                        dve.tensor_tensor(qn[:, j % 2, :].rearrange("p (h d) -> p h d", h=4),
                                          bank_p[j % 2][:, :].rearrange("p (h d) -> p h d", h=4),
                                          rnorm[:, 4 * j:4 * j + 4].unsqueeze(2).broadcast_to([P, 4, P]), ALU.mult)\
                            .then_inc(sem(normed), 1)

                    def shift(i, g):
                        dve.wait_ge(sem(scores), at(scores, i, g + 1))
                        src = bank_s[g][:, :].rearrange("p (h k) -> p h k", h=8)
                        dve.tensor_reduce(smax[:, g, 0, :], src, AX, ALU.max).then_inc(sem(smx), 1)
                        dve.wait_ge(sem(smx), at(smx, i, g + 1))
                        dve.tensor_tensor(E[:, g, :, :], src, smax[:, g, 0, :].unsqueeze(2).broadcast_to([P, 8, SEQ]),
                                          ALU.subtract).then_inc(sem(sub), 1)

                    def weigh(i, g):
                        dve.wait_ge(sem(ex), at(ex, i, g + 1))
                        dve.tensor_reduce(ssum[:, g, 0, :], E[:, g, :, :], AX, ALU.add).then_inc(sem(sm), 1)
                        dve.wait_ge(sem(sm), at(sm, i, g + 1))
                        dve.reciprocal(srec[:, g, 0, :], ssum[:, g, 0, :]).then_inc(sem(rec), 1)
                        dve.wait_ge(sem(rec), at(rec, i, g + 1))
                        dve.tensor_tensor(E[:, g, :, :], E[:, g, :, :],
                                          srec[:, g, 0, :].unsqueeze(2).broadcast_to([P, 8, SEQ]), ALU.mult)\
                            .then_inc(sem(probs), 1)

                    def copy_pv(i, g, b):
                        n = 2 * g + b
                        dve.wait_ge(sem(pv), at(pv, i, n + 1))
                        for a in range(2):
                            ins = dve.tensor_copy(OT[:, 8 * g + a:8 * g + 8:2, b * SEQ:(b + 1) * SEQ],
                                                  banks_o[n][:, a * 256:(a + 1) * 256].rearrange("p (h t) -> p h t", h=4))
                        ins.then_inc(sem(oT), 1)

                    def add(i):
                        dve.wait_ge(sem(y), at(y, i, 1))
                        dve.scalar_tensor_tensor(x[:, i, :], bank_y[:, 0:DIM], tanh_g[:, layer:layer + 1], x[:, i, :],
                                                 ALU.mult, ALU.add).then_inc(sem(added), 1)

                    def tile(i):
                        sum_squares(i, 0)
                        if not first(i):
                            shift(i - 1, 1)
                        norm(i, 0)
                        sum_squares(i, 1)
                        if not is_last(i):
                            ln_stats(dve, s, i + 1)
                        norm(i, 1)
                        sum_squares(i, 2)
                        if not is_last(i):
                            ln_apply(dve, s, i + 1)
                        norm(i, 2)
                        sum_squares(i, 3)
                        if not first(i):
                            weigh(i - 1, 1)
                        norm(i, 3)
                        sum_squares(i, 4)
                        if not first(i):
                            copy_pv(i - 1, 1, 0)
                        norm(i, 4)
                        sum_squares(i, 5)
                        shift(i, 0)
                        norm(i, 5)
                        if not first(i):
                            copy_pv(i - 1, 1, 1)
                        sum_squares(i, 6)
                        weigh(i, 0)
                        norm(i, 6)
                        sum_squares(i, 7)
                        norm(i, 7)
                        if not first(i):
                            add(i - 1)
                        copy_pv(i, 0, 0)
                        copy_pv(i, 0, 1)

                    dve_layernorm(dve, s, 0)
                    over_tiles(dve, tile)
                    shift(TILES - 1, 1)
                    weigh(TILES - 1, 1)
                    copy_pv(TILES - 1, 1, 0)
                    copy_pv(TILES - 1, 1, 1)
                    add(TILES - 1)
            block_ends()

        def masked_attention(layer, key, m, w2, score_scale):
            jobs = 4
            s = ln_signals()
            S = counted
            s["c"], s["ce"], s["co"] = S("c_loaded", 16), S("c_even_loaded", 16), S("c_odd_loaded", 16)
            proj = S("projected", jobs)
            qkT = S("qkT_ready", jobs)
            scores = S("scores_ready", 2)
            masked, recv = (S(n, 2) for n in ("scores_masked", "sum_inverse_valid"))
            smx, sub, ex, sm, rec, probs = (S(n, 2) for n in (
                "score_max", "scores_shifted", "exp_ready", "exp_sum", "sum_inverse", "probs_ready"))
            p_turned = S("probs_turned", 2)
            pT = S("probsT_ready", 2)
            pv = S("pv_ready", 4)
            oT = S("pvT_copied", 4)
            y = S("y_ready", 1)
            added = S("y_added", 1)
            banks_o = [bank_o, bank_p[1], bank_t[0], bank_t[1]]

            with nc.Block() as block:
                @block.sync
                def _(sp):
                    load_contexts(sp, s, pv)

                @block.tensor
                def _(pe):
                    def turn_x(i):
                        pe_turn_x(pe, s, i, bank_p[0], c_in=lambda: pe.wait_ge(sem(s["c"]), at(s["c"], i, 16)),
                                  bank_free=None if first(i) else
                                  (lambda: pe.wait_ge(sem(qkT), at(qkT, i - 1, 3))))

                    def project(i, j):
                        if j >= 2:
                            pe.wait_ge(sem(qkT), at(qkT, i, j - 1))
                        for h in range(4):
                            for k in range(KC):
                                mm = pe.matmul(bank_p[j % 2][:, h * P:(h + 1) * P], m[:, k, 4 * j + h, :],
                                               xcT[:, k, :], start=(k == 0), stop=(k == KC - 1))
                        mm.then_inc(sem(proj), 1)

                    def score(i, g):
                        pe.wait_ge(sem(qkT), at(qkT, i, 2 * g + 2))
                        if not first(i):
                            pe.wait_ge(sem(sub), at(sub, i - 1, g + 1))
                        for h in range(8):
                            for b in range(2):
                                rows = slice(b * SEQ, (b + 1) * SEQ)
                                mm = pe.matmul(bank_s[g][rows, h * SEQ:(h + 1) * SEQ], qT[:, 8 * g + h, rows],
                                               xcT[:, 2, rows], start=True, stop=True)
                        mm.then_inc(sem(scores), 1)

                    def front(i):
                        pe.wait_ge(sem(s["xT"]), at(s["xT"], i, 1))
                        for j in range(jobs):
                            project(i, j)
                            if j == 2:
                                score(i, 0)

                    def values(i, g, b):
                        if b == 0:
                            pe.wait_ge(sem(pT), at(pT, i, g + 1))
                        n = 2 * g + b
                        if n == 0:
                            pe.wait_ge(sem(s["ce"]), at(s["ce"], i, 16))
                            pe.wait_ge(sem(s["co"]), at(s["co"], i, 16))
                        for a, c in enumerate((c_even, c_odd)):
                            mm = pe.matmul(banks_o[n][:, a * 256:(a + 1) * 256], c[:, b, :],
                                           PT[:, g, :, b * SEQ:(b + 1) * SEQ], start=True, stop=True)
                        mm.then_inc(sem(pv), 1)

                    def turn_probs(i):
                        for g in range(2):
                            pe.wait_ge(sem(probs), at(probs, i, g + 1))
                            for a in range(4):
                                mm = pe.transpose(bank_t[g][:, a * P:(a + 1) * P],
                                                  E[:, g, 2 * a:2 * a + 2, :].rearrange("p a b -> p (a b)"), ident[:, :])
                            mm.then_inc(sem(p_turned), 1)

                    def back(i):
                        for g in range(2):
                            for b in range(2):
                                values(i, g, b)
                        for g in range(2):
                            pe.wait_ge(sem(oT), at(oT, i, 2 * g + 2))
                            if g == 0 and not first(i):
                                pe.wait_ge(sem(added), at(added, i, 0))
                            for h in range(8):
                                mm = pe.matmul(bank_y[:, 0:DIM], OT[:, 8 * g + h, :], w2[:, 8 * g + h, :],
                                               start=(g == 0 and h == 0), stop=(g == 1 and h == 7))
                        mm.then_inc(sem(y), 1)

                    def tile(i):
                        front(i)
                        if not first(i):
                            turn_probs(i - 1)
                        score(i, 1)
                        if not is_last(i):
                            turn_x(i + 1)
                        if not first(i):
                            back(i - 1)

                    turn_x(0)
                    over_tiles(pe, tile)
                    turn_probs(TILES - 1)
                    back(TILES - 1)

                @block.scalar
                def _(act):
                    load_next(act, key)

                    def copy_x(i):
                        act.wait_ge(sem(s["turned"]), at(s["turned"], i, 1))
                        if not first(i):
                            act.wait_ge(sem(scores), at(scores, i, 0))
                        act.activation(xcT[:, :, :], bank_p[0][:, 0:3 * P].rearrange("p (a b) -> p a b", b=P),
                                       ACT.Copy).then_inc(sem(s["xT"]), 1)

                    def copy_q(i, j):
                        act.wait_ge(sem(proj), at(proj, i, j + 1))
                        if j == 0 and not first(i):
                            act.wait_ge(sem(scores), at(scores, i, 0))
                        act.activation(qT[:, 4 * j:4 * j + 4, :], bank_p[j % 2][:, :].rearrange("p (h t) -> p h t", h=4),
                                       ACT.Copy).then_inc(sem(qkT), 1)

                    def copy_probs(i):
                        for g in range(2):
                            act.wait_ge(sem(p_turned), at(p_turned, i, g + 1))
                            act.activation(PT[:, g, :, :], bank_t[g][:, :].rearrange("p (a t) -> p a t", a=4), ACT.Copy)\
                                .then_inc(sem(pT), 1)

                    def exps(i):
                        for g in range(2):
                            act.wait_ge(sem(sub), at(sub, i, g + 1))
                            act.activation(E[:, g, :, :], E[:, g, :, :], ACT.Exp, scale=score_scale).then_inc(sem(ex), 1)

                    def tile(i):
                        for j in range(jobs):
                            copy_q(i, j)
                        if not first(i):
                            copy_probs(i - 1)
                        if not is_last(i):
                            copy_x(i + 1)
                        exps(i)

                    copy_x(0)
                    over_tiles(act, tile)
                    copy_probs(TILES - 1)

                @block.gpsimd
                def _(pool):
                    def tile(i):
                        if not within(i, 2):
                            pool_rstd(pool, s, i + 2)
                    pool_rstd(pool, s, 0)
                    pool_rstd(pool, s, 1)
                    over_tiles(pool, tile, tail=2)

                @block.vector
                def _(dve):
                    def shift(i, g):
                        dve.wait_ge(sem(scores), at(scores, i, g + 1))
                        if not first(i):
                            dve.wait_ge(sem(p_turned), at(p_turned, i - 1, g + 1))
                        src = E[:, g, :, :]
                        dve.tensor_tensor(src, bank_s[g][:, :].rearrange("p (h k) -> p h k", h=8),
                                          mask_add[:, i, :].unsqueeze(1).broadcast_to([P, 8, SEQ]), ALU.add)\
                            .then_inc(sem(masked), 1)
                        dve.wait_ge(sem(masked), at(masked, i, g + 1))
                        dve.tensor_reduce(smax[:, g, 0, :], src, AX, ALU.max).then_inc(sem(smx), 1)
                        dve.wait_ge(sem(smx), at(smx, i, g + 1))
                        dve.tensor_tensor(E[:, g, :, :], src, smax[:, g, 0, :].unsqueeze(2).broadcast_to([P, 8, SEQ]),
                                          ALU.subtract).then_inc(sem(sub), 1)

                    def weigh(i, g):
                        dve.wait_ge(sem(ex), at(ex, i, g + 1))
                        dve.tensor_reduce(ssum[:, g, 0, :], E[:, g, :, :], AX, ALU.add).then_inc(sem(sm), 1)
                        dve.wait_ge(sem(sm), at(sm, i, g + 1))
                        dve.reciprocal(srec[:, g, 0, :], ssum[:, g, 0, :]).then_inc(sem(rec), 1)
                        dve.wait_ge(sem(rec), at(rec, i, g + 1))
                        dve.tensor_tensor(srec[:, g, 0, :], srec[:, g, 0, :], mask_any[:, i, :].broadcast_to([P, 8]),
                                          ALU.mult).then_inc(sem(recv), 1)
                        dve.wait_ge(sem(recv), at(recv, i, g + 1))
                        dve.tensor_tensor(E[:, g, :, :], E[:, g, :, :],
                                          srec[:, g, 0, :].unsqueeze(2).broadcast_to([P, 8, SEQ]), ALU.mult)\
                            .then_inc(sem(probs), 1)

                    def copy_pv(i, n):
                        g, b = n // 2, n % 2
                        dve.wait_ge(sem(pv), at(pv, i, n + 1))
                        if n == 0 and not first(i):
                            dve.wait_ge(sem(y), at(y, i, 0))
                        for a in range(2):
                            ins = dve.tensor_copy(OT[:, 8 * g + a:8 * g + 8:2, b * SEQ:(b + 1) * SEQ],
                                                  banks_o[n][:, a * 256:(a + 1) * 256].rearrange("p (h t) -> p h t", h=4))
                        ins.then_inc(sem(oT), 1)

                    def add(i):
                        dve.wait_ge(sem(y), at(y, i, 1))
                        dve.scalar_tensor_tensor(x[:, i, :], bank_y[:, 0:DIM], tanh_g[:, layer:layer + 1], x[:, i, :],
                                                 ALU.mult, ALU.add).then_inc(sem(added), 1)

                    def tile(i):
                        if not within(i, 2):
                            ln_stats(dve, s, i + 2)
                        shift(i, 0)
                        if not first(i):
                            copy_pv(i - 1, 0)
                            copy_pv(i - 1, 1)
                        shift(i, 1)
                        if not within(i, 2):
                            ln_apply(dve, s, i + 2)
                        if not first(i):
                            copy_pv(i - 1, 2)
                            copy_pv(i - 1, 3)
                        weigh(i, 0)
                        weigh(i, 1)
                        if not first(i):
                            add(i - 1)

                    dve_layernorm(dve, s, 0)
                    dve_layernorm(dve, s, 1)
                    over_tiles(dve, tile, tail=2)
                    for n in range(4):
                        copy_pv(TILES - 1, n)
                    add(TILES - 1)
            block_ends()

        mask_add = sb("mask_add", [P, TILES, SEQ])
        mask_u8 = sb("mask_u8", [P, TILES, SEQ], U8)
        mask_any = sb("mask_any", [P, TILES, 1])

        def run_l1x():
            wq, wk, wv = aw(0, KC, 2048), aw(4096, 2048), aw(6144, 2048)
            wo, w2 = aw(8192, 16, DIM), aw(12288, 16, DIM)
            scaled = ctx.enter_context(nc.semaphore("l1_gain"))
            with nc.Block() as block:
                @block.vector
                def _(dve):
                    dve.wait_ge(weights_in["l1x"], w_count["l1x"])
                    dve.tensor_tensor(gcol[:, 2:3], gcol[:, 0:1], gcol[:, 1:2], ALU.mult).then_inc(scaled, 1)
            absorb_part("l1x", 8, None, None, wv, wo, None, w2)
            normed_attention(1, "l1x", wq, wk, w2, float(P) ** 0.5)

        def run_l3x():
            wq, wk, wv = aw(0, KC, 2048), aw(4096, 1024), aw(5120, 1024)
            wo, m, w2 = aw(6144, 16, DIM), aw(10240, KC * 16, P), aw(14336, 16, DIM)
            m = m.rearrange("p (k h) c -> p k h c", k=KC)
            made = ctx.enter_context(nc.semaphore("mask_made"))
            with nc.Block() as block:
                @block.vector
                def _(dve):
                    dve.wait_ge(weights_in["l3x"], w_count["l3x"])
                    dve.tensor_copy(mask_add[:, :, :], mask_u8[:, :, :]).then_inc(made, 1)
                    dve.wait_ge(made, 1)
                    dve.tensor_reduce(mask_any[:, :, 0], mask_add[:, :, :], AX, ALU.max).then_inc(made, 1)
                    dve.wait_ge(made, 2)
                    dve.tensor_scalar(mask_add[:, :, :], mask_add[:, :, :], 1.0, 1e30, ALU.subtract, ALU.mult)\
                        .then_inc(made, 1)
            absorb_part("l3x", 8, wq, wk, wv, wo, m, w2)
            masked_attention(3, "l3x", m, w2, float(P) ** -0.5)

        head_mask = sb("head_mask", [P, 16])
        pair_mask = sb("pair_mask", [P, DIM])
        qkT_n = o_all[:, 0:512].rearrange("p (a t) -> p a t", a=4)
        v_pairs = o_all[:, 512:1024].rearrange("p (b d) -> p b d", b=2)
        o_sb = o_all[:, 1024:1280]
        oT_n = o_all[:, 1280:1536].rearrange("p (k t) -> p k t", k=KC)
        c_parts = o_all[:, 1536:2304].rearrange("p (n k r t) -> p n k r t", n=2, k=3, r=2)
        key_side = sb("key_side", [2, 2, SEQ])
        kv_bias = attn_w[0:2, 2048:2560].rearrange("p (n d) -> p n d", n=2)
        row_bias = attn_w[0:1, 2560:2816]
        out_bias = attn_w[0:1, 2816:3072]
        norm_rows = attn_w[0:6, 3072:3200]
        norm_cols = sb("norm_cols", [P, 6])
        mean_n = sb("mean_n", [P, 2, 32])
        ropes = sb("ropes", [P, TILES, 16])
        ropes_w = attn_w[:, 4096:4352].rearrange("p (n a) -> p n a", n=4)
        ropes_i = attn_w[:, 4352:4416].bitcast(I32)
        pos = sb("pos", [P, TILES, 2])

        def narrow_attention(layer, key, hd, wq, wo, k_weights, v_weights, keys_main):
            split = keys_main < SEQ
            heads = DIM // hd
            in_half = P // hd
            chunks = heads // 8
            segs = [(0, keys_main), (keys_main, SEQ)] if split else [(0, SEQ)]
            score_scale = float(hd) ** -0.5
            kb = qk_all[:, 0:2 * 2 * in_half * SEQ].rearrange("p (f b h t) -> p f b h t", f=2, b=2, h=in_half)
            s = ln_signals()
            S = counted
            s["c"] = S("c_loaded", 16)
            c_split = S("context_split", 2 * len(segs))
            qk = S("qk_projected", 1)
            v = S("v_projected", 1)
            v_in = S("v_spread", 1)
            steps = S("qk_steps", 4 if split else 3)
            sqr, sqe, rn = (S(n, 1 if split else 0) for n in ("squared", "norm_eps", "norm_ready"))
            normed = S("qk_normed", 1)
            qk_turned = S("qk_turned", 1)
            qkT = S("qkT_ready", 3 if split else 1)
            spread = [S("keys_spread_low", 2), S("keys_spread_high", 2)]
            scores = S("scores_ready", chunks)
            nseg = len(segs)
            smx, sub = (S(n, chunks * nseg) for n in ("score_max", "scores_shifted"))
            ex = S("exp_ready", chunks)
            sm, probs = (S(n, chunks * nseg if split else m) for n, m in (("exp_sum", 1), ("probs_ready", 0)))
            rec = S("sum_inverse", chunks if split else 1)
            p_turned = S("probs_turned", chunks)
            pT = S("probsT_ready", chunks)
            pv = S("pv_ready", 1)
            o_in = S("pv_copied", 1)
            o_turned = S("pv_turned", 1)
            oT = S("pvT_ready", 1)
            y = S("y_ready", 1)
            added = S("y_added", 1)

            def spread_keys(eng, i, f):
                eng.wait_ge(sem(qkT), at(qkT, i, per(qkT)))
                if not first(i):
                    eng.wait_ge(sem(scores), at(scores, i, 0))
                for b in range(2):
                    eng.tensor_tensor(
                        kb[:, f, b, :, :],
                        qkT_n[:, 2 + f, b * SEQ:(b + 1) * SEQ].unsqueeze(1).broadcast_to([P, in_half, SEQ]),
                        head_mask[:, 0:in_half].unsqueeze(2).broadcast_to([P, in_half, SEQ]), ALU.mult)\
                        .then_inc(sem(spread[f]), 1)

            with nc.Block() as block:
                @block.sync
                def _(sp):
                    over_tiles(sp, lambda i: load_context(sp, i, s, s["turned"]))

                @block.tensor
                def _(pe):
                    def keys_of(part, b=None):
                        return c_parts[:, part, 0 if b is None else 1 + b, :, :].rearrange("p r t -> p (r t)")

                    def turn_x(i, o_before=False):
                        pe_turn_x(pe, s, i, bank_t[0], c_in=lambda: pe.wait_ge(sem(s["c"]), at(s["c"], i, 16)),
                                  bank_free=(lambda: pe.wait_ge(sem(oT), at(oT, i - 3, 1))) if o_before else None)

                    def project_qk(i):
                        pe.wait_ge(sem(s["xT"]), at(s["xT"], i, 1))
                        for k in range(KC):
                            pe.matmul(bank_p[0][:, 0:DIM], xcT[:, k, :], wq[:, k, :], start=(k == 0),
                                      stop=(not split and k == KC - 1))
                        if split:
                            pe.matmul(bank_p[0][:, 0:DIM], ones[0:1, :], row_bias[:, :], start=False, stop=True)
                        pe.wait_ge(sem(c_split), at(c_split, i, per(c_split)))
                        for n, w in enumerate(k_weights):
                            mm = pe.matmul(bank_p[0][:, DIM:2 * DIM], keys_of(n), w, start=(n == 0),
                                           stop=(not split and n == len(k_weights) - 1))
                        if split:
                            mm = pe.matmul(bank_p[0][:, DIM:2 * DIM], key_side[:, :, :], kv_bias[:, 0, :],
                                           start=False, stop=True)
                        mm.then_inc(sem(qk), 1)

                    def project_v(i):
                        if not first(i):
                            pe.wait_ge(sem(v_in), at(v_in, i, 0))
                        for b in range(2):
                            o = bank_p[1][:, b * DIM:(b + 1) * DIM]
                            for n, w in enumerate(v_weights):
                                mm = pe.matmul(o, keys_of(n, b), w, start=(n == 0),
                                               stop=(not split and n == len(v_weights) - 1))
                            if split:
                                mm = pe.matmul(o, key_side[:, :, :], kv_bias[:, 1, :], start=False, stop=True)
                        mm.then_inc(sem(v), 1)

                    def turn_qk(i):
                        pe.wait_ge(sem(normed), at(normed, i, 1))
                        for a in range(4):
                            mm = pe.transpose(bank_t[1][:, a * P:(a + 1) * P], qn[:, 0, a * P:(a + 1) * P], ident[:, :])
                        mm.then_inc(sem(qk_turned), 1)

                    def score(i):
                        for g in range(chunks):
                            f, h0 = g * 8 // in_half, g * 8 % in_half
                            pe.wait_ge(sem(spread[f]), at(spread[f], i, 2))
                            if g >= 2:
                                pe.wait_ge(sem(sub), at(sub, i, nseg * (g - 1)))
                            for b in range(2):
                                rows = slice(b * SEQ, (b + 1) * SEQ)
                                mm = pe.matmul(bank_s[g % 2][rows, :], qkT_n[:, f, rows], kb[:, f, b, h0:h0 + 8, :],
                                               start=True, stop=True)
                            mm.then_inc(sem(scores), 1)

                    def turn_probs(i, g):
                        if split:
                            pe.wait_ge(sem(probs), at(probs, i, nseg * (g + 1)))
                        else:
                            pe.wait_ge(sem(ex), at(ex, i, g + 1))
                        if g >= 2:
                            pe.wait_ge(sem(pT), at(pT, i, g - 1))
                        else:
                            pe.wait_ge(sem(sub), at(sub, i, nseg * (chunks - 1 + g)))
                        for a in range(4):
                            mm = pe.transpose(bank_s[g % 2][:, a * P:(a + 1) * P],
                                              E[:, g, 2 * a:2 * a + 2, :].rearrange("p a b -> p (a b)"), ident[:, :])
                        mm.then_inc(sem(p_turned), 1)

                    def weigh_values(i, g):
                        pe.wait_ge(sem(pT), at(pT, i, g + 1))
                        if g == 0:
                            pe.wait_ge(sem(v_in), at(v_in, i, 1))
                        for a in range(4):
                            c = slice((8 * g + 2 * a) * hd, (8 * g + 2 * a + 2) * hd)
                            for b in range(2):
                                rows = slice(b * SEQ, (b + 1) * SEQ)
                                mm = pe.matmul(bank_o[rows, c], PT[:, g, a, rows], v_pairs[:, b, c],
                                               start=True, stop=True)
                        if g == chunks - 1:
                            mm.then_inc(sem(pv), 1)

                    def values(i):
                        for g in range(chunks):
                            weigh_values(i, g)

                    def turn_o(i):
                        pe.wait_ge(sem(o_in), at(o_in, i, 1))
                        for k in range(KC):
                            mm = pe.transpose(bank_t[0][:, k * P:(k + 1) * P], o_sb[:, k * P:(k + 1) * P], ident[:, :])
                        mm.then_inc(sem(o_turned), 1)

                    def project_o(i):
                        pe.wait_ge(sem(oT), at(oT, i, 1))
                        if not first(i):
                            pe.wait_ge(sem(added), at(added, i, 0))
                        for k in range(KC):
                            pe.matmul(bank_y[:, 0:DIM], oT_n[:, k, :], wo[:, k, :], start=(k == 0), stop=False)
                        pe.matmul(bank_y[:, 0:DIM], ones[0:1, :], out_bias[:, :], start=False, stop=True)\
                            .then_inc(sem(y), 1)

                    def tile(i):
                        if not first(i):
                            values(i - 1)
                        score(i)
                        if not first(i):
                            turn_o(i - 1)
                        if not within(i, 1):
                            project_v(i + 1)
                            turn_qk(i + 1)
                        if not within(i, 2):
                            turn_x(i + 2, o_before=not first(i))
                        if not first(i):
                            project_o(i - 1)
                        if not within(i, 2):
                            project_qk(i + 2)
                        for g in range(chunks):
                            turn_probs(i, g)

                    turn_x(0)
                    project_qk(0)
                    project_v(0)
                    turn_x(1)
                    turn_qk(0)
                    project_qk(1)
                    over_tiles(pe, tile, tail=3)
                    values(TILES - 1)
                    turn_o(TILES - 1)
                    project_o(TILES - 1)

                @block.scalar
                def _(act):
                    load_next(act, key)

                    def front(i):
                        act.wait_ge(sem(s["turned"]), at(s["turned"], i, 1))
                        if not first(i):
                            act.wait_ge(sem(v), at(v, i, 0))
                        act.activation(xcT[:, :, :], bank_t[0][:, 0:3 * P].rearrange("p (a b) -> p a b", b=P),
                                       ACT.Copy).then_inc(sem(s["xT"]), 1)
                        src = bank_t[0][:, 2 * P:3 * P].rearrange("p (b t) -> p b t", b=2)
                        for n, (a, e) in enumerate(segs):
                            act.activation(c_parts[:, n, 0, :, a:e], src[:, :, a:e], ACT.Copy).then_inc(sem(c_split), 1)
                            act.activation(c_parts[:, n, 1:3, :, a:e],
                                           src[:, :, a:e].unsqueeze(2).broadcast_to([P, 2, 2, e - a]), ACT.Copy)\
                                .then_inc(sem(c_split), 1)

                    def square(i):
                        if split:
                            act.wait_ge(sem(steps), at(steps, i, 3))
                            act.activation(stage[:, 0, :], qn[:, 0, :], ACT.Square).then_inc(sem(sqr), 1)

                    def turned_qk(i):
                        act.wait_ge(sem(qk_turned), at(qk_turned, i, 1))
                        if not first(i):
                            act.wait_ge(sem(scores), at(scores, i, 0))
                        if not split:
                            act.activation(qkT_n[:, :, :], bank_t[1][:, :].rearrange("p (a t) -> p a t", a=4), ACT.Copy)\
                                .then_inc(sem(qkT), 1)
                            return
                        act.activation(qkT_n[:, 0:2, :], bank_t[1][:, 0:2 * P].rearrange("p (a t) -> p a t", a=2),
                                       ACT.Identity, scale=norm_cols[:, 0:1], bias=norm_cols[:, 1:2]).then_inc(sem(qkT), 1)
                        src = bank_t[1][:, 2 * P:4 * P].rearrange("p (f t) -> p f t", t=SEQ)
                        dst = qkT_n[:, 2:4, :].rearrange("p f (b t) -> p (f b) t", b=2)
                        for n, (a, e) in enumerate(segs):
                            act.activation(dst[:, :, a:e], src[:, :, a:e], ACT.Identity,
                                           scale=norm_cols[:, 2 + 2 * n:3 + 2 * n], bias=norm_cols[:, 3 + 2 * n:4 + 2 * n])\
                                .then_inc(sem(qkT), 1)

                    def exps(i, g):
                        act.wait_ge(sem(sub), at(sub, i, nseg * (g + 1)))
                        act.activation(E[:, g, :, :], E[:, g, :, :], ACT.Exp, scale=score_scale).then_inc(sem(ex), 1)

                    def copy_probs(i, g):
                        act.wait_ge(sem(p_turned), at(p_turned, i, g + 1))
                        act.activation(PT[:, g, :, :], bank_s[g % 2][:, :].rearrange("p (a t) -> p a t", a=4), ACT.Copy)\
                            .then_inc(sem(pT), 1)

                    def copy_oT(i):
                        act.wait_ge(sem(o_turned), at(o_turned, i, 1))
                        act.activation(oT_n[:, :, :], bank_t[0][:, 0:KC * P].rearrange("p (a b) -> p a b", b=P), ACT.Copy)\
                            .then_inc(sem(oT), 1)

                    def tile(i):
                        for g in range(chunks - 1):
                            exps(i, g)
                        if not first(i):
                            copy_oT(i - 1)
                        exps(i, chunks - 1)
                        if not within(i, 1):
                            turned_qk(i + 1)
                        if not within(i, 2):
                            front(i + 2)
                        for g in range(chunks // 2):
                            copy_probs(i, g)
                        if not within(i, 2):
                            square(i + 2)
                        for g in range(chunks // 2, chunks):
                            copy_probs(i, g)

                    front(0)
                    square(0)
                    front(1)
                    turned_qk(0)
                    square(1)
                    over_tiles(act, tile, tail=3)
                    copy_oT(TILES - 1)

                @block.gpsimd
                def _(pool):
                    def norm(i):
                        pool.wait_ge(sem(steps), at(steps, i, 4))
                        pool.tensor_tensor(ssq_e[:, :], ssq[:, :], head_eps[:, :], ALU.add).then_inc(sem(sqe), 1)
                        pool.wait_ge(sem(sqe), at(sqe, i, 1))
                        pool.tensor_tensor(rnorm[:, :], ssq_e[:, :], minus_half[:, 0:32], ALU.pow).then_inc(sem(rn), 1)

                    def tile(i):
                        if not within(i, 3):
                            pool_rstd(pool, s, i + 3)
                        if not within(i, 1):
                            spread_keys(pool, i + 1, 1)
                        if split and not within(i, 2):
                            norm(i + 2)

                    for i in range(3):
                        pool_rstd(pool, s, i)
                    if split:
                        norm(0)
                    spread_keys(pool, 0, 1)
                    if split:
                        norm(1)
                    over_tiles(pool, tile, tail=3)

                @block.vector
                def _(dve):
                    def centre_qk(i):
                        src = bank_p[0][:, :].rearrange("p (h d) -> p h d", d=hd)
                        dve.wait_ge(sem(qk), at(qk, i, 1))
                        if not first(i):
                            dve.wait_ge(sem(normed), at(normed, i, 0))
                        dve.tensor_reduce(mean_n[:, 0, :], src, AX, ALU.add).then_inc(sem(steps), 1)
                        dve.wait_ge(sem(steps), at(steps, i, 1))
                        dve.tensor_scalar(mean_n[:, 1, :], mean_n[:, 0, :], 1.0 / hd, None, ALU.mult).then_inc(sem(steps), 1)
                        dve.wait_ge(sem(steps), at(steps, i, 2))
                        if not first(i):
                            dve.wait_ge(sem(qk_turned), at(qk_turned, i, 0))
                        dve.tensor_tensor(qn[:, 0, :].rearrange("p (h d) -> p h d", d=hd), src,
                                          mean_n[:, 1, :].unsqueeze(2).broadcast_to([P, 32, hd]), ALU.subtract)\
                            .then_inc(sem(steps), 1)

                    def sum_squares(i):
                        dve.wait_ge(sem(sqr), at(sqr, i, 1))
                        dve.tensor_reduce(ssq[:, :], stage[:, 0, :].rearrange("p (h d) -> p h d", d=hd), AX, ALU.add)\
                            .then_inc(sem(steps), 1)

                    def scale_qk(i):
                        dst = qn[:, 0, :].rearrange("p (h d) -> p h d", d=hd)
                        dve.wait_ge(sem(rn), at(rn, i, 1))
                        dve.tensor_tensor(dst, dst, rnorm[:, :].unsqueeze(2).broadcast_to([P, 32, hd]), ALU.mult)\
                            .then_inc(sem(normed), 1)

                    def rotate_qk(i):
                        src = bank_p[0][:, :].rearrange("p (h r) -> p h r", r=8)
                        pair = bank_p[0][:, :].rearrange("p (h r two) -> p h r two", r=4, two=2)
                        turn = stage[:, 0, :].rearrange("p (h r two) -> p h r two", r=4, two=2)
                        dve.wait_ge(sem(qk), at(qk, i, 1))
                        if not first(i):
                            dve.wait_ge(sem(normed), at(normed, i, 0))
                            dve.wait_ge(sem(qk_turned), at(qk_turned, i, 0))
                        dve.tensor_tensor(qn[:, 0, :].rearrange("p (h r) -> p h r", r=8), src,
                                          ropes[:, i, 0:8].unsqueeze(1).broadcast_to([P, 64, 8]), ALU.mult)\
                            .then_inc(sem(steps), 1)
                        for n in range(2):
                            dve.tensor_tensor(turn[:, :, :, n], pair[:, :, :, 1 - n],
                                              ropes[:, i, 8 + 4 * n:12 + 4 * n].unsqueeze(1).broadcast_to([P, 64, 4]),
                                              ALU.mult).then_inc(sem(steps), 1)
                        dve.wait_ge(sem(steps), at(steps, i, 3))
                        dve.tensor_tensor(qn[:, 0, :], qn[:, 0, :], stage[:, 0, :], ALU.add).then_inc(sem(normed), 1)

                    def spread_v(i):
                        dve.wait_ge(sem(v), at(v, i, 1))
                        if not first(i):
                            dve.wait_ge(sem(pv), at(pv, i - 1, 1))
                        dve.tensor_tensor(v_pairs[:, :, :], bank_p[1][:, :].rearrange("p (b d) -> p b d", b=2),
                                          pair_mask[:, :].unsqueeze(1).broadcast_to([P, 2, DIM]), ALU.mult)\
                            .then_inc(sem(v_in), 1)

                    def shift(i, g):
                        dve.wait_ge(sem(scores), at(scores, i, g + 1))
                        src = bank_s[g % 2][:, :].rearrange("p (h k) -> p h k", h=8)
                        for n, (a, e) in enumerate(segs):
                            dve.tensor_reduce(smax[:, g, n, :], src[:, :, a:e], AX, ALU.max).then_inc(sem(smx), 1)
                        for n, (a, e) in enumerate(segs):
                            dve.wait_ge(sem(smx), at(smx, i, nseg * g + n + 1))
                            dve.tensor_tensor(E[:, g, :, a:e], src[:, :, a:e],
                                              smax[:, g, n, :].unsqueeze(2).broadcast_to([P, 8, e - a]), ALU.subtract)\
                                .then_inc(sem(sub), 1)

                    def weigh(i, g):
                        dve.wait_ge(sem(ex), at(ex, i, g + 1))
                        for n, (a, e) in enumerate(segs):
                            dve.tensor_reduce(ssum[:, g, n, :], E[:, g, :, a:e], AX, ALU.add).then_inc(sem(sm), 1)
                        dve.wait_ge(sem(sm), at(sm, i, nseg * (g + 1)))
                        dve.reciprocal(srec[:, g, 0:nseg, :], ssum[:, g, 0:nseg, :]).then_inc(sem(rec), 1)
                        dve.wait_ge(sem(rec), at(rec, i, g + 1))
                        for n, (a, e) in enumerate(segs):
                            dve.tensor_tensor(E[:, g, :, a:e], E[:, g, :, a:e],
                                              srec[:, g, n, :].unsqueeze(2).broadcast_to([P, 8, e - a]), ALU.mult)\
                                .then_inc(sem(probs), 1)

                    def sum_exps(i):
                        dve.wait_ge(sem(ex), at(ex, i, chunks))
                        dve.tensor_reduce(ssum[:, 0:chunks, 0, :], E[:, 0:chunks, :, :], AX, ALU.add).then_inc(sem(sm), 1)
                        dve.wait_ge(sem(sm), at(sm, i, 1))
                        dve.reciprocal(srec[:, 0:chunks, 0, :], ssum[:, 0:chunks, 0, :]).then_inc(sem(rec), 1)

                    def copy_o(i):
                        dve.wait_ge(sem(pv), at(pv, i, 1))
                        if split:
                            dve.tensor_copy(o_sb[:, :], bank_o[:, 0:DIM]).then_inc(sem(o_in), 1)
                        else:
                            dve.wait_ge(sem(rec), at(rec, i, 1))
                            dve.tensor_tensor(o_sb[:, :].rearrange("p (g h d) -> p g h d", g=chunks, h=8),
                                              bank_o[:, 0:DIM].rearrange("p (g h d) -> p g h d", g=chunks, h=8),
                                              srec[:, 0:chunks, 0, :].unsqueeze(3).broadcast_to([P, chunks, 8, hd]),
                                              ALU.mult).then_inc(sem(o_in), 1)

                    def add(i):
                        dve.wait_ge(sem(y), at(y, i, 1))
                        dve.scalar_tensor_tensor(x[:, i, :], bank_y[:, 0:DIM], tanh_g[:, layer:layer + 1], x[:, i, :],
                                                 ALU.mult, ALU.add).then_inc(sem(added), 1)

                    def tile(i):
                        if not within(i, 3):
                            ln_stats(dve, s, i + 3)
                        if not first(i):
                            copy_o(i - 1)
                        spread_v(i)
                        shift(i, 0)
                        shift(i, 1)
                        if split and not within(i, 1):
                            scale_qk(i + 1)
                        for g in range(2, chunks):
                            shift(i, g)
                        if split:
                            weigh(i, 0)
                            weigh(i, 1)
                        else:
                            sum_exps(i)
                        if not within(i, 1):
                            spread_keys(dve, i + 1, 0)
                        if not within(i, 2):
                            (centre_qk if split else rotate_qk)(i + 2)
                        if not first(i):
                            add(i - 1)
                        if not within(i, 3):
                            ln_apply(dve, s, i + 3)
                        if split and not within(i, 2):
                            sum_squares(i + 2)

                    for i in range(3):
                        dve_layernorm(dve, s, i)
                        if i == 0:
                            (centre_qk if split else rotate_qk)(0)
                            if split:
                                sum_squares(0)
                    if split:
                        scale_qk(0)
                    (centre_qk if split else rotate_qk)(1)
                    if split:
                        sum_squares(1)
                    spread_keys(dve, 0, 0)
                    over_tiles(dve, tile, tail=3)
                    copy_o(TILES - 1)
                    add(TILES - 1)
            block_ends()

        def make_masks(pool, step, hd):
            n = P // hd
            hm = head_mask[:, 0:n]
            step(pool.memset(hm, 1.0))
            pm = pair_mask[:, :].rearrange("p (j two d) -> p j two d", two=2, d=hd)
            for half in range(2):
                for odd in range(2):
                    step(pool.memset(pm[half * SEQ:(half + 1) * SEQ, :, odd, :], 1.0 if half == odd else 0.0))
            step(pool.affine_select(out=hm, in_=hm, compare_op=ALU.is_ge, fill=0.0, base=0, pattern=[[-hd, n]],
                                    channel_multiplier=1))
            step(pool.affine_select(out=hm, in_=hm, compare_op=ALU.is_ge, fill=0.0, base=hd - 1, pattern=[[hd, n]],
                                    channel_multiplier=-1))

        def in_turn(eng, sem):
            done = [0]

            def step(ins):
                done[0] += 1
                ins.then_inc(sem, 1)
                eng.wait_ge(sem, done[0])
            return step

        def run_l0x():
            hd, main = 16, 48
            wq, wkv, wd, wo = aw(0, KC, DIM), aw(512, 16, 2, 16), aw(1024, 512), aw(1536, KC, DIM)
            made = ctx.enter_context(nc.semaphore("l0_masks"))
            cols = ctx.enter_context(nc.semaphore("l0_norm_cols"))
            with nc.Block() as block:
                @block.gpsimd
                def _(pool):
                    step = in_turn(pool, made)
                    make_masks(pool, step, hd)
                    step(pool.memset(o_all[:, 1536:2304], 0.0))
                    step(pool.memset(key_side[:, :, :], 1.0))
                    step(pool.affine_select(out=key_side[:, :, :], in_=key_side[:, :, :], compare_op=ALU.is_ge, fill=0.0,
                                            base=main - 1, pattern=[[0, 2], [-1, SEQ]], channel_multiplier=SEQ))
                    step(pool.affine_select(out=key_side[:, :, :], in_=key_side[:, :, :], compare_op=ALU.is_ge, fill=0.0,
                                            base=SEQ - main, pattern=[[0, 2], [1, SEQ]], channel_multiplier=-SEQ))

                @block.tensor
                def _(pe):
                    pe.wait_ge(weights_in["l0x"], w_count["l0x"])
                    pe.transpose(bank_t[0][:, 0:6], norm_rows[:, :], ident[0:6, 0:6]).then_inc(cols, 1)

                @block.vector
                def _(dve):
                    dve.wait_ge(cols, 1)
                    dve.tensor_copy(norm_cols[:, :], bank_t[0][:, 0:6]).then_inc(cols, 1)
                    dve.wait_ge(cols, 2)
                    dve.tensor_scalar(norm_cols[:, 0:6:2], norm_cols[:, 0:6:2], float(hd) ** 0.5, None, ALU.mult)\
                        .then_inc(cols, 1)
            narrow_attention(0, "l0x", hd, wq, wo, [wkv[:, :, 0, :], wd[:, 0:DIM]], [wkv[:, :, 1, :], wd[:, DIM:2 * DIM]],
                             main)

        def run_l2x():
            hd = 8
            wq, wkv, wo = aw(0, KC, DIM), aw(512, 512), aw(1024, KC, DIM)
            made = ctx.enter_context(nc.semaphore("l2_masks"))
            r = ctx.enter_context(nc.semaphore("rope_steps"))
            sines = ctx.enter_context(nc.semaphore("rope_sines"))
            pi = PI
            with nc.Block() as block:
                @block.gpsimd
                def _(pool):
                    make_masks(pool, in_turn(pool, made), hd)

                @block.vector
                def _(dve):
                    ang, tmp, sin_in, cos_in = (ropes_w[:, n, :] for n in range(4))
                    step = in_turn(dve, r)

                    def wrapped(ap):
                        step(dve.tensor_scalar(tmp, ap, pi, -2 * pi, ALU.is_gt, ALU.mult))
                        step(dve.tensor_tensor(ap, ap, tmp, ALU.add))
                        step(dve.tensor_scalar(tmp, ap, -pi, 2 * pi, ALU.is_lt, ALU.mult))
                        step(dve.tensor_tensor(ap, ap, tmp, ALU.add))
                        step(dve.tensor_scalar(ap, ap, 3.1415925, -3.1415925, ALU.min, ALU.max))

                    dve.wait_ge(weights_in["l2x"], w_count["l2x"])
                    a4 = ang.rearrange("p (n a f) -> p n a f", a=2, f=2)
                    for f, freq in enumerate((1.0, 10000.0 ** -0.5)):
                        step(dve.tensor_scalar(a4[:, :, :, f], pos[:, :, :], freq, None, ALU.mult))
                    step(dve.tensor_scalar(tmp, ang, 1.0 / (2 * pi), None, ALU.mult))
                    step(dve.tensor_copy(ropes_i[:, :], tmp))
                    step(dve.tensor_copy(tmp, ropes_i[:, :]))
                    step(dve.scalar_tensor_tensor(ang, tmp, -6.28125, ang, ALU.mult, ALU.add))
                    step(dve.scalar_tensor_tensor(sin_in, tmp, -(2 * pi - 6.28125), ang, ALU.mult, ALU.add))
                    step(dve.tensor_scalar(cos_in, sin_in, pi / 2, None, ALU.add))
                    wrapped(sin_in)
                    wrapped(cos_in)
                    dve.wait_ge(sines, 2)
                    c4 = cos_in.rearrange("p (n r) -> p n r", r=4)
                    s4 = sin_in.rearrange("p (n r) -> p n r", r=4)
                    pair = ropes[:, :, 0:8].rearrange("p n (r two) -> p n r two", two=2)
                    step(dve.tensor_copy(pair[:, :, :, 0], c4))
                    step(dve.tensor_copy(pair[:, :, :, 1], c4))
                    step(dve.tensor_scalar(ropes[:, :, 8:12], s4, -1.0, None, ALU.mult))
                    step(dve.tensor_copy(ropes[:, :, 12:16], s4))

                @block.scalar
                def _(act):
                    act.wait_ge(r, 18)
                    act.activation(ropes_w[:, 2, :], ropes_w[:, 2, :], ACT.Sin).then_inc(sines, 1)
                    act.activation(ropes_w[:, 3, :], ropes_w[:, 3, :], ACT.Sin).then_inc(sines, 1)
            narrow_attention(2, "l2x", hd, wq, wo, [wkv[:, 0:DIM]], [wkv[:, DIM:2 * DIM]], SEQ)

        def run_l3f():
            key, hid = "l3f", 16
            w_in = fw(0, KC, EXPERTS + P)
            up_T = fw(512, DIM)
            raw_down, raw_router = fw(1024, DIM), ffn_w[0:EXPERTS, 1536:1536 + DIM]
            raw_up = fw(2048, KC, EXPERTS, hid)
            wt = ctx.enter_context(nc.semaphore("l3f_turned"))
            wk_ = ctx.enter_context(nc.semaphore("l3f_kept"))
            with nc.Block() as block:
                @block.tensor
                def _(pe):
                    pe.wait_ge(weights_in[key], w_count[key])
                    for c in range(KC):
                        pe.transpose(bank_t[0][:, c * P:(c + 1) * P], raw_down[:, c * P:(c + 1) * P], ident[:, :])
                    for c in range(KC):
                        mm = pe.transpose(bank_t[0][:, DIM + c * P:DIM + (c + 1) * P],
                                          raw_up[:, c, :, :].rearrange("p e i -> p (e i)"), ident[:, :])
                    for c in range(KC):
                        mm = pe.transpose(bank_t[1][:, c * EXPERTS:(c + 1) * EXPERTS],
                                          raw_router[:, c * P:(c + 1) * P], ident[0:EXPERTS, 0:EXPERTS])
                    mm.then_inc(wt, 1)

                @block.vector
                def _(dve):
                    dve.wait_ge(wt, 1)
                    dve.tensor_copy(w_in[:, :, EXPERTS:EXPERTS + P],
                                    bank_t[0][:, 0:DIM].rearrange("p (k n) -> p k n", k=KC)).then_inc(wk_, 1)
                    dve.tensor_copy(w_in[:, :, 0:EXPERTS],
                                    bank_t[1][:, 0:KC * EXPERTS].rearrange("p (k n) -> p k n", k=KC)).then_inc(wk_, 1)
                    dve.tensor_copy(up_T, bank_t[0][:, DIM:2 * DIM]).then_inc(wk_, 1)

            s = ln_signals()
            S = counted
            proj = S("projected", 1)
            th_s = S("tanh_ready", 1)
            hid_s = S("hidden_half", 1)
            lg_in = S("logits_copied", 1)
            g_steps = S("gate_steps", 8)
            ex_s = S("exp_ready", 1)
            act_in = S("hidden_ready", 1)
            turned = S("hidden_turned", 1)
            hTr = S("hiddenT_ready", 1)
            down = S("down_ready", 1)
            added = S("expert_added", 1)
            gated = S("gates_ready", 1)
            es, er, nm = lead_t, g_first, g_second

            with nc.Block() as block:
                @block.tensor
                def _(pe):
                    def tile(i):
                        pe_turn_x(pe, s, i, bank_t[0])
                        pe.wait_ge(sem(s["xT"]), at(s["xT"], i, 1))
                        if not first(i):
                            pe.wait_ge(sem(act_in), at(act_in, i, 0))
                        for k in range(KC):
                            mm = pe.matmul(bank_p[0][:, 0:EXPERTS + P], xcT[:, k, :], w_in[:, k, :], start=(k == 0),
                                           stop=(k == KC - 1))
                        mm.then_inc(sem(proj), 1)
                        pe.wait_ge(sem(act_in), at(act_in, i, 1))
                        pe.transpose(bank_t[1][:, 0:P], hh[:, 0, 0:P], ident[:, :]).then_inc(sem(turned), 1)
                        pe.wait_ge(sem(hTr), at(hTr, i, 1))
                        if not first(i):
                            pe.wait_ge(sem(added), at(added, i, 0))
                        pe.matmul(bank_y[:, 0:DIM], hT[:, 0, 0, :], up_T, start=True, stop=True).then_inc(sem(down), 1)
                    over_tiles(pe, tile)

                @block.scalar
                def _(act):
                    load_next(act, key)

                    def tile(i):
                        act.wait_ge(sem(s["turned"]), at(s["turned"], i, 1))
                        if not first(i):
                            act.wait_ge(sem(proj), at(proj, i, 0))
                        act.activation(xcT[:, 0:KC, :], bank_t[0][:, 0:KC * P].rearrange("p (a b) -> p a b", b=P),
                                       ACT.Copy).then_inc(sem(s["xT"]), 1)
                        act.wait_ge(sem(proj), at(proj, i, 1))
                        act.activation(th[:, 0, 0:P], bank_p[0][:, EXPERTS:EXPERTS + P], ACT.Tanh, scale=0.5)\
                            .then_inc(sem(th_s), 1)
                        act.wait_ge(sem(g_steps), at(g_steps, i, 2))
                        act.activation(pick[:, 0, :], lg[:, :], ACT.Exp, bias=nm[:, 0:1], accum_out=es[:, :])\
                            .then_inc(sem(ex_s), 1)
                        act.wait_ge(sem(turned), at(turned, i, 1))
                        act.activation(hT[:, 0, 0, :], bank_t[1][:, 0:P], ACT.Copy).then_inc(sem(hTr), 1)
                    over_tiles(act, tile)

                @block.gpsimd
                def _(pool):
                    over_tiles(pool, lambda i: pool_rstd(pool, s, i))

                @block.vector
                def _(dve):
                    def tile(i):
                        if not is_last(i):
                            dve_layernorm(dve, s, i + 1)
                        dve.wait_ge(sem(th_s), at(th_s, i, 1))
                        if not first(i):
                            dve.wait_ge(sem(turned), at(turned, i, 0))
                        dve.scalar_tensor_tensor(hh[:, 0, 0:P], th[:, 0, 0:P], 1.0, bank_p[0][:, EXPERTS:EXPERTS + P],
                                                 ALU.add, ALU.mult).then_inc(sem(hid_s), 1)
                        dve.tensor_copy(lg[:, :], bank_p[0][:, 0:EXPERTS]).then_inc(sem(lg_in), 1)
                        wait_apart(dve, sem(lg_in), at(lg_in, i, 1))
                        dve.max(top[:, :], lg[:, :]).then_inc(sem(g_steps), 1)
                        dve.wait_ge(sem(g_steps), at(g_steps, i, 1))
                        dve.tensor_scalar(nm[:, :], top[:, 0:1], -1.0, None, ALU.mult).then_inc(sem(g_steps), 1)
                        dve.max_index(top_i[:, :], top[:, :], lg[:, :]).then_inc(sem(g_steps), 1)
                        dve.wait_ge(sem(g_steps), at(g_steps, i, 3))
                        dve.tensor_copy(top_f[:, :], top_i[:, 0:2]).then_inc(sem(g_steps), 1)
                        dve.wait_ge(sem(ex_s), at(ex_s, i, 1))
                        dve.reciprocal(er[:, :], es[:, :]).then_inc(sem(g_steps), 1)
                        dve.wait_ge(sem(g_steps), at(g_steps, i, 5))
                        dve.tensor_scalar(er[:, :], er[:, :], half_g[:, 3:4], None, ALU.mult).then_inc(sem(g_steps), 1)
                        dve.tensor_scalar(gate[:, :], iota8[:, :], top_f[:, 0:1], None, ALU.is_equal).then_inc(sem(g_steps), 1)
                        dve.wait_ge(sem(g_steps), at(g_steps, i, 7))
                        dve.scalar_tensor_tensor(gate[:, :], iota8[:, :], top_f[:, 1:2], gate[:, :], ALU.is_equal,
                                                 ALU.add).then_inc(sem(g_steps), 1)
                        dve.wait_ge(sem(g_steps), at(g_steps, i, 8))
                        dve.scalar_tensor_tensor(gate[:, :], gate[:, :], er[:, 0:1], pick[:, 0, :], ALU.mult, ALU.mult)\
                            .then_inc(sem(gated), 1)
                        dve.wait_ge(sem(gated), at(gated, i, 1))
                        dve.tensor_tensor(hh[:, 0, 0:P].rearrange("p (e i) -> p e i", e=EXPERTS),
                                          hh[:, 0, 0:P].rearrange("p (e i) -> p e i", e=EXPERTS),
                                          gate[:, :].unsqueeze(2).broadcast_to([P, EXPERTS, hid]), ALU.mult)\
                            .then_inc(sem(act_in), 1)
                        dve.wait_ge(sem(down), at(down, i, 1))
                        dve.tensor_tensor(x[:, i, :], bank_y[:, 0:DIM], x[:, i, :], ALU.add).then_inc(sem(added), 1)

                    dve_layernorm(dve, s, 0)
                    over_tiles(dve, tile)
            block_ends()

        def moe_loads(sp, layer, key, gate_w, up_w, down_w, router_w, hid):
            wd = ffn_w[:, KC * EXPERTS * 2 * hid:]
            load(sp, key, router[:, layer, :, :], router_w.rearrange("(k p) e -> p k e", p=P))
            for k in range(KC):
                wgu = ffn_w[:, k * EXPERTS * 2 * hid:(k + 1) * EXPERTS * 2 * hid]
                for a, w in enumerate((gate_w, up_w)):
                    rows = w[:, k * P:(k + 1) * P, :]
                    if hid % P == 0:
                        chunks = hid // P
                        src = rows.rearrange("e p (c f) -> p e c f", c=chunks)
                        dst = wgu.rearrange("p (e c a f) -> p e c a f", e=EXPERTS, c=chunks, a=2)[:, :, :, a, :]
                        for c in range(chunks):
                            load(sp, key, dst[:, :, c, :], src[:, :, c, :])
                        continue
                    rest, body = SEQ, hid - SEQ
                    src = rows.rearrange("(j odd) p f -> odd p j f", odd=2)
                    dst = wgu.rearrange("p (j c) -> p j c", j=EXPERTS // 2)
                    for odd in range(2):
                        off = a * 2 * rest + odd * rest
                        load(sp, key, dst[:, :, off:off + rest], src[odd, :, :, body:hid])
                        off = 4 * rest + odd * 2 * body + a * body
                        load(sp, key, dst[:, :, off:off + body], src[odd, :, :, 0:body])
            if hid % P == 0:
                for c in range(hid // P):
                    load(sp, key, wd[:, c * EXPERTS * DIM:(c + 1) * EXPERTS * DIM].rearrange("p (e d) -> p e d", e=EXPERTS),
                         down_w[:, c * P:(c + 1) * P, :].rearrange("e p d -> p e d"))
                return
            load(sp, key, wd[0:body, 0:EXPERTS * DIM].rearrange("p (e d) -> p e d", e=EXPERTS),
                 down_w[:, 0:body, :].rearrange("e p d -> p e d"))
            for odd in range(2):
                load(sp, key, wd[odd * rest:(odd + 1) * rest, EXPERTS * DIM:12 * DIM].rearrange("p (j d) -> p j d", d=DIM),
                     down_w[:, body:hid, :].rearrange("(j odd) p d -> odd p j d", odd=2)[odd])

        MOE = {
            "l0f": (0, 128, "L0_ffn_wi_0", "L0_ffn_wi_1", "L0_ffn_wo", "L0_ffn_w_gate"),
            "l1f": (1, 176, "L1_ffn_Wg", "L1_ffn_Wu", "L1_ffn_Wd", "L1_ffn_Wr"),
            "l2f": (2, 256, "L2_ffn_Wg", "L2_ffn_Wu", "L2_ffn_Wd", "L2_ffn_Wr"),
        }

        def run_moe(key):
            layer, hid = MOE[key][:2]
            moe_part(layer, key, hid, w_count[key])

        def load_moe(sp, key):
            layer, hid, g, u, d, r = MOE[key]
            moe_loads(sp, layer, key, io[g], io[u], io[d], io[r], hid)

        def load_l0x(sp):
            hd = 16
            wq, wd, wo = aw(0, KC, DIM), aw(1024, 512), aw(1536, KC, DIM)
            k = "l0x"
            load(sp, k, wq, io["L0_xattn_Wq"].rearrange("(k p) n -> p k n", p=P))
            load(sp, k, attn_w[:, 512:768], io["L0_xattn_Wk"])
            load(sp, k, attn_w[:, 768:1024], io["L0_xattn_Wv"])
            load(sp, k, wd, io["L0_xattn_Wkv_dca"])
            load(sp, k, wo, io["L0_xattn_Wo"].rearrange("(k p) n -> p k n", p=P))
            load(sp, k, row_bias[:, :], io["L0_xattn_bq"].unsqueeze(0))
            load(sp, k, out_bias[:, :], io["L0_xattn_bo"].unsqueeze(0))
            for half, name in enumerate(("L0_xattn_bk", "L0_xattn_bv")):
                src = io[name].rearrange("(h t d) -> t h d", t=2, d=hd)
                for t in range(2):
                    load(sp, k, kv_bias[0:1, t, half * P:(half + 1) * P].rearrange("p (h d) -> p h d", d=hd),
                         src[t:t + 1])
            load(sp, k, kv_bias[1:2, :, :], io["L0_xattn_bkv_dca"].rearrange("(a t n) -> a t n", a=1, t=2))
            for n, name in enumerate(("qn_w", "qn_b", "kn_w", "kn_b", "kn_dca_w", "kn_dca_b")):
                load(sp, k, norm_rows[n:n + 1, :].rearrange("p (h d) -> p h d", d=hd),
                     io["L0_xattn_" + name].rearrange("(a b d) -> a b d", a=1, b=1).broadcast_to([1, P // hd, hd]))

        def load_l1x(sp):
            wq, wk, wv = aw(0, KC, 2048), aw(4096, 2048), aw(6144, 2048)
            wo, w2 = aw(8192, 16, DIM), aw(12288, 16, DIM)
            load(sp, "l1x", wq, io["L1_xattn_Wq"].rearrange("(k p) n -> p k n", p=P))
            load(sp, "l1x", wk, io["L1_xattn_Wk"])
            load(sp, "l1x", wv, io["L1_xattn_Wv"])
            load(sp, "l1x", wo, io["L1_xattn_Wo"].rearrange("(h p) d -> p h d", p=P))
            load(sp, "l1x", gcol[:, 0:1], io["L1_xattn_gq"].rearrange("(p a) -> p a", a=1))
            load(sp, "l1x", gcol[:, 1:2], io["L1_xattn_gk"].rearrange("(p a) -> p a", a=1))

        def load_l2x(sp):
            wq, wkv, wo = aw(0, KC, DIM), aw(512, 512), aw(1024, KC, DIM)
            k = "l2x"
            load(sp, k, wq, io["L2_xattn_Wq"].rearrange("(k p) n -> p k n", p=P))
            load(sp, k, wkv, io["L2_xattn_Wkv"])
            load(sp, k, wo, io["L2_xattn_Wout"].rearrange("(k p) n -> p k n", p=P))
            load(sp, k, out_bias[:, :], io["L2_xattn_bout"].unsqueeze(0))
            load(sp, k, pos[:, :, :], io["fside_BxSx2_0"].rearrange("b s a -> (b s) a")
                 .rearrange("(n p) a -> p n a", p=P))

        def load_l3x(sp):
            wq, wk, wv = aw(0, KC, 2048), aw(4096, 1024), aw(5120, 1024)
            wo = aw(6144, 16, DIM)
            load(sp, "l3x", wq, io["L3_xattn_Wq"].rearrange("(k p) n -> p k n", p=P))
            load(sp, "l3x", wk, io["L3_xattn_Wk"])
            load(sp, "l3x", wv, io["L3_xattn_Wv"])
            load(sp, "l3x", wo, io["L3_xattn_Wo"].rearrange("(h p) d -> p h d", p=P))
            rows = io["mask_BxS2_bf1"].rearrange("(n b) k -> b n k", b=2)
            for b in range(2):
                load(sp, "l3x", mask_u8[b * SEQ:(b + 1) * SEQ, :, :],
                     rows[b:b + 1].broadcast_to([SEQ, TILES, SEQ]))

        def load_l3f(sp):
            key, hid = "l3f", 16
            raw_down, raw_router = fw(1024, DIM), ffn_w[0:EXPERTS, 1536:1536 + DIM]
            raw_up = fw(2048, KC, EXPERTS, hid)
            load(sp, key, raw_down, io["L3_ffn_down_w"].rearrange("e i h -> (e i) h"))
            load(sp, key, raw_router, io["L3_ffn_router_w"])
            for c in range(KC):
                load(sp, key, raw_up[:, c, :, :],
                     io["L3_ffn_up_w"][:, c * P:(c + 1) * P, :].rearrange("e p i -> p e i"))

        loaders = {"l0x": load_l0x, "l1x": load_l1x, "l2x": load_l2x, "l3x": load_l3x, "l3f": load_l3f}

        def load_part(queue, key):
            if key in loaders:
                loaders[key](queue)
            elif key is not None:
                load_moe(queue, key)

        def load_next(queue, key):
            n = parts.index(key) + 1
            if n < len(parts) and not (key[2] == parts[n][2]):
                load_part(queue, parts[n])
                loaded.append(parts[n])

        loaded = []

        def weights_of(key):
            if key not in loaded:
                with nc.Block() as block:
                    @block.sync
                    def _(sp):
                        load_part(sp, key)

        run = {"l0x": run_l0x, "l1x": run_l1x, "l2x": run_l2x, "l3x": run_l3x, "l3f": run_l3f}
        for key in parts:
            weights_of(key)
            run[key]() if key in run else run_moe(key)

        with nc.Block() as block:
            @block.sync
            def _(sp):
                sp.dma_start(out.rearrange("b s d -> (b s) d").rearrange("(n p) d -> p n d", p=P), x[:, :, :])\
                    .then_inc(out_stored, 16)
                sp.wait_ge(out_stored, 16)


PARTS = ("l0x", "l0f", "l1x", "l1f", "l2x", "l2f", "l3x", "l3f")


def kernel(**inputs):
    import numpy as np
    from concourse import bacc
    from concourse.bass_utils import run_bass_kernel_spmd

    nc = bacc.Bacc("TRN2", target_bir_lowering=False, num_devices=1)
    arrays, io = {}, {}
    for name, value in inputs.items():
        a = np.ascontiguousarray(value)
        if a.dtype == np.bool_:
            a = a.view(np.uint8)
        arrays[f"in_{name}_dram"] = a
        io[name] = nc.dram_tensor(f"in_{name}_dram", a.shape, mybir.dt.from_np(a.dtype), kind="ExternalInput").ap()
    out = nc.dram_tensor("out_0_dram", (BATCH, SEQ, DIM), F32, kind="ExternalOutput").ap()
    flamingo_kernel(nc, io, out, PARTS)
    r = run_bass_kernel_spmd(nc, [arrays], core_ids=[0])
    return r.results[0]["out_0_dram"]
```
